# Optimizing a Trainium2 kernel written in Bass

```python
import numpy as np
import jax
import jax.numpy as jnp

def _softmax(x, axis=-1):
    return jax.nn.softmax(x, axis=axis)

def _gelu(x):
    return jax.nn.gelu(x, approximate=True)

def _silu(x):
    return jax.nn.silu(x)

def _sigmoid(x):
    return jax.nn.sigmoid(x)

def _layernorm(x, axis=-1, eps=1e-05):
    m = jnp.mean(x, axis=axis, keepdims=True)
    v = jnp.var(x, axis=axis, keepdims=True)
    return (x - m) / jnp.sqrt(v + eps)

def _scatter_add(tgt, idx, src, axis=0):
    return tgt.at[idx].add(src)

def _segment_sum(src, seg, n):
    return jax.ops.segment_sum(src, seg, n)
kernel_name = 'mk_gnn_resnorm_d4_gnn_r64_86caaf'

def setup_inputs(seed: int=0):
    np.random.seed(seed)
    _w = jnp.asarray

    def _rec_inputs():
        import jax
        import jax.numpy as jnp
        _gk = jax.random.key(seed)
        x = -0.0003713 + 1 * jax.random.normal(jax.random.fold_in(_gk, 1), (100000, 128), jnp.float32)
        src = jax.random.randint(jax.random.fold_in(_gk, 2), (25000,), 0, 100000, jnp.int32)
        dst = jnp.minimum((100000 * jax.random.uniform(jax.random.fold_in(_gk, 3), (25000,)) ** 2.0).astype(jnp.int32), 99999)
        _o = jnp.argsort(dst, stable=True)
        src = src[_o]
        dst = dst[_o]
        edge_weight = jax.random.uniform(jax.random.fold_in(_gk, 13), (25000,), jnp.float32, 0.0, 1)
        return (x, src, dst, edge_weight)
    x, src, dst, edge_weight = _rec_inputs()

    def _L0_gnn_setup():
        import jax, jax.numpy as jnp
        import numpy as np
        N_NODES = 100000
        N_EDGES = 50000
        D_IN = 128
        D_OUT = 128
        key = jax.random.key(seed)
        k1, k2, k3, k4, k5, k6 = jax.random.split(key, 6)
        x = jax.random.normal(k1, (N_NODES, D_IN), dtype=jnp.float32)
        edge_row = jax.random.randint(k2, (N_EDGES,), 0, N_NODES)
        edge_col = jax.random.randint(k3, (N_EDGES,), 0, N_NODES)
        edge_vals = jax.random.uniform(k4, (N_EDGES,), dtype=jnp.float32)
        stdv = 1.0 / np.sqrt(D_OUT)
        weight = jax.random.uniform(k5, (D_IN, D_OUT), dtype=jnp.float32, minval=-stdv, maxval=stdv)
        bias_param = jax.random.uniform(k6, (D_OUT,), dtype=jnp.float32, minval=-stdv, maxval=stdv)
        return {'x': x, 'edge_row': edge_row, 'edge_col': edge_col, 'edge_vals': edge_vals, 'weight': weight, 'bias_param': bias_param}
    _L0_gnn_all = _L0_gnn_setup()
    _L0_gnn_in = {k: v for k, v in _L0_gnn_all.items() if k in ('weight', 'bias_param')}
    del _L0_gnn_all

    def _L1_gnn_setup():
        import jax, jax.numpy as jnp
        import numpy as np
        N = 100000
        E = 9375
        D_IN = 128
        D_OUT = 128
        K = 2
        ALPHA = 0.5
        key = jax.random.key(seed)
        k1, k2, k3, k4 = jax.random.split(key, 4)
        x = jax.random.normal(k1, (N, D_IN), dtype=jnp.float32)
        edge_index = jax.random.randint(k2, (2, E), 0, N, dtype=jnp.int64)
        W = jax.random.normal(k3, (D_OUT, D_IN), dtype=jnp.float32) * (1.0 / np.sqrt(D_IN))
        b = jax.random.normal(k4, (D_OUT,), dtype=jnp.float32) * 0.01
        return {'x': x, 'edge_index': edge_index, 'W': W, 'b': b}
    _L1_gnn_all = _L1_gnn_setup()
    _L1_gnn_in = {k: v for k, v in _L1_gnn_all.items() if k in ('W', 'b')}
    del _L1_gnn_all

    def _L2_gnn_setup():
        import jax, jax.numpy as jnp
        import numpy as np
        N, E, F = (50000, 12500, 128)
        DELTA = 1.0
        EPS = 1e-05

        def _pna_forward(x, edge_index, W_pre, b_pre, W_post, b_post, W_lin, b_lin):
            src, dst = (edge_index[0], edge_index[1])
            n = x.shape[0]
            h = jnp.concatenate([x[dst], x[src]], axis=-1)
            m = h @ W_pre.T + b_pre
            deg = jax.ops.segment_sum(jnp.ones((m.shape[0],), m.dtype), dst, num_segments=n)
            deg_c = jnp.maximum(deg, 1.0)[:, None]
            has_edge = (deg > 0)[:, None]
            mx = jax.ops.segment_max(m, dst, num_segments=n)
            mx = jnp.where(has_edge, mx, 0.0)
            mn = jax.ops.segment_min(m, dst, num_segments=n)
            mn = jnp.where(has_edge, mn, 0.0)
            s1 = jax.ops.segment_sum(m, dst, num_segments=n)
            s2 = jax.ops.segment_sum(m * m, dst, num_segments=n)
            mean = s1 / deg_c
            var = s2 / deg_c - mean * mean
            std = jnp.sqrt(jax.nn.relu(var) + EPS)
            agg = jnp.concatenate([mx, mn, mean, std], axis=-1)
            log_deg = jnp.log(deg_c + 1.0)
            amp = log_deg / DELTA
            att = DELTA / log_deg
            scaled = jnp.concatenate([agg, agg * amp, agg * att], axis=-1)
            out = jnp.concatenate([x, scaled], axis=-1) @ W_post.T + b_post
            return out @ W_lin.T + b_lin
        key = jax.random.key(seed)
        ks = jax.random.split(key, 6)
        x = jax.random.normal(ks[0], (N, F), dtype=jnp.float32)
        edge_index = jax.random.randint(ks[1], (2, E), 0, N, dtype=jnp.int32)
        W_pre = jax.random.normal(ks[2], (F, 2 * F), dtype=jnp.float32) * (2 * F) ** (-0.5)
        b_pre = jnp.zeros((F,), jnp.float32)
        W_post = jax.random.normal(ks[3], (F, 13 * F), dtype=jnp.float32) * (13 * F) ** (-0.5)
        b_post = jnp.zeros((F,), jnp.float32)
        W_lin = jax.random.normal(ks[4], (F, F), dtype=jnp.float32) * F ** (-0.5)
        b_lin = jnp.zeros((F,), jnp.float32)
        return {'x': x, 'edge_index': edge_index, 'W_pre': W_pre, 'b_pre': b_pre, 'W_post': W_post, 'b_post': b_post, 'W_lin': W_lin, 'b_lin': b_lin}
    _L2_gnn_all = _L2_gnn_setup()
    _L2_gnn_in = {k: v for k, v in _L2_gnn_all.items() if k in ('W_pre', 'b_pre', 'W_post', 'b_post', 'W_lin', 'b_lin')}
    del _L2_gnn_all

    def _L3_gnn_setup():
        import jax, jax.numpy as jnp
        import numpy as np
        N_NODES = 100000
        N_EDGES = 25000
        D_IN = 128
        D_OUT = 128
        key = jax.random.key(seed)
        k1, k2, k3, k4 = jax.random.split(key, 4)
        x = jax.random.normal(k1, (N_NODES, D_IN), dtype=jnp.float32)
        edge_index = jax.random.randint(k2, (2, N_EDGES), 0, N_NODES, dtype=jnp.int64)
        scale = 1.0 / np.sqrt(D_IN)
        W_l = jax.random.normal(k3, (D_OUT, D_IN), dtype=jnp.float32) * scale
        W_r = jax.random.normal(k4, (D_OUT, D_IN), dtype=jnp.float32) * scale
        b = jnp.zeros((D_OUT,), dtype=jnp.float32)
        return {'x': x, 'edge_index': edge_index, 'W_l': W_l, 'W_r': W_r, 'b': b}
    _L3_gnn_all = _L3_gnn_setup()
    _L3_gnn_in = {k: v for k, v in _L3_gnn_all.items() if k in ('W_l', 'W_r', 'b')}
    del _L3_gnn_all
    return {'x': x, 'src': src, 'dst': dst, 'edge_weight': edge_weight, 'L0_gnn_weight': _L0_gnn_in['weight'], 'L0_gnn_bias_param': _L0_gnn_in['bias_param'], 'L1_gnn_W': _L1_gnn_in['W'], 'L1_gnn_b': _L1_gnn_in['b'], 'L2_gnn_W_pre': _L2_gnn_in['W_pre'], 'L2_gnn_b_pre': _L2_gnn_in['b_pre'], 'L2_gnn_W_post': _L2_gnn_in['W_post'], 'L2_gnn_b_post': _L2_gnn_in['b_post'], 'L2_gnn_W_lin': _L2_gnn_in['W_lin'], 'L2_gnn_b_lin': _L2_gnn_in['b_lin'], 'L3_gnn_W_l': _L3_gnn_in['W_l'], 'L3_gnn_W_r': _L3_gnn_in['W_r'], 'L3_gnn_b': _L3_gnn_in['b']}

def reference(x, src, dst, edge_weight, L0_gnn_weight, L0_gnn_bias_param, L1_gnn_W, L1_gnn_b, L2_gnn_W_pre, L2_gnn_b_pre, L2_gnn_W_post, L2_gnn_b_post, L2_gnn_W_lin, L2_gnn_b_lin, L3_gnn_W_l, L3_gnn_W_r, L3_gnn_b):
    import jax
    import jax.numpy as jnp

    def _L0_gnn_ref(x, edge_row, edge_col, edge_vals, weight, bias_param):
        import jax, jax.numpy as jnp
        import numpy as np
        N_NODES = 100000
        N_EDGES = 50000
        D_IN = 128
        D_OUT = 128
        support = x @ weight
        messages = edge_vals[:, None] * support[edge_col]
        output = jax.ops.segment_sum(messages, edge_row, num_segments=N_NODES)
        return output + bias_param

    def _L1_gnn_ref(x, edge_index, W, b):
        import jax, jax.numpy as jnp
        import numpy as np
        N = 100000
        E = 9375
        D_IN = 128
        D_OUT = 128
        K = 2
        ALPHA = 0.5
        n = x.shape[0]
        loops = jnp.tile(jnp.arange(n, dtype=edge_index.dtype)[None, :], (2, 1))
        ei = jnp.concatenate([edge_index, loops], axis=1)
        row, col = (ei[0], ei[1])
        deg = jnp.zeros((n,), dtype=x.dtype).at[col].add(1.0)
        deg_inv_left = jnp.where(deg > 0, deg ** (-ALPHA), 0.0)
        deg_inv_right = jnp.where(deg > 0, deg ** (ALPHA - 1.0), 0.0)
        edge_weight = (deg_inv_left[row] * deg_inv_right[col])[:, None]
        for _ in range(K):
            x = jnp.zeros_like(x).at[row].add(edge_weight * x[col])
        return x @ W.T + b

    def _L2_gnn_ref(x, edge_index, W_pre, b_pre, W_post, b_post, W_lin, b_lin):
        import jax, jax.numpy as jnp
        import numpy as np
        N, E, F = (50000, 12500, 128)
        DELTA = 1.0
        EPS = 1e-05

        def _pna_forward(x, edge_index, W_pre, b_pre, W_post, b_post, W_lin, b_lin):
            src, dst = (edge_index[0], edge_index[1])
            n = x.shape[0]
            h = jnp.concatenate([x[dst], x[src]], axis=-1)
            m = h @ W_pre.T + b_pre
            deg = jax.ops.segment_sum(jnp.ones((m.shape[0],), m.dtype), dst, num_segments=n)
            deg_c = jnp.maximum(deg, 1.0)[:, None]
            has_edge = (deg > 0)[:, None]
            mx = jax.ops.segment_max(m, dst, num_segments=n)
            mx = jnp.where(has_edge, mx, 0.0)
            mn = jax.ops.segment_min(m, dst, num_segments=n)
            mn = jnp.where(has_edge, mn, 0.0)
            s1 = jax.ops.segment_sum(m, dst, num_segments=n)
            s2 = jax.ops.segment_sum(m * m, dst, num_segments=n)
            mean = s1 / deg_c
            var = s2 / deg_c - mean * mean
            std = jnp.sqrt(jax.nn.relu(var) + EPS)
            agg = jnp.concatenate([mx, mn, mean, std], axis=-1)
            log_deg = jnp.log(deg_c + 1.0)
            amp = log_deg / DELTA
            att = DELTA / log_deg
            scaled = jnp.concatenate([agg, agg * amp, agg * att], axis=-1)
            out = jnp.concatenate([x, scaled], axis=-1) @ W_post.T + b_post
            return out @ W_lin.T + b_lin
        return _pna_forward(x, edge_index, W_pre, b_pre, W_post, b_post, W_lin, b_lin)

    def _L3_gnn_ref(x, edge_index, W_l, W_r, b):
        import jax, jax.numpy as jnp
        import numpy as np
        N_NODES = 100000
        N_EDGES = 25000
        D_IN = 128
        D_OUT = 128
        src = edge_index[0]
        dst = edge_index[1]
        n = x.shape[0]
        agg = jax.ops.segment_sum(x[src], dst, num_segments=n)
        cnt = jax.ops.segment_sum(jnp.ones_like(src, dtype=x.dtype), dst, num_segments=n)
        mean = agg / jnp.maximum(cnt, 1.0)[:, None]
        out = jnp.einsum('nd,od->no', mean, W_l) + b + jnp.einsum('nd,od->no', x, W_r)
        return jax.nn.relu(out)
    edge_index = jnp.stack([src, dst])
    x = _layernorm(x + _L0_gnn_ref(x, src, dst, edge_weight, L0_gnn_weight, L0_gnn_bias_param), axis=-1)
    x = _layernorm(x + _L1_gnn_ref(x, edge_index, L1_gnn_W, L1_gnn_b), axis=-1)
    x = _layernorm(x + _L2_gnn_ref(x, edge_index, L2_gnn_W_pre, L2_gnn_b_pre, L2_gnn_W_post, L2_gnn_b_post, L2_gnn_W_lin, L2_gnn_b_lin), axis=-1)
    x = _layernorm(x + _L3_gnn_ref(x, edge_index, L3_gnn_W_l, L3_gnn_W_r, L3_gnn_b), axis=-1)
    return x

_drawn_inputs = setup_inputs


def setup_inputs(seed=0):
    import zlib

    import numpy as np

    out = dict(_drawn_inputs(seed))
    spreads = {'L2_gnn_b_pre': (0.0, 0.305),
     'L2_gnn_b_post': (0.0, 0.1),
     'L2_gnn_b_lin': (0.0, 0.1),
     'L3_gnn_b': (0.0, 0.1)}
    factors = {'L1_gnn_b': 6.589}
    for name, (base, spread) in spreads.items():
        noise = np.random.default_rng([zlib.crc32(name.encode()), seed]).standard_normal(out[name].shape)
        drawn = base * np.exp(spread * noise) if base else spread * noise
        out[name] = jnp.asarray(drawn.astype(out[name].dtype))
    for name, factor in factors.items():
        out[name] = (out[name] * factor).astype(out[name].dtype)
    return out
```

```python
from contextlib import ExitStack

import concourse.bass as bass
from concourse import mybir

ALU = mybir.AluOpType
ACT = mybir.ActivationFunctionType
F32 = mybir.dt.float32
F16 = mybir.dt.float16
I32 = mybir.dt.int32

P = 128
D = 128
EPS = 1e-5
LN2 = 0.6931471805599453

N = 100000
E = 25000
T = 4
STEP = T * P
NSTEP = 50
SLOTS = NSTEP * STEP
TILES = SLOTS // P
PAD_KEY = N
EDGE_ROWS = E // TILES
FAR = 1 << 20

LO_BITS = 8
LO = 1 << LO_BITS
HI_PARTS = 4
HI_ROWS = -(-(N + 1) // (LO * HI_PARTS))
HI = HI_PARTS * HI_ROWS

G = 5
NG = TILES // G

SWEEP = -(-N // STEP)
HALF = TILES // 2
BIG = 3.0e38


def wait(eng, sem, count):
    if isinstance(count, int) and count <= 0:
        return
    eng.wait_ge(sem, count)


def pairs(eng, steps, body):
    body(0, 0)
    body(0, 1)
    with eng.Fori(1, steps // 2, 1) as h:
        body(h, 0)
        body(h, 1)


def gnn_kernel(nc, x, src, dst, edge_weight, w0, b0, w1, b1, w_pre, b_pre, w_post, b_post,
               w_lin, b_lin, w_l, w_r, b3, out):
    with ExitStack() as ctx:
        def sb(name, shape, dt=F32):
            return ctx.enter_context(nc.sbuf_tensor(name, shape, dt))

        def sem(name):
            return ctx.enter_context(nc.semaphore(name))

        def dram(name, shape, dt=F32):
            return nc.dram_tensor(name, shape, dt, kind="Internal").ap()

        recs = dram("recs", (SLOTS, 4), I32)
        recs_lo = [dram(f"recs_lo{q}", (SLOTS, 4), I32) for q in range(2)]
        sorted_recs = [dram(f"sorted_recs{q}", (SLOTS + 2, 4), I32) for q in range(2)]
        dinv_table = dram("dinv_table", (HI * LO, 1))
        u_table = dram("u_table", (N, D))
        v_table = dram("v_table", (N, D))
        y1_table = dram("y1_table", (N, D))
        y2_table = dram("y2_table", (N, D))
        y0_slots = dram("y0_slots", (SLOTS, D))
        u_slots = dram("u_slots", (SLOTS, D))
        v_slots = dram("v_slots", (SLOTS, D))
        y2_slots = dram("y2_slots", (SLOTS, D))

        bank = [ctx.enter_context(nc.psum_tensor(f"bank{i}", [P, 512], F32)) for i in range(8)]

        ident = sb("ident", [P, P])
        before = sb("before", [P, P], F16)
        not_before = sb("not_before", [P, P], F16)
        ones16 = sb("ones16", [P, P], F16)
        zeros16 = sb("zeros16", [P, 512], F16)
        count_i = sb("count_i", [P, HI], I32)
        count16 = sb("count16", [P, HI], F16)
        ones_row = sb("ones_row", [1, P])
        ones_step = sb("ones_step", [P, 512])
        eps_col = sb("eps_col", [P, 1])
        one_col = sb("one_col", [P, 1])
        std_cols = sb("std_cols", [P, 3])
        w0_sb = sb("w0_sb", [P, D])
        w1_raw = sb("w1_raw", [P, D])
        w_pre_raw = sb("w_pre_raw", [P, 2 * D])
        w_post_sb = sb("w_post_sb", [P, 13 * D])
        w_lin_raw = sb("w_lin_raw", [P, D])
        w_l_raw = sb("w_l_raw", [P, D])
        w_r_raw = sb("w_r_raw", [P, D])
        w1_t = sb("w1_t", [P, D])
        w_dst_t = sb("w_dst_t", [P, D])
        w_src_t = sb("w_src_t", [P, D])
        w_lin_t = sb("w_lin_t", [P, D])
        w_l_t = sb("w_l_t", [P, D])
        w_r_t = sb("w_r_t", [P, D])
        w_own = sb("w_own", [P, D])
        w_agg = sb("w_agg", [P, 4, 3 * D])
        b0_row = sb("b0_row", [1, D])
        b1_row = sb("b1_row", [1, D])
        b3_row = sb("b3_row", [1, D])
        b_lin_row = sb("b_lin_row", [1, D])
        b_post_col = sb("b_post_col", [P, 1])
        b_pre_col = sb("b_pre_col", [P, 1])
        b2_row = sb("b2_row", [1, D])
        b2_alone = sb("b2_alone", [1, D])
        b0_all = sb("b0_all", [P, D])
        b1_all = sb("b1_all", [P, D])

        list_w = sb("list_w", [P, TILES])
        list_key = [sb(f"list_key{q}", [P, TILES], I32) for q in range(2)]
        list_other = [sb(f"list_other{q}", [P, TILES], I32) for q in range(2)]
        list_write = [sb(f"list_write{q}", [P, TILES], I32) for q in range(2)]
        list_keep = [sb(f"list_keep{q}", [P, TILES]) for q in range(2)]
        dinv_own = sb("dinv_own", [P, TILES])
        dinv2_own = sb("dinv2_own", [P, TILES])
        inv_count = sb("inv_count", [P, TILES])

        raw_i = sb("raw_i", [P, 3, TILES], I32)
        rec_all = sb("rec_all", [P, TILES, 4], I32)
        rec = sb("rec", [P, 2, G, 4], I32)
        digit_i = sb("digit_i", [P, 4, G], I32)
        digit = sb("digit", [P, 4, G])
        onehot = sb("onehot", [P, 2, 2 * (LO + HI)], F16)
        rank_terms = sb("rank_terms", [P, HI])
        position = sb("position", [P, G])
        position_i = sb("position_i", [P, 2, G], I32)
        totals = sb("totals", [P, 2 * (LO + HI)])
        inclusive = sb("inclusive", [P, 2 * (LO + HI)])
        first_place = sb("first_place", [P, 2 * (LO + HI)])
        degree = sb("degree", [P, HI_PARTS * LO])
        fence = sb("fence", [2, 4], I32)
        prep = sb("prep", [HALF, 3, P, 4], I32)
        prep_f = sb("prep_f", [HALF, 6, P])

        rows_a = sb("rows_a", [P, 2, T, D])
        rows_b = sb("rows_b", [P, 2, T, D])
        rows_c = sb("rows_c", [P, 2, T, D])
        idx_a = sb("idx_a", [P, 2, T], I32)
        idx_b = sb("idx_b", [P, 2, T], I32)
        idx_w = sb("idx_w", [P, 2, T], I32)
        dinv_in = sb("dinv_in", [P, 2, T])
        keep_cols = sb("keep_cols", [P, T])
        keep_row = sb("keep_row", [P, 2, STEP])
        low_row = sb("low_row", [P, 2, STEP])
        high_row = sb("high_row", [P, 2, STEP])
        agg = sb("agg", [P, 2, STEP])
        agg_max = sb("agg_max", [P, 2, STEP])
        agg_min = sb("agg_min", [P, 2, STEP])
        agg_sq = sb("agg_sq", [P, 2, STEP])
        agg_n = sb("agg_n", [P, 2, STEP])
        msg = sb("msg", [P, STEP])
        msg_sq = sb("msg_sq", [P, STEP])
        turned_a = sb("turned_a", [P, STEP])
        turned_b = sb("turned_b", [P, STEP])
        inv_n = sb("inv_n", [P, STEP])
        mean = sb("mean", [P, STEP])
        mean_sq = sb("mean_sq", [P, STEP])
        var = sb("var", [P, STEP])
        dev = sb("dev", [P, STEP])
        plain = sb("plain", [P, T, D])
        pre = sb("pre", [P, T, D])
        pre_b = sb("pre_b", [P, T, D])
        fresh = sb("fresh", [P, 2, T, D])
        fresh_b = sb("fresh_b", [P, 2, T, D])
        fresh_c = sb("fresh_c", [P, 2, T, D])
        stats = sb("stats", [P, T, 6])
        moments = sb("moments", [P, T, 2])
        std = sb("std", [P, T])
        rstd = sb("rstd", [P, T])
        scales = sb("scales", [P, 3, T])


        def by_slot(table, j):
            return table[bass.ds(j * STEP, STEP), :].rearrange("(t p) d -> p t d", p=P)

        def by_node(table, j):
            start = N - STEP if isinstance(j, int) and j == SWEEP - 1 else j * STEP
            return table[bass.ds(start, STEP), :].rearrange("(p t) d -> p t d", t=T)

        def tiles(a):
            return a.rearrange("p (t d) -> p t d", t=T)

        def bank4(i):
            return tiles(bank[i][:])

        def over_tiles(a):
            return a.rearrange("p (t d) -> p t d", t=1).broadcast_to([P, T, D])

        def gather(to, table, idx, done, bound):
            nc.gpsimd.indirect_dma_start(
                out=to, out_offset=None, in_=table, in_offset=bass.IndirectOffsetOnAxis(ap=idx, axis=0),
                bounds_check=bound, oob_is_err=False).then_inc(done, 16)

        def scatter(table, idx, rows, done, bound):
            nc.gpsimd.indirect_dma_start(
                out=table, out_offset=bass.IndirectOffsetOnAxis(ap=idx, axis=0), in_=rows, in_offset=None,
                bounds_check=bound, oob_is_err=False).then_inc(done, 16)

        pool_gate = nc.alloc_semaphore("pool_gate")
        dve_gate = nc.alloc_semaphore("dve_gate")
        act_gate = nc.alloc_semaphore("act_gate")

        def phase(build, *args):
            sems = []

            def sem(name):
                sems.append(nc.alloc_semaphore(f"{name}_{len(sems)}_{nc.next_id()}"))
                return sems[-1]
            block = nc.Block()
            with block as b:
                build(b, sem, *args)
            nc.clear_and_free_semaphores(sems)
            nc.all_engine_barrier()

        def set_up(block, sem):
            filled = sem("filled")
            set_dve = sem("set_dve")
            selected = sem("selected")
            loaded = sem("loaded")
            edges_in = sem("edges_in")
            counted = sem("counted")
            interleaved = sem("interleaved")
            recs_out = sem("recs_out")
            w_turned = sem("w_turned")
            w_copied = sem("w_copied")
            merged = sem("merged")
            merged_out = sem("merged_out")
            raw = ((w1_raw, w1_t), (w_lin_raw, w_lin_t), (w_l_raw, w_l_t), (w_r_raw, w_r_t))

            @block.sync
            def _(sp):
                for to, what in ((w0_sb, w0), (w1_raw, w1), (w_pre_raw, w_pre), (w_post_sb, w_post),
                                 (w_lin_raw, w_lin), (w_l_raw, w_l), (w_r_raw, w_r)):
                    sp.dma_start(to[:], what).then_inc(loaded, 16)
                for to, what in ((b0_row, b0), (b1_row, b1), (b3_row, b3), (b_lin_row, b_lin)):
                    sp.dma_start(to[:], what.rearrange("(a d) -> a d", a=1)).then_inc(loaded, 16)
                for to, what in ((b_post_col, b_post), (b_pre_col, b_pre)):
                    sp.dma_start(to[:], what.rearrange("(d a) -> d a", a=1)).then_inc(loaded, 16)
                sp.wait_ge(filled, 1)
                for n, what in enumerate((src, dst)):
                    sp.dma_start(raw_i[0:EDGE_ROWS, n, :], what.rearrange("(p j) -> p j", j=TILES))\
                        .then_inc(edges_in, 16)
                sp.dma_start(raw_i[0:EDGE_ROWS, 2, :].bitcast(F32),
                             edge_weight.rearrange("(p j) -> p j", j=TILES)).then_inc(edges_in, 16)
                sp.wait_ge(interleaved, 1)
                sp.dma_start(recs.rearrange("(p j) c -> p j c", j=TILES), rec_all[:]).then_inc(recs_out, 16)
                for q in range(2):
                    sp.dma_start(sorted_recs[q][0:1, :], fence[0:1, :]).then_inc(recs_out, 16)
                    sp.dma_start(sorted_recs[q][SLOTS + 1:SLOTS + 2, :], fence[1:2, :]).then_inc(recs_out, 16)
                sp.wait_ge(recs_out, 80)

            @block.gpsimd
            def _(pool):
                nc.gpsimd.memset(raw_i[:, 0:2, :], PAD_KEY)
                nc.gpsimd.memset(raw_i[:, 2, :], 0)
                nc.gpsimd.memset(ident[:], 0.0)
                nc.gpsimd.memset(before[:], 1.0)
                nc.gpsimd.memset(not_before[:], 1.0)
                nc.gpsimd.memset(fence[:], PAD_KEY + 1).then_inc(filled, 1)
                pool.wait_ge(filled, 1)
                nc.gpsimd.affine_select(out=ident[:], in_=ident[:], compare_op=ALU.not_equal, fill=1.0,
                                        base=0, pattern=[[-1, P]], channel_multiplier=1)
                nc.gpsimd.affine_select(out=before[:], in_=before[:], compare_op=ALU.is_gt, fill=0.0,
                                        base=0, pattern=[[1, P]], channel_multiplier=-1)
                nc.gpsimd.affine_select(out=not_before[:], in_=not_before[:], compare_op=ALU.is_ge, fill=0.0,
                                        base=0, pattern=[[-1, P]], channel_multiplier=1)
                nc.gpsimd.iota(count_i[:], pattern=[[1, HI]], base=0, channel_multiplier=0)\
                    .then_inc(selected, 1)

            @block.tensor
            def _(pe):
                pe.wait_ge(loaded, 16 * 13)
                pe.wait_ge(selected, 1)
                pe.wait_ge(set_dve, 1)
                for n, (a, _) in enumerate(raw):
                    pe.transpose(bank[n][:, 0:D], a[:], ident[:]).then_inc(w_turned, 1)
                for n in range(2):
                    pe.transpose(bank[4 + n][:, 0:D], w_pre_raw[:, n * D:(n + 1) * D], ident[:])\
                        .then_inc(w_turned, 1)
                for n, b in enumerate((b0_row, b1_row)):
                    pe.matmul(bank[6 + n][:, 0:D], ones_row[:], b[:], start=True, stop=True)\
                        .then_inc(w_turned, 1)
                pe.wait_ge(w_copied, 8)
                for n in range(13):
                    to = bank[n // 4][:, (n % 4) * D:(n % 4 + 1) * D]
                    mm = pe.matmul(to, w_post_sb[:, n * D:(n + 1) * D], w_lin_t[:], start=True, stop=True)
                pe.matmul(bank[4][0:1, 0:D], b_post_col[:], w_lin_t[:], start=True, stop=True)\
                    .then_inc(merged, 1)
                pe.wait_ge(merged_out, 1)
                for n in range(3):
                    mm = pe.matmul(bank[5][0:1, 0:D], std_cols[:, n:n + 1], w_agg[:, 3, n * D:(n + 1) * D],
                                   start=(n == 0), stop=(n == 2))
                mm.then_inc(merged, 1)

            @block.vector
            def _(dve):
                dve.memset(ones16[:], 1.0)
                dve.memset(zeros16[:], 0.0)
                dve.memset(ones_row[:], 1.0)
                dve.memset(ones_step[:], 1.0)
                dve.memset(eps_col[:], EPS)
                dve.memset(one_col[:], 1.0)
                dve.memset(std_cols[:, 0:1], EPS ** 0.5)
                dve.memset(std_cols[:, 1:2], EPS ** 0.5 * LN2)
                dve.memset(std_cols[:, 2:3], EPS ** 0.5 / LN2)
                dve.memset(rows_a[:], 0.0)
                dve.memset(rows_b[:], 0.0)
                dve.memset(dinv_in[:], 0.0)
                dve.memset(agg[:], 0.0)
                dve.memset(agg_max[:], 0.0)
                dve.memset(agg_min[:], 0.0)
                dve.memset(agg_sq[:], 0.0)
                dve.memset(agg_n[:], 0.0).then_inc(set_dve, 1)
                dve.wait_ge(selected, 1)
                dve.tensor_copy(count16[:], count_i[:])
                dve.wait_ge(edges_in, 48)
                for n in range(3):
                    dve.tensor_copy(rec_all[:, :, n], raw_i[:, n, :])
                dve.tensor_scalar(rec_all[:, :, 3], raw_i[:, 2, :], 0, None, ALU.bitwise_and)\
                    .then_inc(interleaved, 1)
                for n, (_, to) in enumerate(raw):
                    dve.wait_ge(w_turned, n + 1)
                    dve.tensor_copy(to[:], bank[n][:, 0:D]).then_inc(w_copied, 1)
                for n, to in enumerate((w_dst_t, w_src_t, b0_all, b1_all)):
                    dve.wait_ge(w_turned, n + 5)
                    dve.tensor_copy(to[:], bank[4 + n][:, 0:D]).then_inc(w_copied, 1)
                dve.wait_ge(merged, 1)
                dve.tensor_tensor(w_own[:], bank[0][:, 0:D], ident[:], ALU.add)
                dve.tensor_tensor(b2_row[:], bank[4][0:1, 0:D], b_lin_row[:], ALU.add)
                for n in range(1, 13):
                    a, s = (n - 1) % 4, (n - 1) // 4
                    last = dve.tensor_copy(w_agg[:, a, s * D:(s + 1) * D],
                                           bank[n // 4][:, (n % 4) * D:(n % 4 + 1) * D])
                last.then_inc(merged_out, 1)
                dve.wait_ge(merged, 2)
                dve.wait_ge(merged_out, 1)
                dve.tensor_tensor(b2_alone[:], bank[5][0:1, 0:D], b2_row[:], ALU.add)

        phase(set_up)

        SRC_LO, DST_LO, SRC_HI, DST_HI = 0, LO, 2 * LO, 2 * LO + HI
        FIELDS = ((0, SRC_LO, LO, 0), (1, DST_LO, LO, 0), (0, SRC_HI, HI, LO_BITS), (1, DST_HI, HI, LO_BITS))

        def digit_of(dve, to, field, par, shift):
            return dve.tensor_scalar(to, rec[:, par, :, field], shift, (LO - 1) if shift == 0 else 0xFFFF,
                                     ALU.logical_shift_right, ALU.bitwise_and)

        def census(block, sem):
            loaded = [sem(f"loaded{i}") for i in range(2)]
            digits_int = sem("digits_int")
            digits_ready = sem("digits_ready")
            onehots = sem("onehots")
            counted = sem("counted")
            copied = sem("copied")
            summed_up = sem("summed_up")
            places = sem("places")
            std_made = sem("std_made")
            inverted = sem("inverted")
            table_out = sem("table_out")

            @block.sync
            def _(sp):
                def load(h, par):
                    wait(sp, digits_int, 2 * h + par - 1)
                    sp.dma_start(rec[:, par], recs[bass.ds((2 * h + par) * G * P, G * P), :]
                                 .rearrange("(t p) c -> p t c", p=P)).then_inc(loaded[par], 16)
                pairs(sp, NG, load)
                sp.wait_ge(inverted, 1)
                sp.dma_start(dinv_table.rearrange("(c p l) a -> p c (l a)", c=HI_PARTS, l=LO),
                             degree[0:HI_ROWS, :].rearrange("p (c l) -> p c l", c=HI_PARTS))\
                    .then_inc(table_out, 16)
                sp.wait_ge(table_out, 16)

            @block.vector
            def _(dve):
                def step(h, par):
                    j = 2 * h + par
                    wait(dve, loaded[par], 16 * (h + 1))
                    wait(dve, onehots, G * j)
                    for n, (field, _, _, shift) in enumerate(FIELDS):
                        last = digit_of(dve, digit_i[:, n, :], field, par, shift)
                    last.then_inc(digits_int, 1)
                    wait(dve, digits_int, j + 1)
                    dve.tensor_copy(digit[:], digit_i[:]).then_inc(digits_ready, 1)
                    wait(dve, digits_ready, j + 1)
                    for t in range(G):
                        tile = G * j + t
                        side = (G * par + t) % 2
                        wait(dve, counted, tile - 1)
                        for n, (_, at, width, _) in enumerate(FIELDS):
                            last = dve.tensor_scalar(onehot[:, side, at:at + width], count16[:, 0:width],
                                                     digit[:, n, t:t + 1], None, ALU.is_equal)
                        last.then_inc(onehots, 1)
                pairs(dve, NG, step)
                dve.wait_ge(counted, TILES)
                dve.tensor_copy(totals[:, 0:2 * LO], bank[0][:])
                dve.tensor_copy(totals[:, SRC_HI:SRC_HI + HI], bank[1][:, 0:HI])
                dve.tensor_copy(totals[:, DST_HI:DST_HI + HI], bank[2][:, 0:HI]).then_inc(copied, 1)
                dve.wait_ge(copied, 1)
                for n, (_, at, width, _) in enumerate(FIELDS):
                    last = dve.tensor_tensor_scan(inclusive[:, at:at + width], ones_step[:, 0:width],
                                                  totals[:, at:at + width], 0.0, ALU.mult, ALU.add)
                last.then_inc(summed_up, 1)
                dve.wait_ge(summed_up, 1)
                dve.tensor_tensor(first_place[:], inclusive[:], totals[:], ALU.subtract).then_inc(places, 1)
                dve.wait_ge(places, 1)
                dve.tensor_scalar(first_place[:, SRC_HI:], first_place[:, SRC_HI:], 1.0, None, ALU.add)
                dve.wait_ge(std_made, 1)
                dve.reciprocal(degree[0:HI_ROWS, :], degree[0:HI_ROWS, :]).then_inc(inverted, 1)

            @block.scalar
            def _(act):
                act.wait_ge(counted, TILES)
                for n in range(2):
                    last = act.activation(degree[0:HI_ROWS, n * 512:(n + 1) * 512], bank[3 + n][0:HI_ROWS, :],
                                          ACT.Sqrt, bias=one_col[0:HI_ROWS, :])
                last.then_inc(std_made, 1)

            @block.tensor
            def _(pe):
                for n in range(5):
                    pe.matmul(bank[n][:], zeros16[:, 0:P], zeros16[:], start=True, stop=True)

                def step(h, par):
                    j = 2 * h + par
                    for t in range(G):
                        side = (G * par + t) % 2
                        wait(pe, onehots, G * j + t + 1)
                        pe.matmul(bank[0][:], ones16[:], onehot[:, side, 0:2 * LO], start=False, stop=True,
                                  skip_group_check=True)
                        pe.matmul(bank[1][:, 0:HI], ones16[:], onehot[:, side, SRC_HI:SRC_HI + HI],
                                  start=False, stop=True, skip_group_check=True)
                        pe.matmul(bank[2][:, 0:HI], ones16[:], onehot[:, side, DST_HI:DST_HI + HI],
                                  start=False, stop=True, skip_group_check=True)
                        for c in range(HI_PARTS):
                            at = DST_HI + c * HI_ROWS
                            mm = pe.matmul(bank[3 + c // 2][0:HI_ROWS, (c % 2) * LO:(c % 2 + 1) * LO],
                                           onehot[:, side, at:at + HI_ROWS], onehot[:, side, DST_LO:DST_LO + LO],
                                           start=False, stop=True, skip_group_check=True)
                        mm.then_inc(counted, 1)
                pairs(pe, NG, step)

        phase(census)

        def sort_pass(block, sem, table, to, field, at, width, shift):
            loaded = [sem(f"loaded{i}") for i in range(2)]
            digits_int = sem("digits_int")
            digits_ready = sem("digits_ready")
            onehots = sem("onehots")
            prefixed = sem("prefixed")
            ranked = sem("ranked")
            positions = sem("positions")
            placed = [sem(f"placed{i}") for i in range(2)]
            gated = sem("gated")

            @block.sync
            def _(sp):
                def load(h, par):
                    wait(sp, placed[par], 16 * G * h)
                    sp.dma_start(rec[:, par], table[bass.ds((2 * h + par) * G * P, G * P), :]
                                 .rearrange("(t p) c -> p t c", p=P)).then_inc(loaded[par], 16)
                pairs(sp, NG, load)

            @block.vector
            def _(dve):
                def step(h, par):
                    j = 2 * h + par
                    wait(dve, loaded[par], 16 * (h + 1))
                    wait(dve, onehots, G * j)
                    digit_of(dve, digit_i[:, 0, :], field, par, shift).then_inc(digits_int, 1)
                    wait(dve, digits_int, j + 1)
                    dve.tensor_copy(digit[:, 0, :], digit_i[:, 0, :]).then_inc(digits_ready, 1)
                    wait(dve, digits_ready, j + 1)

                    def make_onehot(t):
                        wait(dve, ranked, G * j + t - 1)
                        wait(dve, prefixed, 2 * (G * j + t - 1))
                        dve.tensor_scalar(onehot[:, (G * par + t) % 2, 0:width], count16[:, 0:width],
                                          digit[:, 0, t:t + 1], None, ALU.is_equal).then_inc(onehots, 1)
                    make_onehot(0)
                    for t in range(G):
                        if t + 1 < G:
                            make_onehot(t + 1)
                        wait(dve, onehots, G * j + t + 1)
                        wait(dve, ranked, G * j + t)
                        if t == 0:
                            wait(dve, positions, j)
                        wait(dve, prefixed, 2 * (G * j + t) + 1)
                        dve.tensor_tensor_reduce(
                            out=rank_terms[:, 0:width], in0=onehot[:, (G * par + t) % 2, 0:width],
                            in1=bank[0][:, 0:width], scale=1.0, scalar=0.0, op0=ALU.mult, op1=ALU.add,
                            accum_out=position[:, t:t + 1]).then_inc(ranked, 1)
                    wait(dve, ranked, G * (j + 1))
                    wait(dve, placed[par], 16 * G * h)
                    dve.tensor_copy(position_i[:, par], position[:]).then_inc(positions, 1)
                pairs(dve, NG, step)

            @block.tensor
            def _(pe):
                pe.matmul(bank[0][:, 0:width], ident[:], first_place[:, at:at + width], start=True, stop=True)

                def step(h, par):
                    j = 2 * h + par
                    for t in range(G):
                        one = onehot[:, (G * par + t) % 2, 0:width]
                        wait(pe, onehots, G * j + t + 1)
                        pe.matmul(bank[0][:, 0:width], before[:], one, start=False, stop=True,
                                  skip_group_check=True).then_inc(prefixed, 1)
                        wait(pe, ranked, G * j + t + 1)
                        pe.matmul(bank[0][:, 0:width], not_before[:], one, start=False, stop=True,
                                  skip_group_check=True).then_inc(prefixed, 1)
                pairs(pe, NG, step)

            @block.gpsimd
            def _(pool):
                bound = nc.gpsimd.to_reg(SLOTS + 1)

                def step(h, par):
                    wait(pool, positions, 2 * h + par + 1)
                    pool.sem_inc(gated, 1)
                    for t in range(G):
                        scatter(to, position_i[:, par, t:t + 1], rec[:, par, t, :], placed[par], bound)
                pairs(pool, NG, step)
                for par in range(2):
                    pool.wait_ge(placed[par], NG // 2 * 16 * G)
                    pool.sem_inc(gated, 1)

        def make_list(block, sem, q):
            loaded = sem("loaded")
            as_float = sem("as_float")
            flags = sem("flags")
            hidden = sem("hidden")
            ready = sem("ready")
            turned = sem("turned")
            copied = sem("copied")
            key, other = q, 1 - q

            @block.sync
            def _(sp):
                for half in range(2):
                    wait(sp, as_float, half)
                    wait(sp, flags, half)
                    for s in range(3):
                        first = half * HALF * P + s
                        sp.dma_start(prep[:, s], sorted_recs[q][first:first + HALF * P, :]
                                     .rearrange("(t p) c -> t p c", p=P)).then_inc(loaded, 16)

            @block.vector
            def _(dve):
                for half in range(2):
                    dve.wait_ge(loaded, 48 * (half + 1))
                    wait(dve, turned, half)
                    dve.tensor_copy(prep_f[:, 0], prep[:, 1, :, key])
                    dve.tensor_copy(prep_f[:, 1], prep[:, 1, :, other])
                    dve.tensor_copy(prep_f[:, 2].bitcast(I32), prep[:, 1, :, 2])
                    dve.tensor_tensor(prep_f[:, 3], prep[:, 1, :, key], prep[:, 0, :, key], ALU.is_equal)
                    dve.tensor_tensor(prep_f[:, 4], prep[:, 1, :, key], prep[:, 2, :, key], ALU.is_equal)\
                        .then_inc(as_float, 1)
                    dve.wait_ge(as_float, half + 1)
                    dve.tensor_scalar(prep_f[:, 5], prep_f[:, 4], float(FAR), None, ALU.mult)\
                        .then_inc(hidden, 1)
                    dve.wait_ge(hidden, half + 1)
                    dve.tensor_tensor(prep_f[:, 5], prep_f[:, 5], prep_f[:, 0], ALU.add).then_inc(flags, 1)
                    cols = slice(half * HALF, (half + 1) * HALF)
                    dve.wait_ge(turned, half + 1)
                    dve.tensor_copy(list_key[q][:, cols], bank[0][:, 0:HALF])
                    dve.tensor_copy(list_other[q][:, cols], bank[1][:, 0:HALF])
                    if q == 0:
                        dve.tensor_copy(list_w[:, cols], bank[2][:, 0:HALF])
                    dve.tensor_copy(list_keep[q][:, cols], bank[3][:, 0:HALF])
                    dve.tensor_copy(list_write[q][:, cols], bank[4][:, 0:HALF]).then_inc(copied, 1)

            @block.tensor
            def _(pe):
                for half in range(2):
                    pe.wait_ge(flags, half + 1)
                    wait(pe, copied, half)
                    for n, part in enumerate((0, 1, 2, 3, 5)):
                        mm = pe.transpose(bank[n][:, 0:HALF], prep_f[:, part], ident[0:HALF, 0:HALF])
                    mm.then_inc(turned, 1)

        for q, (lo_at, hi_at) in enumerate(((SRC_LO, SRC_HI), (DST_LO, DST_HI))):
            phase(sort_pass, recs, recs_lo[q], q, lo_at, LO, 0)
            phase(sort_pass, recs_lo[q], sorted_recs[q], q, hi_at, HI, LO_BITS)
            phase(make_list, q)

        class Norm:
            def __init__(self, sem, name):
                self.stats = sem(f"{name}_stats")
                self.moments = sem(f"{name}_moments")
                self.std = sem(f"{name}_std")
                self.rstd = sem(f"{name}_rstd")
                self.done = sem(f"{name}_done")

        def norm_moments(dve, ln, j, rows):
            for t in range(T):
                last = dve.bn_stats(stats[:, t, :], rows[:, t, :])
            last.then_inc(ln.stats, 1)
            wait(dve, ln.stats, j + 1)
            dve.sem_inc(dve_gate, 1)
            for t in range(T):
                last = dve.bn_aggr(moments[:, t, :], stats[:, t, :])
            last.then_inc(ln.moments, 1)

        def norm_std(act, ln, j):
            wait(act, ln.moments, j + 1)
            act.activation(std[:], moments[:, :, 1], ACT.Sqrt, bias=eps_col[:]).then_inc(ln.std, 1)

        def norm_rows(dve, ln, j, rows, to):
            wait(dve, ln.std, j + 1)
            dve.reciprocal(rstd[:], std[:]).then_inc(ln.rstd, 1)
            wait(dve, ln.rstd, j + 1)
            for t in range(T):
                last = dve.tensor_scalar(to[:, t, :], rows[:, t, :], moments[:, t, 0:1], rstd[:, t:t + 1],
                                         ALU.subtract, ALU.mult)
            last.then_inc(ln.done, 1)

        def sweep_steps(eng, body):
            body(0, 0)
            body(0, 1)
            with eng.Fori(1, SWEEP // 2 - 1, 1) as h:
                body(h, 0)
                body(h, 1)
            body(SWEEP // 2 - 1, 0)
            body(SWEEP // 2 - 1, 1)

        def ahead(eng, steps, first, second, apart=0):
            first(0, 0)
            first(0, 1)
            second(0, 0)
            first(1, 0)
            second(0, 1)
            first(1, 1)
            last = steps // 2 - 1
            with eng.Fori(1, last - apart, 1) as h:
                second(h, 0)
                first(h + 1, 0)
                second(h, 1)
                first(h + 1, 1)
            for h in range(last - apart, last):
                second(h, 0)
                first(h + 1, 0)
                second(h, 1)
                first(h + 1, 1)
            second(last, 0)
            second(last, 1)

        def sweep_one(block, sem):
            loaded = [sem(f"loaded{i}") for i in range(2)]
            stored = [sem(f"stored{i}") for i in range(2)]
            with_b0 = sem("with_b0")
            ln0 = Norm(sem, "y0")
            ln1 = Norm(sem, "y1")
            squares = sem("squares")
            fourths = sem("fourths")
            scaled = sem("scaled")
            with_b1 = sem("with_b1")
            turned = sem("turned")
            copied = sem("copied")
            projected = sem("projected")
            summed = sem("summed")

            @block.sync
            def _(sp):
                def load(h, par):
                    j = 2 * h + par
                    wait(sp, with_b0, j - 1)
                    wait(sp, fourths, j - 1)
                    wait(sp, scaled, j - 1)
                    sp.dma_start(rows_a[:, par], by_node(x, j)).then_inc(loaded[par], 16)
                    sp.dma_start(dinv_in[:, par].rearrange("p (t a) -> p t a", a=1),
                                 by_node(dinv_table[0:N, :], j)).then_inc(loaded[par], 16)

                def store(h, par):
                    j = 2 * h + par
                    wait(sp, scaled, j + 1)
                    if isinstance(j, int) and j == SWEEP - 1:
                        wait(sp, stored[1 - par], 48 * (h + 1))
                    sp.dma_start(by_node(u_table, j), fresh_b[:, par]).then_inc(stored[par], 16)
                    sp.dma_start(by_node(v_table, j), fresh_c[:, par]).then_inc(stored[par], 16)
                    wait(sp, ln1.done, j + 1)
                    sp.dma_start(by_node(y1_table, j), fresh[:, par]).then_inc(stored[par], 16)
                ahead(sp, SWEEP, load, store, apart=1)
                for par in range(2):
                    sp.wait_ge(stored[par], 48 * (SWEEP // 2))

            @block.vector
            def _(dve):
                def step(h, par):
                    j = 2 * h + par
                    wait(dve, loaded[par], 32 * (h + 1))
                    wait(dve, ln0.done, j)
                    dve.tensor_tensor(pre[:], rows_a[:, par], over_tiles(b0_all[:]), ALU.add)\
                        .then_inc(with_b0, 1)
                    wait(dve, scaled, j)
                    dve.tensor_tensor(scales[:, 0], dinv_in[:, par], dinv_in[:, par], ALU.mult)\
                        .then_inc(squares, 1)
                    wait(dve, squares, j + 1)
                    dve.tensor_tensor(scales[:, 1], scales[:, 0], dinv_in[:, par], ALU.mult)
                    dve.tensor_tensor(scales[:, 2], scales[:, 0], scales[:, 0], ALU.mult).then_inc(fourths, 1)
                    wait(dve, with_b0, j + 1)
                    norm_moments(dve, ln0, j, pre)
                    wait(dve, summed, j)
                    wait(dve, turned, j)
                    norm_rows(dve, ln0, j, pre, plain)
                    wait(dve, ln0.done, j + 1)
                    dve.tensor_tensor(pre_b[:], plain[:], over_tiles(b1_all[:]), ALU.add).then_inc(with_b1, 1)
                    wait(dve, with_b1, j + 1)
                    wait(dve, projected, j + 1)
                    for t in range(T):
                        last = dve.scalar_tensor_tensor(out=pre_b[:, t], in0=bank4(1)[:, t],
                                                        scalar=scales[:, 2, t:t + 1], in1=pre_b[:, t],
                                                        op0=ALU.mult, op1=ALU.add)
                    last.then_inc(summed, 1)
                    wait(dve, summed, j + 1)
                    norm_moments(dve, ln1, j, pre_b)
                    wait(dve, stored[par], 48 * h)
                    norm_rows(dve, ln1, j, pre_b, fresh[:, par])
                    wait(dve, ln1.done, j + 1)
                sweep_steps(dve, step)

            @block.scalar
            def _(act):
                def step(h, par):
                    j = 2 * h + par
                    norm_std(act, ln0, j)
                    wait(act, ln0.done, j + 1)
                    wait(act, turned, j + 1)
                    wait(act, projected, j)
                    act.copy(turned_a[:], bank[0][:]).then_inc(copied, 1)
                    wait(act, stored[par], 48 * h)
                    wait(act, loaded[par], 32 * (h + 1))
                    wait(act, fourths, j + 1)
                    for t in range(T):
                        act.activation(fresh_b[:, par, t], plain[:, t], ACT.Copy, scale=dinv_in[:, par, t:t + 1])
                        last = act.activation(fresh_c[:, par, t], plain[:, t], ACT.Copy,
                                              scale=scales[:, 1, t:t + 1])
                    last.then_inc(scaled, 1)
                    norm_std(act, ln1, j)
                sweep_steps(act, step)

            @block.tensor
            def _(pe):
                def step(h, par):
                    j = 2 * h + par
                    wait(pe, ln0.done, j + 1)
                    wait(pe, copied, j)
                    for t in range(T):
                        mm = pe.transpose(bank[0][:, t * P:(t + 1) * P], plain[:, t], ident[:])
                    mm.then_inc(turned, 1)
                    wait(pe, copied, j + 1)
                    wait(pe, summed, j)
                    for t in range(T):
                        mm = pe.matmul(bank[1][:, t * D:(t + 1) * D], turned_a[:, t * P:(t + 1) * P], w1_t[:],
                                       start=True, stop=True)
                    mm.then_inc(projected, 1)
                sweep_steps(pe, step)

        phase(sweep_one)

        def pool_steps(pool, sem, arrays, gathers, scatters, gathered, scattered, per_step):
            idx_ready = sem("idx_ready")

            def fetch(h, par):
                j = 2 * h + par
                wait(pool, gathered[par], per_step * h)
                wait(pool, scattered[par], 64 * h)
                pool.sem_inc(pool_gate, 1)
                for to, lists in arrays:
                    last = nc.gpsimd.tensor_copy(to[:, par], lists[:, bass.ds(j * T, T)])
                last.then_inc(idx_ready, 1)
                wait(pool, idx_ready, j + 1)
                pool.sem_inc(pool_gate, 1)
                gathers(h, par)
            ahead(pool, NSTEP, fetch, scatters)
            for par in range(2):
                pool.wait_ge(scattered[par], 64 * (NSTEP // 2))
                pool.sem_inc(pool_gate, 1)

        def keep_to_row_pe(pe, j, keep_in, keep_turned, keep_copied):
            wait(pe, keep_in, j + 1)
            wait(pe, keep_copied, j)
            for t in range(T):
                mm = pe.transpose(bank[0][:, t * P:(t + 1) * P], keep_cols[:, t:t + 1].broadcast_to([P, P]), ident[:])
            mm.then_inc(keep_turned, 1)

        def keep_to_cols_dve(dve, j, q, keep_in, keep_turned):
            wait(dve, keep_turned, j)
            dve.sem_inc(dve_gate, 1)
            dve.tensor_copy(keep_cols[:], list_keep[q][:, bass.ds(j * T, T)]).then_inc(keep_in, 1)

        def layer_0(block, sem):
            gathered = [sem(f"gathered{i}") for i in range(2)]
            scattered = [sem(f"scattered{i}") for i in range(2)]
            stored = [sem(f"stored{i}") for i in range(2)]
            keep_in = sem("keep_in")
            keep_turned = sem("keep_turned")
            keep_copied = sem("keep_copied")
            weighted = sem("weighted")
            turned = sem("turned")
            scanned = sem("scanned")
            projected = sem("projected")
            summed = sem("summed")
            dinv_kept = sem("dinv_kept")
            scaled = sem("scaled")
            ln = Norm(sem, "y0")

            @block.gpsimd
            def _(pool):
                bound = nc.gpsimd.to_reg(N - 1)

                def gathers(h, par):
                    j = 2 * h + par
                    wait(pool, turned, j - 1)
                    wait(pool, summed, j - 1)
                    wait(pool, dinv_kept, j - 1)
                    wait(pool, scaled, j - 1)
                    pool.sem_inc(pool_gate, 1)
                    for t in range(T):
                        gather(rows_a[:, par, t], x, idx_a[:, par, t:t + 1], gathered[par], bound)
                    for t in range(T):
                        gather(rows_b[:, par, t], x, idx_b[:, par, t:t + 1], gathered[par], bound)
                    for t in range(T):
                        gather(dinv_in[:, par, t:t + 1], dinv_table, idx_b[:, par, t:t + 1], gathered[par], bound)

                def scatters(h, par):
                    wait(pool, scaled, 2 * h + par + 1)
                    pool.sem_inc(pool_gate, 1)
                    for t in range(T):
                        scatter(u_table, idx_w[:, par, t:t + 1], fresh_b[:, par, t], scattered[par], bound)
                pool_steps(pool, sem, ((idx_a, list_other[0]), (idx_b, list_key[0]), (idx_w, list_write[0])),
                           gathers, scatters, gathered, scattered, 192)

            @block.sync
            def _(sp):
                def store(h, par):
                    j = 2 * h + par
                    wait(sp, scaled, j + 1)
                    sp.dma_start(by_slot(y0_slots, j), fresh[:, par]).then_inc(stored[par], 16)
                    sp.dma_start(by_slot(u_slots, j), fresh_b[:, par]).then_inc(stored[par], 16)
                pairs(sp, NSTEP, store)
                for par in range(2):
                    sp.wait_ge(stored[par], 32 * (NSTEP // 2))

            @block.vector
            def _(dve):
                def step(h, par):
                    j = 2 * h + par
                    keep_to_cols_dve(dve, j, 0, keep_in, keep_turned)
                    wait(dve, gathered[par], 192 * (h + 1))
                    dve.sem_inc(dve_gate, 1)
                    for t in range(T):
                        last = dve.tensor_scalar(rows_a[:, par, t], rows_a[:, par, t],
                                                 list_w[:, bass.ds(j * T + t, 1)], None, ALU.mult)
                    last.then_inc(weighted, 1)
                    dve.tensor_copy(dinv_own[:, bass.ds(j * T, T)], dinv_in[:, par]).then_inc(dinv_kept, 1)
                    wait(dve, turned, j + 1)
                    wait(dve, keep_copied, j + 1)
                    wait(dve, scanned, j)
                    wait(dve, projected, j - 1)
                    dve.tensor_tensor_scan(agg[:, par], keep_row[:, par], bank[1][:],
                                           agg[:, 1 - par, STEP - 1:STEP], ALU.mult, ALU.add).then_inc(scanned, 1)
                    wait(dve, projected, j + 1)
                    wait(dve, ln.done, j)
                    dve.tensor_tensor(pre[:], bank4(2), rows_b[:, par], ALU.add).then_inc(summed, 1)
                    wait(dve, summed, j + 1)
                    norm_moments(dve, ln, j, pre)
                    wait(dve, stored[par], 32 * h)
                    norm_rows(dve, ln, j, pre, fresh[:, par])
                pairs(dve, NSTEP, step)

            @block.scalar
            def _(act):
                def step(h, par):
                    j = 2 * h + par
                    wait(act, keep_turned, j + 1)
                    wait(act, scanned, j - 1)
                    act.copy(keep_row[:, par], bank[0][:]).then_inc(keep_copied, 1)
                    norm_std(act, ln, j)
                    wait(act, stored[par], 32 * h)
                    wait(act, scattered[par], 64 * h)
                    wait(act, gathered[par], 192 * (h + 1))
                    wait(act, ln.done, j + 1)
                    for t in range(T):
                        last = act.activation(fresh_b[:, par, t], fresh[:, par, t], ACT.Copy,
                                              scale=dinv_in[:, par, t:t + 1])
                    last.then_inc(scaled, 1)
                pairs(act, NSTEP, step)

            @block.tensor
            def _(pe):
                def step(h, par):
                    j = 2 * h + par
                    keep_to_row_pe(pe, j, keep_in, keep_turned, keep_copied)
                    wait(pe, weighted, j + 1)
                    wait(pe, scanned, j)
                    for t in range(T):
                        mm = pe.transpose(bank[1][:, t * P:(t + 1) * P], rows_a[:, par, t], ident[:])
                    mm.then_inc(turned, 1)
                    wait(pe, scanned, j + 1)
                    wait(pe, summed, j)
                    for t in range(T):
                        to = bank[2][:, t * D:(t + 1) * D]
                        pe.matmul(to, agg[:, par, t * P:(t + 1) * P], w0_sb[:], start=True, stop=False)
                        mm = pe.matmul(to, ones_row[:], b0_row[:], start=False, stop=True)
                    mm.then_inc(projected, 1)
                pairs(pe, NSTEP, step)

        phase(layer_0)

        def hop_1(block, sem):
            gathered = [sem(f"gathered{i}") for i in range(2)]
            scattered = [sem(f"scattered{i}") for i in range(2)]
            stored = [sem(f"stored{i}") for i in range(2)]
            loaded = [sem(f"loaded{i}") for i in range(2)]
            keep_in = sem("keep_in")
            keep_turned = sem("keep_turned")
            keep_copied = sem("keep_copied")
            turned = sem("turned")
            scanned = sem("scanned")
            returned = sem("returned")
            summed = sem("summed")
            inv_deg = sem("inv_deg")
            hopped = sem("hopped")

            @block.gpsimd
            def _(pool):
                bound = nc.gpsimd.to_reg(N - 1)

                def gathers(h, par):
                    wait(pool, turned, 2 * h + par - 1)
                    pool.sem_inc(pool_gate, 1)
                    for t in range(T):
                        gather(rows_a[:, par, t], u_table, idx_a[:, par, t:t + 1], gathered[par], bound)

                def scatters(h, par):
                    wait(pool, hopped, 2 * h + par + 1)
                    pool.sem_inc(pool_gate, 1)
                    for t in range(T):
                        scatter(v_table, idx_w[:, par, t:t + 1], fresh[:, par, t], scattered[par], bound)
                pool_steps(pool, sem, ((idx_a, list_other[0]), (idx_w, list_write[0])),
                           gathers, scatters, gathered, scattered, 64)

            @block.sync
            def _(sp):
                def load(h, par):
                    j = 2 * h + par
                    wait(sp, summed, j - 1)
                    sp.dma_start(rows_b[:, par], by_slot(u_slots, j)).then_inc(loaded[par], 16)

                def store(h, par):
                    j = 2 * h + par
                    wait(sp, hopped, j + 1)
                    sp.dma_start(by_slot(v_slots, j), fresh[:, par]).then_inc(stored[par], 16)
                ahead(sp, NSTEP, load, store)
                for par in range(2):
                    sp.wait_ge(stored[par], 16 * (NSTEP // 2))

            @block.vector
            def _(dve):
                dve.tensor_tensor(dinv2_own[:], dinv_own[:], dinv_own[:], ALU.mult).then_inc(inv_deg, 1)
                dve.wait_ge(inv_deg, 1)

                def step(h, par):
                    j = 2 * h + par
                    keep_to_cols_dve(dve, j, 0, keep_in, keep_turned)
                    wait(dve, turned, j + 1)
                    wait(dve, keep_copied, j + 1)
                    wait(dve, scanned, j)
                    wait(dve, returned, j - 1)
                    dve.tensor_tensor_scan(agg[:, par], keep_row[:, par], bank[1][:],
                                           agg[:, 1 - par, STEP - 1:STEP], ALU.mult, ALU.add).then_inc(scanned, 1)
                    wait(dve, returned, j + 1)
                    wait(dve, loaded[par], 16 * (h + 1))
                    wait(dve, hopped, j)
                    dve.tensor_tensor(pre[:], bank4(2), rows_b[:, par], ALU.add).then_inc(summed, 1)
                pairs(dve, NSTEP, step)

            @block.scalar
            def _(act):
                act.wait_ge(inv_deg, 1)

                def step(h, par):
                    j = 2 * h + par
                    wait(act, keep_turned, j + 1)
                    wait(act, scanned, j - 1)
                    act.copy(keep_row[:, par], bank[0][:]).then_inc(keep_copied, 1)
                    wait(act, stored[par], 16 * h)
                    wait(act, scattered[par], 64 * h)
                    wait(act, summed, j + 1)
                    act.sem_inc(act_gate, 1)
                    for t in range(T):
                        last = act.activation(fresh[:, par, t], pre[:, t], ACT.Copy,
                                              scale=dinv2_own[:, bass.ds(j * T + t, 1)])
                    last.then_inc(hopped, 1)
                pairs(act, NSTEP, step)

            @block.tensor
            def _(pe):
                def step(h, par):
                    j = 2 * h + par
                    keep_to_row_pe(pe, j, keep_in, keep_turned, keep_copied)
                    wait(pe, gathered[par], 64 * (h + 1))
                    wait(pe, scanned, j)
                    for t in range(T):
                        mm = pe.transpose(bank[1][:, t * P:(t + 1) * P], rows_a[:, par, t], ident[:])
                    mm.then_inc(turned, 1)
                    wait(pe, scanned, j + 1)
                    wait(pe, summed, j)
                    for t in range(T):
                        mm = pe.transpose(bank[2][:, t * D:(t + 1) * D], agg[:, par, t * P:(t + 1) * P], ident[:])
                    mm.then_inc(returned, 1)
                pairs(pe, NSTEP, step)

        phase(hop_1)

        def hop_2(block, sem):
            gathered = [sem(f"gathered{i}") for i in range(2)]
            scattered = [sem(f"scattered{i}") for i in range(2)]
            loaded = [sem(f"loaded{i}") for i in range(2)]
            keep_in = sem("keep_in")
            keep_turned = sem("keep_turned")
            keep_copied = sem("keep_copied")
            turned = sem("turned")
            scanned = sem("scanned")
            own_turned = sem("own_turned")
            joined = sem("joined")
            projected = sem("projected")
            with_b1 = sem("with_b1")
            summed = sem("summed")
            ln = Norm(sem, "y1")

            @block.gpsimd
            def _(pool):
                bound = nc.gpsimd.to_reg(N - 1)

                def gathers(h, par):
                    wait(pool, turned, 2 * h + par - 1)
                    pool.sem_inc(pool_gate, 1)
                    for t in range(T):
                        gather(rows_a[:, par, t], v_table, idx_a[:, par, t:t + 1], gathered[par], bound)

                def scatters(h, par):
                    wait(pool, ln.done, 2 * h + par + 1)
                    pool.sem_inc(pool_gate, 1)
                    for t in range(T):
                        scatter(y1_table, idx_w[:, par, t:t + 1], fresh[:, par, t], scattered[par], bound)
                pool_steps(pool, sem, ((idx_a, list_other[0]), (idx_w, list_write[0])),
                           gathers, scatters, gathered, scattered, 64)

            @block.sync
            def _(sp):
                def load(h, par):
                    j = 2 * h + par
                    wait(sp, own_turned, j - 1)
                    wait(sp, with_b1, j - 1)
                    sp.dma_start(rows_b[:, par], by_slot(v_slots, j)).then_inc(loaded[par], 16)
                    sp.dma_start(rows_c[:, par], by_slot(y0_slots, j)).then_inc(loaded[par], 16)
                pairs(sp, NSTEP, load)

            @block.vector
            def _(dve):
                def step(h, par):
                    j = 2 * h + par
                    keep_to_cols_dve(dve, j, 0, keep_in, keep_turned)
                    wait(dve, loaded[par], 32 * (h + 1))
                    wait(dve, ln.done, j)
                    dve.tensor_tensor(pre[:], rows_c[:, par], over_tiles(b1_all[:]), ALU.add).then_inc(with_b1, 1)
                    wait(dve, turned, j + 1)
                    wait(dve, keep_copied, j + 1)
                    wait(dve, scanned, j)
                    wait(dve, joined, j)
                    dve.tensor_tensor_scan(agg[:, par], keep_row[:, par], bank[1][:],
                                           agg[:, 1 - par, STEP - 1:STEP], ALU.mult, ALU.add).then_inc(scanned, 1)
                    wait(dve, scanned, j + 1)
                    wait(dve, own_turned, j + 1)
                    wait(dve, projected, j)
                    dve.tensor_tensor(turned_a[:], bank[3][:], agg[:, par], ALU.add).then_inc(joined, 1)
                    wait(dve, projected, j + 1)
                    wait(dve, with_b1, j + 1)
                    dve.sem_inc(dve_gate, 1)
                    for t in range(T):
                        last = dve.scalar_tensor_tensor(out=pre[:, t], in0=bank4(2)[:, t],
                                                        scalar=dinv_own[:, bass.ds(j * T + t, 1)], in1=pre[:, t],
                                                        op0=ALU.mult, op1=ALU.add)
                    last.then_inc(summed, 1)
                    wait(dve, summed, j + 1)
                    norm_moments(dve, ln, j, pre)
                    wait(dve, scattered[par], 64 * h)
                    norm_rows(dve, ln, j, pre, fresh[:, par])
                pairs(dve, NSTEP, step)

            @block.scalar
            def _(act):
                def step(h, par):
                    j = 2 * h + par
                    wait(act, keep_turned, j + 1)
                    wait(act, scanned, j - 1)
                    act.copy(keep_row[:, par], bank[0][:]).then_inc(keep_copied, 1)
                    norm_std(act, ln, j)
                pairs(act, NSTEP, step)

            @block.tensor
            def _(pe):
                def step(h, par):
                    j = 2 * h + par
                    keep_to_row_pe(pe, j, keep_in, keep_turned, keep_copied)
                    wait(pe, loaded[par], 32 * (h + 1))
                    wait(pe, joined, j)
                    for t in range(T):
                        mm = pe.transpose(bank[3][:, t * P:(t + 1) * P], rows_b[:, par, t], ident[:])
                    mm.then_inc(own_turned, 1)
                    wait(pe, gathered[par], 64 * (h + 1))
                    wait(pe, scanned, j)
                    for t in range(T):
                        mm = pe.transpose(bank[1][:, t * P:(t + 1) * P], rows_a[:, par, t], ident[:])
                    mm.then_inc(turned, 1)
                    wait(pe, joined, j + 1)
                    wait(pe, summed, j)
                    for t in range(T):
                        mm = pe.matmul(bank[2][:, t * D:(t + 1) * D], turned_a[:, t * P:(t + 1) * P], w1_t[:],
                                       start=True, stop=True)
                    mm.then_inc(projected, 1)
                pairs(pe, NSTEP, step)

        phase(hop_2)

        def sweep_two(block, sem):
            loaded = [sem(f"loaded{i}") for i in range(2)]
            stored = [sem(f"stored{i}") for i in range(2)]
            turned = sem("turned")
            copied = sem("copied")
            projected = sem("projected")
            turned_2 = sem("turned_2")
            copied_2 = sem("copied_2")
            projected_2 = sem("projected_2")
            summed = sem("summed")
            ln2 = Norm(sem, "y2")
            ln3 = Norm(sem, "y3")

            @block.sync
            def _(sp):
                def load(h, par):
                    j = 2 * h + par
                    wait(sp, turned, j - 1)
                    sp.dma_start(rows_a[:, par], by_node(y1_table, j)).then_inc(loaded[par], 16)

                def store(h, par):
                    j = 2 * h + par
                    wait(sp, ln2.done, j + 1)
                    if isinstance(j, int) and j == SWEEP - 1:
                        wait(sp, stored[1 - par], 32 * (h + 1))
                    sp.dma_start(by_node(y2_table, j), fresh_b[:, par]).then_inc(stored[par], 16)
                    wait(sp, ln3.done, j + 1)
                    sp.dma_start(by_node(out, j), fresh[:, par]).then_inc(stored[par], 16)
                ahead(sp, SWEEP, load, store, apart=1)
                for par in range(2):
                    sp.wait_ge(stored[par], 32 * (SWEEP // 2))

            @block.vector
            def _(dve):
                def step(h, par):
                    j = 2 * h + par
                    wait(dve, projected, j + 1)
                    norm_moments(dve, ln2, j, bank4(1))
                    wait(dve, stored[par], 32 * h)
                    norm_rows(dve, ln2, j, bank4(1), fresh_b[:, par])
                    wait(dve, projected_2, j + 1)
                    wait(dve, ln2.done, j + 1)
                    wait(dve, ln3.done, j)
                    dve.scalar_tensor_tensor(out=pre[:], in0=bank4(3), scalar=0.0, in1=fresh_b[:, par],
                                             op0=ALU.max, op1=ALU.add).then_inc(summed, 1)
                    wait(dve, summed, j + 1)
                    norm_moments(dve, ln3, j, pre)
                    norm_rows(dve, ln3, j, pre, fresh[:, par])
                sweep_steps(dve, step)

            @block.scalar
            def _(act):
                def step(h, par):
                    j = 2 * h + par
                    wait(act, turned, j + 1)
                    wait(act, projected, j)
                    act.copy(turned_a[:], bank[0][:]).then_inc(copied, 1)
                    norm_std(act, ln2, j)
                    wait(act, turned_2, j + 1)
                    wait(act, projected_2, j)
                    act.copy(turned_b[:], bank[2][:]).then_inc(copied_2, 1)
                    norm_std(act, ln3, j)
                sweep_steps(act, step)

            @block.tensor
            def _(pe):
                def step(h, par):
                    j = 2 * h + par
                    wait(pe, loaded[par], 16 * (h + 1))
                    wait(pe, copied, j)
                    for t in range(T):
                        mm = pe.transpose(bank[0][:, t * P:(t + 1) * P], rows_a[:, par, t], ident[:])
                    mm.then_inc(turned, 1)
                    wait(pe, copied, j + 1)
                    wait(pe, ln2.done, j)
                    for t in range(T):
                        to = bank[1][:, t * D:(t + 1) * D]
                        pe.matmul(to, turned_a[:, t * P:(t + 1) * P], w_own[:], start=True, stop=False)
                        mm = pe.matmul(to, ones_row[:], b2_alone[:], start=False, stop=True)
                    mm.then_inc(projected, 1)
                    wait(pe, ln2.done, j + 1)
                    wait(pe, copied_2, j)
                    for t in range(T):
                        mm = pe.transpose(bank[2][:, t * P:(t + 1) * P], fresh_b[:, par, t], ident[:])
                    mm.then_inc(turned_2, 1)
                    wait(pe, copied_2, j + 1)
                    wait(pe, summed, j)
                    for t in range(T):
                        to = bank[3][:, t * D:(t + 1) * D]
                        pe.matmul(to, turned_b[:, t * P:(t + 1) * P], w_r_t[:], start=True, stop=False)
                        mm = pe.matmul(to, ones_row[:], b3_row[:], start=False, stop=True)
                    mm.then_inc(projected_2, 1)
                sweep_steps(pe, step)

        phase(sweep_two)

        def layer_2(block, sem):
            gathered = [sem(f"gathered{i}") for i in range(2)]
            scattered = [sem(f"scattered{i}") for i in range(2)]
            stored = [sem(f"stored{i}") for i in range(2)]
            keep_in = sem("keep_in")
            keep_turned = sem("keep_turned")
            keep_copied = sem("keep_copied")
            turned_own = sem("turned_own")
            turned_src = sem("turned_src")
            copied_own = sem("copied_own")
            copied_src = sem("copied_src")
            message = sem("message")
            messages_out = sem("messages_out")
            summed_n = sem("summed_n")
            summed_m = sem("summed_m")
            summed_sq = sem("summed_sq")
            found_max = sem("found_max")
            found_min = sem("found_min")
            inverted = sem("inverted")
            mean_made = sem("mean_made")
            mean_squared = sem("mean_squared")
            sq_scaled = sem("sq_scaled")
            var_made = sem("var_made")
            var_cut = sem("var_cut")
            dev_made = sem("dev_made")
            n_turned = sem("n_turned")
            log_made = sem("log_made")
            scales_made = sem("scales_made")
            projected = sem("projected")
            plain_out = sem("plain_out")
            amplified = sem("amplified")
            summed = sem("summed")
            ln = Norm(sem, "y2")

            @block.gpsimd
            def _(pool):
                bound = nc.gpsimd.to_reg(N - 1)

                def gathers(h, par):
                    j = 2 * h + par
                    wait(pool, turned_own, j - 1)
                    wait(pool, turned_src, j - 1)
                    pool.sem_inc(pool_gate, 1)
                    for t in range(T):
                        gather(rows_a[:, par, t], y1_table, idx_a[:, par, t:t + 1], gathered[par], bound)
                    for t in range(T):
                        gather(rows_b[:, par, t], y1_table, idx_b[:, par, t:t + 1], gathered[par], bound)

                def scatters(h, par):
                    wait(pool, ln.done, 2 * h + par + 1)
                    pool.sem_inc(pool_gate, 1)
                    for t in range(T):
                        scatter(y2_table, idx_w[:, par, t:t + 1], fresh[:, par, t], scattered[par], bound)
                pool_steps(pool, sem, ((idx_a, list_key[1]), (idx_b, list_other[1]), (idx_w, list_write[1])),
                           gathers, scatters, gathered, scattered, 128)

            @block.sync
            def _(sp):
                def store(h, par):
                    j = 2 * h + par
                    wait(sp, ln.done, j + 1)
                    sp.dma_start(by_slot(y2_slots, j), fresh[:, par]).then_inc(stored[par], 16)
                pairs(sp, NSTEP, store)
                for par in range(2):
                    sp.wait_ge(stored[par], 16 * (NSTEP // 2))

            @block.tensor
            def _(pe):
                def step(h, par):
                    j = 2 * h + par
                    keep_to_row_pe(pe, j, keep_in, keep_turned, keep_copied)
                    wait(pe, gathered[par], 128 * (h + 1))
                    wait(pe, copied_own, j)
                    for t in range(T):
                        mm = pe.transpose(bank[1][:, t * P:(t + 1) * P], rows_a[:, par, t], ident[:])
                    mm.then_inc(turned_own, 1)
                    wait(pe, copied_src, j)
                    for t in range(T):
                        mm = pe.transpose(bank[2][:, t * P:(t + 1) * P], rows_b[:, par, t], ident[:])
                    mm.then_inc(turned_src, 1)
                    wait(pe, copied_own, j + 1)
                    wait(pe, copied_src, j + 1)
                    wait(pe, messages_out, j)
                    pe.matmul(bank[3][:], w_dst_t[:], turned_a[:], start=True, stop=False)
                    pe.matmul(bank[3][:], w_src_t[:], turned_b[:], start=False, stop=True).then_inc(message, 1)
                    wait(pe, summed_n, j + 1)
                    wait(pe, log_made, j)
                    wait(pe, inverted, j)
                    for t in range(T):
                        mm = pe.matmul(bank[4][:, t:t + 1], agg_n[:, par, t * P:(t + 1) * P], ident[:, 0:1],
                                       start=True, stop=True)
                    mm.then_inc(n_turned, 1)
                    wait(pe, found_max, j + 1)
                    wait(pe, found_min, j + 1)
                    wait(pe, mean_made, j + 1)
                    wait(pe, dev_made, j + 1)
                    for t in range(T):
                        tile = T * j + t
                        cols = slice(t * P, (t + 1) * P)
                        wait(pe, summed, tile - 1)
                        wait(pe, plain_out, tile - 1)
                        to = bank[5 + t % 2]
                        pe.matmul(to[:, 0:D], turned_a[:, cols], w_own[:], start=True, stop=False,
                                  skip_group_check=True)
                        pe.matmul(to[:, 0:D], ones_row[:], b2_row[:], start=False, stop=False,
                                  skip_group_check=True)
                        for n, a in enumerate((agg_max[:, par, cols], agg_min[:, par, cols], mean[:, cols],
                                               dev[:, cols])):
                            mm = pe.matmul(to[:, 0:3 * D], a, w_agg[:, n], start=False, stop=(n == 3),
                                           skip_group_check=True)
                        mm.then_inc(projected, 1)
                pairs(pe, NSTEP, step)

            @block.scalar
            def _(act):
                def step(h, par):
                    j = 2 * h + par
                    wait(act, keep_turned, j + 1)
                    wait(act, summed_sq, j - 1)
                    wait(act, found_min, j - 1)
                    act.copy(keep_row[:, par], bank[0][:])
                    act.activation(low_row[:, par], bank[0][:], ACT.Copy, scale=BIG, bias=-BIG)
                    act.activation(high_row[:, par], bank[0][:], ACT.Copy, scale=-BIG, bias=BIG)\
                        .then_inc(keep_copied, 1)
                    wait(act, turned_own, j + 1)
                    wait(act, projected, T * j)
                    act.copy(turned_a[:], bank[1][:]).then_inc(copied_own, 1)
                    wait(act, message, j + 1)
                    wait(act, summed_sq, j)
                    wait(act, found_min, j)
                    act.activation(msg[:], bank[3][:], ACT.Identity, bias=b_pre_col[:])
                    act.activation(msg_sq[:], bank[3][:], ACT.Square, bias=b_pre_col[:]).then_inc(messages_out, 1)
                    wait(act, mean_made, j + 1)
                    wait(act, var_made, j)
                    act.activation(mean_sq[:], mean[:], ACT.Square).then_inc(mean_squared, 1)
                    wait(act, n_turned, j + 1)
                    wait(act, scales_made, j)
                    wait(act, summed, T * j)
                    act.activation(scales[:, 1], bank[4][:, 0:T], ACT.Ln, bias=one_col[:]).then_inc(log_made, 1)
                    wait(act, var_cut, j + 1)
                    act.activation(dev[:], var[:], ACT.Sqrt, bias=eps_col[:]).then_inc(dev_made, 1)
                    for t in range(T):
                        tile = T * j + t
                        wait(act, projected, tile + 1)
                        wait(act, amplified, tile)
                        act.copy(plain[:, t], bank[5 + t % 2][:, 0:D]).then_inc(plain_out, 1)
                    norm_std(act, ln, j)
                pairs(act, NSTEP, step)

            @block.vector
            def _(dve):
                def step(h, par):
                    j = 2 * h + par
                    keep_to_cols_dve(dve, j, 1, keep_in, keep_turned)
                    wait(dve, turned_src, j + 1)
                    wait(dve, message, j)
                    dve.tensor_copy(turned_b[:], bank[2][:]).then_inc(copied_src, 1)
                    wait(dve, keep_copied, j + 1)
                    wait(dve, summed_n, j)
                    last_of = slice(STEP - 1, STEP)
                    dve.tensor_tensor_scan(agg_n[:, par], keep_row[:, par], ones_step[:],
                                           agg_n[:, 1 - par, last_of], ALU.mult, ALU.add).then_inc(summed_n, 1)
                    wait(dve, summed_n, j + 1)
                    dve.reciprocal(inv_n[:], agg_n[:, par])
                    wait(dve, n_turned, j + 1)
                    dve.sem_inc(dve_gate, 1)
                    dve.reciprocal(inv_count[:, bass.ds(j * T, T)], bank[4][:, 0:T]).then_inc(inverted, 1)
                    wait(dve, messages_out, j + 1)
                    wait(dve, projected, T * (j - 1))
                    dve.tensor_tensor_scan(agg[:, par], keep_row[:, par], msg[:],
                                           agg[:, 1 - par, last_of], ALU.mult, ALU.add).then_inc(summed_m, 1)
                    wait(dve, summed_m, j + 1)
                    wait(dve, inverted, j + 1)
                    wait(dve, projected, T * j)
                    dve.tensor_tensor(mean[:], agg[:, par], inv_n[:], ALU.mult).then_inc(mean_made, 1)
                    dve.tensor_tensor_scan(agg_sq[:, par], keep_row[:, par], msg_sq[:],
                                           agg_sq[:, 1 - par, last_of], ALU.mult, ALU.add).then_inc(summed_sq, 1)
                    wait(dve, summed_sq, j + 1)
                    wait(dve, dev_made, j)
                    dve.tensor_tensor(var[:], agg_sq[:, par], inv_n[:], ALU.mult).then_inc(sq_scaled, 1)
                    wait(dve, sq_scaled, j + 1)
                    wait(dve, mean_squared, j + 1)
                    dve.tensor_tensor(var[:], var[:], mean_sq[:], ALU.subtract).then_inc(var_made, 1)
                    wait(dve, var_made, j + 1)
                    dve.tensor_scalar(var[:], var[:], 0.0, None, ALU.max).then_inc(var_cut, 1)
                    wait(dve, found_max, j)
                    dve.tensor_tensor_scan(agg_max[:, par], low_row[:, par], msg[:],
                                           agg_max[:, 1 - par, last_of], ALU.add, ALU.max).then_inc(found_max, 1)
                    wait(dve, found_min, j)
                    dve.tensor_tensor_scan(agg_min[:, par], high_row[:, par], msg[:],
                                           agg_min[:, 1 - par, last_of], ALU.add, ALU.min).then_inc(found_min, 1)
                    wait(dve, log_made, j + 1)
                    wait(dve, summed, T * j)
                    dve.reciprocal(scales[:, 2], scales[:, 1]).then_inc(scales_made, 1)
                    wait(dve, scales_made, j + 1)
                    wait(dve, ln.done, j)
                    for t in range(T):
                        tile = T * j + t
                        psum = bank[5 + t % 2]
                        wait(dve, plain_out, tile + 1)
                        dve.scalar_tensor_tensor(out=pre[:, t], in0=psum[:, D:2 * D], scalar=scales[:, 1, t:t + 1],
                                                 in1=plain[:, t], op0=ALU.mult, op1=ALU.add).then_inc(amplified, 1)
                        wait(dve, amplified, tile + 1)
                        dve.scalar_tensor_tensor(out=pre[:, t], in0=psum[:, 2 * D:3 * D],
                                                 scalar=scales[:, 2, t:t + 1], in1=pre[:, t],
                                                 op0=ALU.mult, op1=ALU.add).then_inc(summed, 1)
                    wait(dve, summed, T * (j + 1))
                    norm_moments(dve, ln, j, pre)
                    wait(dve, stored[par], 16 * h)
                    wait(dve, scattered[par], 64 * h)
                    norm_rows(dve, ln, j, pre, fresh[:, par])
                pairs(dve, NSTEP, step)

        phase(layer_2)

        def layer_3(block, sem):
            gathered = [sem(f"gathered{i}") for i in range(2)]
            scattered = [sem(f"scattered{i}") for i in range(2)]
            loaded = [sem(f"loaded{i}") for i in range(2)]
            keep_in = sem("keep_in")
            keep_turned = sem("keep_turned")
            keep_copied = sem("keep_copied")
            turned = sem("turned")
            scanned = sem("scanned")
            own_turned = sem("own_turned")
            own_copied = sem("own_copied")
            own_projected = sem("own_projected")
            own_out = sem("own_out")
            projected = sem("projected")
            joined = sem("joined")
            summed = sem("summed")
            ln = Norm(sem, "y3")

            @block.gpsimd
            def _(pool):
                bound = nc.gpsimd.to_reg(N - 1)

                def gathers(h, par):
                    wait(pool, turned, 2 * h + par - 1)
                    pool.sem_inc(pool_gate, 1)
                    for t in range(T):
                        gather(rows_a[:, par, t], y2_table, idx_a[:, par, t:t + 1], gathered[par], bound)

                def scatters(h, par):
                    wait(pool, ln.done, 2 * h + par + 1)
                    pool.sem_inc(pool_gate, 1)
                    for t in range(T):
                        scatter(out, idx_w[:, par, t:t + 1], fresh[:, par, t], scattered[par], bound)
                pool_steps(pool, sem, ((idx_a, list_other[1]), (idx_w, list_write[1])),
                           gathers, scatters, gathered, scattered, 64)

            @block.sync
            def _(sp):
                def load(h, par):
                    j = 2 * h + par
                    wait(sp, own_turned, j - 1)
                    wait(sp, summed, j - 1)
                    sp.dma_start(rows_b[:, par], by_slot(y2_slots, j)).then_inc(loaded[par], 16)
                pairs(sp, NSTEP, load)

            @block.vector
            def _(dve):
                def step(h, par):
                    j = 2 * h + par
                    keep_to_cols_dve(dve, j, 1, keep_in, keep_turned)
                    wait(dve, turned, j + 1)
                    wait(dve, keep_copied, j + 1)
                    wait(dve, scanned, j)
                    wait(dve, projected, j - 1)
                    dve.tensor_tensor_scan(agg[:, par], keep_row[:, par], bank[1][:],
                                           agg[:, 1 - par, STEP - 1:STEP], ALU.mult, ALU.add).then_inc(scanned, 1)
                    wait(dve, projected, j + 1)
                    wait(dve, own_out, j + 1)
                    wait(dve, ln.done, j)
                    dve.sem_inc(dve_gate, 1)
                    for t in range(T):
                        last = dve.scalar_tensor_tensor(out=pre_b[:, t], in0=bank4(2)[:, t],
                                                        scalar=inv_count[:, bass.ds(j * T + t, 1)],
                                                        in1=plain[:, t], op0=ALU.mult, op1=ALU.add)
                    last.then_inc(joined, 1)
                    wait(dve, joined, j + 1)
                    dve.scalar_tensor_tensor(out=pre[:], in0=pre_b[:], scalar=0.0, in1=rows_b[:, par],
                                             op0=ALU.max, op1=ALU.add).then_inc(summed, 1)
                    wait(dve, summed, j + 1)
                    norm_moments(dve, ln, j, pre)
                    wait(dve, scattered[par], 64 * h)
                    norm_rows(dve, ln, j, pre, fresh[:, par])
                pairs(dve, NSTEP, step)

            @block.scalar
            def _(act):
                def step(h, par):
                    j = 2 * h + par
                    wait(act, keep_turned, j + 1)
                    wait(act, scanned, j - 1)
                    act.copy(keep_row[:, par], bank[0][:]).then_inc(keep_copied, 1)
                    wait(act, own_turned, j + 1)
                    wait(act, own_projected, j)
                    act.copy(turned_a[:], bank[3][:]).then_inc(own_copied, 1)
                    wait(act, own_projected, j + 1)
                    wait(act, joined, j)
                    act.copy(plain[:], bank4(4)).then_inc(own_out, 1)
                    norm_std(act, ln, j)
                pairs(act, NSTEP, step)

            @block.tensor
            def _(pe):
                def step(h, par):
                    j = 2 * h + par
                    keep_to_row_pe(pe, j, keep_in, keep_turned, keep_copied)
                    wait(pe, loaded[par], 16 * (h + 1))
                    wait(pe, own_copied, j)
                    for t in range(T):
                        mm = pe.transpose(bank[3][:, t * P:(t + 1) * P], rows_b[:, par, t], ident[:])
                    mm.then_inc(own_turned, 1)
                    wait(pe, gathered[par], 64 * (h + 1))
                    wait(pe, scanned, j)
                    for t in range(T):
                        mm = pe.transpose(bank[1][:, t * P:(t + 1) * P], rows_a[:, par, t], ident[:])
                    mm.then_inc(turned, 1)
                    wait(pe, own_copied, j + 1)
                    wait(pe, own_out, j)
                    for t in range(T):
                        to = bank[4][:, t * D:(t + 1) * D]
                        pe.matmul(to, turned_a[:, t * P:(t + 1) * P], w_r_t[:], start=True, stop=False)
                        mm = pe.matmul(to, ones_row[:], b3_row[:], start=False, stop=True)
                    mm.then_inc(own_projected, 1)
                    wait(pe, scanned, j + 1)
                    wait(pe, joined, j)
                    for t in range(T):
                        mm = pe.matmul(bank[2][:, t * D:(t + 1) * D], agg[:, par, t * P:(t + 1) * P], w_l_t[:],
                                       start=True, stop=True)
                    mm.then_inc(projected, 1)
                pairs(pe, NSTEP, step)

        phase(layer_3)


_INS = ["x", "src", "dst", "edge_weight", "L0_gnn_weight", "L0_gnn_bias_param", "L1_gnn_W", "L1_gnn_b",
        "L2_gnn_W_pre", "L2_gnn_b_pre", "L2_gnn_W_post", "L2_gnn_b_post", "L2_gnn_W_lin", "L2_gnn_b_lin",
        "L3_gnn_W_l", "L3_gnn_W_r", "L3_gnn_b"]


def kernel(**inputs):
    import numpy as _np
    import concourse.bacc as _bacc
    from concourse.bass_utils import run_bass_kernel_spmd as _run

    nc = _bacc.Bacc("TRN2", target_bir_lowering=False, num_devices=1)
    arrays, args = {}, []
    for name in _INS:
        a = _np.ascontiguousarray(inputs[name])
        arrays[f"in_{name}_dram"] = a
        args.append(nc.dram_tensor(f"in_{name}_dram", a.shape, mybir.dt.from_np(a.dtype), kind="ExternalInput").ap())
    args.append(nc.dram_tensor("out_0_dram", (N, D), F32, kind="ExternalOutput").ap())
    gnn_kernel(nc, *args)
    r = _run(nc, [arrays], core_ids=[0])
    return r.results[0]["out_0_dram"]
```

```python
from contextlib import ExitStack

import concourse.bass as bass
from concourse import mybir

ALU = mybir.AluOpType
ACT = mybir.ActivationFunctionType
F32 = mybir.dt.float32
F16 = mybir.dt.float16
BF16 = mybir.dt.bfloat16
I32 = mybir.dt.int32

P = 128
D = 128
EPS = 1e-5
LN2 = 0.6931471805599453

N = 100000
E = 25000
T = 4
STEP = T * P
NSTEP = 50
SLOTS = NSTEP * STEP
TILES = SLOTS // P
PAD_KEY = N
EDGE_ROWS = E // TILES
FAR = 1 << 20

LO_BITS = 8
LO = 1 << LO_BITS
HI_PARTS = 4
HI_ROWS = -(-(N + 1) // (LO * HI_PARTS))
HI = HI_PARTS * HI_ROWS

G = 5
NG = TILES // G

SWEEP = -(-N // STEP)
HALF = TILES // 2
BIG = 3.0e38


def wait(eng, sem, count):
    if isinstance(count, int) and count <= 0:
        return
    eng.wait_ge(sem, count)


def pairs(eng, steps, body):
    body(0, 0)
    body(0, 1)
    with eng.Fori(1, steps // 2, 1) as h:
        body(h, 0)
        body(h, 1)


def staggered(eng, steps, stages, apart=0, unroll=2):
    def at(turn, place):
        for lag, body in stages:
            side = (place - lag) % unroll
            h = turn + (place - lag - side) // unroll
            if not isinstance(h, int) or 0 <= unroll * h + side < steps:
                body(h, side)
    lags = [lag for lag, _ in stages]
    first = -(-(max(lags) + unroll) // unroll)
    last = steps // unroll - apart
    for s in range(unroll * first):
        at(s // unroll, s % unroll)
    with eng.Fori(first, last, 1) as h:
        for place in range(unroll):
            at(h, place)
    for s in range(unroll * last, steps + max(lags)):
        at(s // unroll, s % unroll)


def gnn_kernel(nc, x, src, dst, edge_weight, w0, b0, w1, b1, w_pre, b_pre, w_post, b_post,
               w_lin, b_lin, w_l, w_r, b3, out):
    with ExitStack() as ctx:
        def sb(name, shape, dt=F32):
            return ctx.enter_context(nc.sbuf_tensor(name, shape, dt))

        def sem(name):
            return ctx.enter_context(nc.semaphore(name))

        def dram(name, shape, dt=F32):
            return nc.dram_tensor(name, shape, dt, kind="Internal").ap()

        recs = dram("recs", (SLOTS, 4), I32)
        recs_lo = [dram(f"recs_lo{q}", (SLOTS, 4), I32) for q in range(2)]
        sorted_recs = [dram(f"sorted_recs{q}", (SLOTS + 2, 4), I32) for q in range(2)]
        dinv_table = dram("dinv_table", (HI * LO, 1))
        u_table = dram("u_table", (N, D))
        v_table = dram("v_table", (N, D))
        y1_table = dram("y1_table", (N, D))
        y2_table = dram("y2_table", (N, D))
        y0_slots = dram("y0_slots", (SLOTS, D))
        u_slots = dram("u_slots", (SLOTS, D))
        v_slots = dram("v_slots", (SLOTS, D))
        y2_slots = dram("y2_slots", (SLOTS, D))

        bank = [ctx.enter_context(nc.psum_tensor(f"bank{i}", [P, 512], F32)) for i in range(8)]

        ident = sb("ident", [P, P])
        before = sb("before", [P, P], F16)
        not_before = sb("not_before", [P, P], F16)
        ones16 = sb("ones16", [P, P], F16)
        zeros16 = sb("zeros16", [P, 512], F16)
        count16 = sb("count16", [P, HI], F16)
        ones_row = sb("ones_row", [1, P])
        ones_step = sb("ones_step", [P, 512])
        eps_col = sb("eps_col", [P, 1])
        one_col = sb("one_col", [P, 1])
        w0_sb = sb("w0_sb", [P, D])
        w1_t = sb("w1_t", [P, D])
        w_dst_t = sb("w_dst_t", [P, D])
        w_src_t = sb("w_src_t", [P, D])
        w_lin_t = sb("w_lin_t", [P, D])
        w_l_t = sb("w_l_t", [P, D])
        w_r_t = sb("w_r_t", [P, D])
        w_own = sb("w_own", [P, D])
        w_agg = sb("w_agg", [P, 4, 3 * D])
        b_pre_col = sb("b_pre_col", [P, 1])
        center = sb("center", [P, P])
        w1_c = sb("w1_c", [P, D])
        w_r_c = sb("w_r_c", [P, D])
        w_two = sb("w_two", [P, 2 * D])
        bias3 = sb("bias3", [3, 6 * D], BF16)
        ones3 = sb("ones3", [3, P], BF16)
        b3_all = sb("b3_all", [P, D])
        b0_all = sb("b0_all", [P, D])
        b1_all = sb("b1_all", [P, D])

        list_w = sb("list_w", [P, TILES])
        list_key = [sb(f"list_key{q}", [P, TILES], I32) for q in range(2)]
        list_other = [sb(f"list_other{q}", [P, TILES], I32) for q in range(2)]
        list_write = [sb(f"list_write{q}", [P, TILES], I32) for q in range(2)]
        list_keep = [sb(f"list_keep{q}", [P, TILES]) for q in range(2)]
        dinv_own = sb("dinv_own", [P, TILES])
        dinv2_own = sb("dinv2_own", [P, TILES])
        inv_count = sb("inv_count", [P, TILES])

        rows_a = sb("rows_a", [P, 2, T, D])
        idx_a = sb("idx_a", [P, 4, T], I32)
        idx_b = sb("idx_b", [P, 4, T], I32)
        idx_w = sb("idx_w", [P, 4, T], I32)
        keep_cols = sb("keep_cols", [P, T])
        keep_row = sb("keep_row", [P, 2, STEP])
        low_row = sb("low_row", [P, 2, STEP])
        high_row = sb("high_row", [P, 2, STEP])
        agg = sb("agg", [P, 2, STEP])
        agg_max = sb("agg_max", [P, 2, STEP])
        agg_min = sb("agg_min", [P, 2, STEP])
        agg_sq = sb("agg_sq", [P, 2, STEP])
        agg_n = sb("agg_n", [P, 2, STEP])
        msg = sb("msg", [P, STEP])
        msg_sq = sb("msg_sq", [P, STEP])
        inv_n = sb("inv_n", [P, STEP])
        mean_sq = sb("mean_sq", [P, STEP])
        var = sb("var", [P, STEP])
        pre = sb("pre", [P, T, D])
        pre_b = sb("pre_b", [P, T, D])
        stats = sb("stats", [P, T, 6])
        moments = sb("moments", [P, T, 2])
        std = sb("std", [P, T])
        rstd = sb("rstd", [P, T])

        sort_memory = ExitStack()

        def sort_sb(name, shape, dt=F32):
            return sort_memory.enter_context(nc.sbuf_tensor(name, shape, dt))
        w1_raw = sort_sb("w1_raw", [P, D])
        w_pre_raw = sort_sb("w_pre_raw", [P, 2 * D])
        w_post_sb = sort_sb("w_post_sb", [P, 13 * D])
        w_lin_raw = sort_sb("w_lin_raw", [P, D])
        w_l_raw = sort_sb("w_l_raw", [P, D])
        w_r_raw = sort_sb("w_r_raw", [P, D])
        b0_row = sort_sb("b0_row", [1, D])
        b1_row = sort_sb("b1_row", [1, D])
        b3_row = sort_sb("b3_row", [1, D])
        b_lin_row = sort_sb("b_lin_row", [1, D])
        b_post_col = sort_sb("b_post_col", [P, 1])
        b2_row = sort_sb("b2_row", [1, D])
        b2_alone = sort_sb("b2_alone", [1, D])
        w_own_t = sort_sb("w_own_t", [P, D])
        b0_col = sort_sb("b0_col", [P, 1])
        b2_alone_col = sort_sb("b2_alone_col", [P, 1])
        bias = sort_sb("bias", [1, 6 * D])
        bias_rest = sort_sb("bias_rest", [1, 2, 6 * D])
        bias_part = sort_sb("bias_part", [1, 3, 6 * D], BF16)
        count_i = sort_sb("count_i", [P, HI], I32)
        std_cols = sort_sb("std_cols", [P, 3])
        raw_i = sort_sb("raw_i", [P, 3, TILES], I32)
        rec_all = sort_sb("rec_all", [P, TILES, 4], I32)
        rec = sort_sb("rec", [P, 2, G, 4], I32)
        digit_i = sort_sb("digit_i", [P, 4, G], I32)
        digit = sort_sb("digit", [P, 4, G])
        onehot = sort_sb("onehot", [P, 2, 2 * (LO + HI)], F16)
        rank_terms = sort_sb("rank_terms", [P, HI])
        position = sort_sb("position", [P, G])
        position_i = sort_sb("position_i", [P, 2, G], I32)
        totals = sort_sb("totals", [P, 2 * (LO + HI)])
        inclusive = sort_sb("inclusive", [P, 2 * (LO + HI)])
        first_place = sort_sb("first_place", [P, 2 * (LO + HI)])
        degree = sort_sb("degree", [P, HI_PARTS * LO])
        fence = sort_sb("fence", [2, 4], I32)
        prep = sort_sb("prep", [HALF, 3, P, 4], I32)
        prep_f = sort_sb("prep_f", [HALF, 6, P])


        def by_slot(table, j):
            return table[bass.ds(j * STEP, STEP), :].rearrange("(t p) d -> p t d", p=P)

        def by_node(table, j):
            start = N - STEP if isinstance(j, int) and j == SWEEP - 1 else j * STEP
            return table[bass.ds(start, STEP), :].rearrange("(p t) d -> p t d", t=T)

        def tiles(a):
            return a.rearrange("p (t d) -> p t d", t=T)

        def bank4(i):
            return tiles(bank[i][:])

        def over_tiles(a):
            return a.rearrange("p (t d) -> p t d", t=1).broadcast_to([P, T, D])

        def gather(to, table, idx, done, bound):
            nc.gpsimd.indirect_dma_start(
                out=to, out_offset=None, in_=table, in_offset=bass.IndirectOffsetOnAxis(ap=idx, axis=0),
                bounds_check=bound, oob_is_err=False).then_inc(done, 16)

        def scatter(table, idx, rows, done, bound):
            nc.gpsimd.indirect_dma_start(
                out=table, out_offset=bass.IndirectOffsetOnAxis(ap=idx, axis=0), in_=rows, in_offset=None,
                bounds_check=bound, oob_is_err=False).then_inc(done, 16)

        pool_gate = nc.alloc_semaphore("pool_gate")
        dve_gate = nc.alloc_semaphore("dve_gate")
        act_gate = nc.alloc_semaphore("act_gate")

        def phase(build, *args):
            sems = []

            def sem(name):
                sems.append(nc.alloc_semaphore(f"{name}_{len(sems)}_{nc.next_id()}"))
                return sems[-1]
            block = nc.Block()
            with block as b:
                build(b, sem, *args)
            nc.clear_and_free_semaphores(sems)
            nc.all_engine_barrier()

        BIAS_ONE, BIAS_TWO, BIAS_B0, BIAS_B2, BIAS_B3 = 0, D, 3 * D, 4 * D, 5 * D

        def add_bias(pe, to, at, width=D, last=True):
            return pe.matmul(to, ones3[:], bias3[:, at:at + width], start=False, stop=last,
                             skip_group_check=not last)

        def set_up(block, sem):
            filled = sem("filled")
            set_dve = sem("set_dve")
            selected = sem("selected")
            loaded = sem("loaded")
            edges_in = sem("edges_in")
            counted = sem("counted")
            interleaved = sem("interleaved")
            recs_out = sem("recs_out")
            w_turned = sem("w_turned")
            w_copied = sem("w_copied")
            merged = sem("merged")
            merged_out = sem("merged_out")
            bias_made = sem("bias_made")
            bias_split = sem("bias_split")
            raw = ((w1_raw, w1_t), (w_lin_raw, w_lin_t), (w_l_raw, w_l_t), (w_r_raw, w_r_t))

            @block.sync
            def _(sp):
                for to, what in ((w0_sb, w0), (w1_raw, w1), (w_pre_raw, w_pre), (w_post_sb, w_post),
                                 (w_lin_raw, w_lin), (w_l_raw, w_l), (w_r_raw, w_r)):
                    sp.dma_start(to[:], what).then_inc(loaded, 16)
                for to, what in ((b0_row, b0), (b1_row, b1), (b3_row, b3), (b_lin_row, b_lin)):
                    sp.dma_start(to[:], what.rearrange("(a d) -> a d", a=1)).then_inc(loaded, 16)
                for to, what in ((b_post_col, b_post), (b_pre_col, b_pre), (b0_col, b0)):
                    sp.dma_start(to[:], what.rearrange("(d a) -> d a", a=1)).then_inc(loaded, 16)
                sp.wait_ge(filled, 1)
                for n, what in enumerate((src, dst)):
                    sp.dma_start(raw_i[0:EDGE_ROWS, n, :], what.rearrange("(p j) -> p j", j=TILES))\
                        .then_inc(edges_in, 16)
                sp.dma_start(raw_i[0:EDGE_ROWS, 2, :].bitcast(F32),
                             edge_weight.rearrange("(p j) -> p j", j=TILES)).then_inc(edges_in, 16)
                sp.wait_ge(interleaved, 1)
                sp.dma_start(recs.rearrange("(p j) c -> p j c", j=TILES), rec_all[:]).then_inc(recs_out, 16)
                for q in range(2):
                    sp.dma_start(sorted_recs[q][0:1, :], fence[0:1, :]).then_inc(recs_out, 16)
                    sp.dma_start(sorted_recs[q][SLOTS + 1:SLOTS + 2, :], fence[1:2, :]).then_inc(recs_out, 16)
                sp.wait_ge(bias_split, 3)
                for n in range(3):
                    sp.dma_start(bias3[n:n + 1, :], bias_part[0:1, n, :]).then_inc(recs_out, 16)
                sp.wait_ge(recs_out, 128)

            @block.gpsimd
            def _(pool):
                nc.gpsimd.memset(raw_i[:, 0:2, :], PAD_KEY)
                nc.gpsimd.memset(raw_i[:, 2, :], 0)
                nc.gpsimd.memset(ident[:], 0.0)
                nc.gpsimd.memset(before[:], 1.0)
                nc.gpsimd.memset(not_before[:], 1.0)
                nc.gpsimd.memset(fence[:], PAD_KEY + 1).then_inc(filled, 1)
                pool.wait_ge(filled, 1)
                nc.gpsimd.affine_select(out=ident[:], in_=ident[:], compare_op=ALU.not_equal, fill=1.0,
                                        base=0, pattern=[[-1, P]], channel_multiplier=1)
                nc.gpsimd.affine_select(out=before[:], in_=before[:], compare_op=ALU.is_gt, fill=0.0,
                                        base=0, pattern=[[1, P]], channel_multiplier=-1)
                nc.gpsimd.affine_select(out=not_before[:], in_=not_before[:], compare_op=ALU.is_ge, fill=0.0,
                                        base=0, pattern=[[-1, P]], channel_multiplier=1)
                nc.gpsimd.memset(center[:], -1.0 / D)
                nc.gpsimd.iota(count_i[:], pattern=[[1, HI]], base=0, channel_multiplier=0)\
                    .then_inc(selected, 1)

            @block.tensor
            def _(pe):
                pe.wait_ge(loaded, 16 * 14)
                pe.wait_ge(selected, 1)
                pe.wait_ge(set_dve, 1)
                for n, (a, _) in enumerate(raw):
                    pe.transpose(bank[n][:, 0:D], a[:], ident[:]).then_inc(w_turned, 1)
                for n in range(2):
                    pe.transpose(bank[4 + n][:, 0:D], w_pre_raw[:, n * D:(n + 1) * D], ident[:])\
                        .then_inc(w_turned, 1)
                for n, b in enumerate((b0_row, b1_row)):
                    pe.matmul(bank[6 + n][:, 0:D], ones_row[:], b[:], start=True, stop=True)\
                        .then_inc(w_turned, 1)
                pe.wait_ge(w_copied, 8)
                for n in range(13):
                    to = bank[n // 4][:, (n % 4) * D:(n % 4 + 1) * D]
                    mm = pe.matmul(to, w_post_sb[:, n * D:(n + 1) * D], w_lin_t[:], start=True, stop=True)
                pe.matmul(bank[4][0:1, 0:D], b_post_col[:], w_lin_t[:], start=True, stop=True)\
                    .then_inc(merged, 1)
                pe.wait_ge(merged_out, 1)
                for n in range(3):
                    mm = pe.matmul(bank[5][0:1, 0:D], std_cols[:, n:n + 1], w_agg[:, 3, n * D:(n + 1) * D],
                                   start=(n == 0), stop=(n == 2))
                mm.then_inc(merged, 1)
                pe.wait_ge(merged_out, 2)
                pe.matmul(bank[0][:, 0:D], center[:], w1_t[:], start=True, stop=True)
                pe.matmul(bank[1][:, 0:D], center[:], w_r_t[:], start=True, stop=True)
                pe.transpose(bank[2][:, 0:D], w_own[:], ident[:])
                pe.matmul(bank[3][:, 0:1], b2_alone[:], ones_row[:, 0:1], start=True, stop=True)
                pe.matmul(bank[6][:, 0:D], ones_row[:], b3_row[:], start=True, stop=True).then_inc(merged, 1)
                pe.wait_ge(merged_out, 3)
                pe.matmul(bank[4][:, 0:D], w_own_t[:], w_r_c[:], start=True, stop=True)
                pe.matmul(bank[5][0:1, 0:D], b0_col[:], w1_c[:], start=True, stop=True)
                pe.matmul(bank[7][0:1, 0:D], b2_alone_col[:], w_r_c[:], start=True, stop=True)\
                    .then_inc(merged, 1)

            @block.vector
            def _(dve):
                dve.memset(ones16[:], 1.0)
                dve.memset(zeros16[:], 0.0)
                dve.memset(ones_row[:], 1.0)
                dve.memset(ones3[:], 1.0)
                dve.memset(ones_step[:], 1.0)
                dve.memset(eps_col[:], EPS)
                dve.memset(one_col[:], 1.0)
                dve.memset(std_cols[:, 0:1], EPS ** 0.5)
                dve.memset(std_cols[:, 1:2], EPS ** 0.5 * LN2)
                dve.memset(std_cols[:, 2:3], EPS ** 0.5 / LN2)
                dve.memset(agg[:], 0.0)
                dve.memset(agg_max[:], 0.0)
                dve.memset(agg_min[:], 0.0)
                dve.memset(agg_sq[:], 0.0)
                dve.memset(agg_n[:], 0.0).then_inc(set_dve, 1)
                dve.wait_ge(selected, 1)
                dve.tensor_copy(count16[:], count_i[:])
                dve.wait_ge(edges_in, 48)
                for n in range(3):
                    dve.tensor_copy(rec_all[:, :, n], raw_i[:, n, :])
                dve.tensor_scalar(rec_all[:, :, 3], raw_i[:, 2, :], 0, None, ALU.bitwise_and)\
                    .then_inc(interleaved, 1)
                for n, (_, to) in enumerate(raw):
                    dve.wait_ge(w_turned, n + 1)
                    dve.tensor_copy(to[:], bank[n][:, 0:D]).then_inc(w_copied, 1)
                for n, to in enumerate((w_dst_t, w_src_t, b0_all, b1_all)):
                    dve.wait_ge(w_turned, n + 5)
                    dve.tensor_copy(to[:], bank[4 + n][:, 0:D]).then_inc(w_copied, 1)
                dve.wait_ge(merged, 1)
                dve.tensor_tensor(w_own[:], bank[0][:, 0:D], ident[:], ALU.add)
                dve.tensor_tensor(b2_row[:], bank[4][0:1, 0:D], b_lin_row[:], ALU.add)
                for n in range(1, 13):
                    a, s = (n - 1) % 4, (n - 1) // 4
                    last = dve.tensor_copy(w_agg[:, a, s * D:(s + 1) * D],
                                           bank[n // 4][:, (n % 4) * D:(n % 4 + 1) * D])
                last.then_inc(merged_out, 1)
                dve.wait_ge(merged, 2)
                dve.wait_ge(merged_out, 1)
                dve.tensor_tensor(center[:], center[:], ident[:], ALU.add)
                dve.tensor_tensor(b2_alone[:], bank[5][0:1, 0:D], b2_row[:], ALU.add).then_inc(merged_out, 1)
                dve.wait_ge(merged, 3)
                dve.tensor_copy(w1_c[:], bank[0][:, 0:D])
                dve.tensor_copy(w_r_c[:], bank[1][:, 0:D])
                dve.tensor_copy(w_own_t[:], bank[2][:, 0:D])
                dve.tensor_copy(b2_alone_col[:], bank[3][:, 0:1])
                dve.tensor_copy(b3_all[:], bank[6][:, 0:D]).then_inc(merged_out, 1)
                dve.wait_ge(merged, 4)
                dve.wait_ge(merged_out, 2)
                dve.tensor_copy(w_two[:, 0:D], w_own[:])
                dve.tensor_copy(w_two[:, D:2 * D], bank[4][:, 0:D])
                dve.tensor_copy(bias[:, BIAS_ONE:BIAS_ONE + D], bank[5][0:1, 0:D])
                dve.tensor_copy(bias[:, BIAS_TWO:BIAS_TWO + D], b2_alone[:])
                dve.tensor_copy(bias[:, BIAS_TWO + D:BIAS_TWO + 2 * D], bank[7][0:1, 0:D])
                dve.tensor_copy(bias[:, BIAS_B0:BIAS_B0 + D], b0_row[:])
                dve.tensor_copy(bias[:, BIAS_B2:BIAS_B2 + D], b2_row[:])
                dve.tensor_copy(bias[:, BIAS_B3:BIAS_B3 + D], b3_row[:]).then_inc(bias_made, 1)
                dve.wait_ge(bias_made, 1)
                rest = bias[:]
                for n in range(3):
                    dve.tensor_copy(bias_part[:, n, :], rest).then_inc(bias_split, 1)
                    dve.wait_ge(bias_split, n + 1)
                    if n < 2:
                        dve.tensor_tensor(bias_rest[:, n, :], rest, bias_part[:, n, :], ALU.subtract)\
                            .then_inc(bias_made, 1)
                        dve.wait_ge(bias_made, n + 2)
                        rest = bias_rest[:, n, :]

        phase(set_up)

        SRC_LO, DST_LO, SRC_HI, DST_HI = 0, LO, 2 * LO, 2 * LO + HI
        FIELDS = ((0, SRC_LO, LO, 0), (1, DST_LO, LO, 0), (0, SRC_HI, HI, LO_BITS), (1, DST_HI, HI, LO_BITS))

        def digit_of(dve, to, field, par, shift):
            return dve.tensor_scalar(to, rec[:, par, :, field], shift, (LO - 1) if shift == 0 else 0xFFFF,
                                     ALU.logical_shift_right, ALU.bitwise_and)

        def census(block, sem):
            loaded = [sem(f"loaded{i}") for i in range(2)]
            digits_int = sem("digits_int")
            digits_ready = sem("digits_ready")
            onehots = sem("onehots")
            counted = sem("counted")
            copied = sem("copied")
            summed_up = sem("summed_up")
            places = sem("places")
            std_made = sem("std_made")
            inverted = sem("inverted")
            table_out = sem("table_out")

            @block.sync
            def _(sp):
                def load(h, par):
                    wait(sp, digits_int, 2 * h + par - 1)
                    sp.dma_start(rec[:, par], recs[bass.ds((2 * h + par) * G * P, G * P), :]
                                 .rearrange("(t p) c -> p t c", p=P)).then_inc(loaded[par], 16)
                pairs(sp, NG, load)
                sp.wait_ge(inverted, 1)
                sp.dma_start(dinv_table.rearrange("(c p l) a -> p c (l a)", c=HI_PARTS, l=LO),
                             degree[0:HI_ROWS, :].rearrange("p (c l) -> p c l", c=HI_PARTS))\
                    .then_inc(table_out, 16)
                sp.wait_ge(table_out, 16)

            @block.vector
            def _(dve):
                def step(h, par):
                    j = 2 * h + par
                    wait(dve, loaded[par], 16 * (h + 1))
                    wait(dve, onehots, G * j)
                    for n, (field, _, _, shift) in enumerate(FIELDS):
                        last = digit_of(dve, digit_i[:, n, :], field, par, shift)
                    last.then_inc(digits_int, 1)
                    wait(dve, digits_int, j + 1)
                    dve.tensor_copy(digit[:], digit_i[:]).then_inc(digits_ready, 1)
                    wait(dve, digits_ready, j + 1)
                    for t in range(G):
                        tile = G * j + t
                        side = (G * par + t) % 2
                        wait(dve, counted, tile - 1)
                        for n, (_, at, width, _) in enumerate(FIELDS):
                            last = dve.tensor_scalar(onehot[:, side, at:at + width], count16[:, 0:width],
                                                     digit[:, n, t:t + 1], None, ALU.is_equal)
                        last.then_inc(onehots, 1)
                pairs(dve, NG, step)
                dve.wait_ge(counted, TILES)
                dve.tensor_copy(totals[:, 0:2 * LO], bank[0][:])
                dve.tensor_copy(totals[:, SRC_HI:SRC_HI + HI], bank[1][:, 0:HI])
                dve.tensor_copy(totals[:, DST_HI:DST_HI + HI], bank[2][:, 0:HI]).then_inc(copied, 1)
                dve.wait_ge(copied, 1)
                for n, (_, at, width, _) in enumerate(FIELDS):
                    last = dve.tensor_tensor_scan(inclusive[:, at:at + width], ones_step[:, 0:width],
                                                  totals[:, at:at + width], 0.0, ALU.mult, ALU.add)
                last.then_inc(summed_up, 1)
                dve.wait_ge(summed_up, 1)
                dve.tensor_tensor(first_place[:], inclusive[:], totals[:], ALU.subtract).then_inc(places, 1)
                dve.wait_ge(places, 1)
                dve.tensor_scalar(first_place[:, SRC_HI:], first_place[:, SRC_HI:], 1.0, None, ALU.add)
                dve.wait_ge(std_made, 1)
                dve.reciprocal(degree[0:HI_ROWS, :], degree[0:HI_ROWS, :]).then_inc(inverted, 1)

            @block.scalar
            def _(act):
                act.wait_ge(counted, TILES)
                for n in range(2):
                    last = act.activation(degree[0:HI_ROWS, n * 512:(n + 1) * 512], bank[3 + n][0:HI_ROWS, :],
                                          ACT.Sqrt, bias=one_col[0:HI_ROWS, :])
                last.then_inc(std_made, 1)

            @block.tensor
            def _(pe):
                for n in range(5):
                    pe.matmul(bank[n][:], zeros16[:, 0:P], zeros16[:], start=True, stop=True)

                def step(h, par):
                    j = 2 * h + par
                    for t in range(G):
                        side = (G * par + t) % 2
                        wait(pe, onehots, G * j + t + 1)
                        pe.matmul(bank[0][:], ones16[:], onehot[:, side, 0:2 * LO], start=False, stop=True,
                                  skip_group_check=True)
                        pe.matmul(bank[1][:, 0:HI], ones16[:], onehot[:, side, SRC_HI:SRC_HI + HI],
                                  start=False, stop=True, skip_group_check=True)
                        pe.matmul(bank[2][:, 0:HI], ones16[:], onehot[:, side, DST_HI:DST_HI + HI],
                                  start=False, stop=True, skip_group_check=True)
                        for c in range(HI_PARTS):
                            at = DST_HI + c * HI_ROWS
                            mm = pe.matmul(bank[3 + c // 2][0:HI_ROWS, (c % 2) * LO:(c % 2 + 1) * LO],
                                           onehot[:, side, at:at + HI_ROWS], onehot[:, side, DST_LO:DST_LO + LO],
                                           start=False, stop=True, skip_group_check=True)
                        mm.then_inc(counted, 1)
                pairs(pe, NG, step)

        phase(census)

        def sort_pass(block, sem, table, to, field, at, width, shift):
            loaded = [sem(f"loaded{i}") for i in range(2)]
            digits_int = sem("digits_int")
            digits_ready = sem("digits_ready")
            onehots = sem("onehots")
            prefixed = sem("prefixed")
            ranked = sem("ranked")
            positions = sem("positions")
            placed = [sem(f"placed{i}") for i in range(2)]
            gated = sem("gated")

            @block.sync
            def _(sp):
                def load(h, par):
                    wait(sp, placed[par], 16 * G * h)
                    sp.dma_start(rec[:, par], table[bass.ds((2 * h + par) * G * P, G * P), :]
                                 .rearrange("(t p) c -> p t c", p=P)).then_inc(loaded[par], 16)
                pairs(sp, NG, load)

            @block.vector
            def _(dve):
                def step(h, par):
                    j = 2 * h + par
                    wait(dve, loaded[par], 16 * (h + 1))
                    wait(dve, onehots, G * j)
                    digit_of(dve, digit_i[:, 0, :], field, par, shift).then_inc(digits_int, 1)
                    wait(dve, digits_int, j + 1)
                    dve.tensor_copy(digit[:, 0, :], digit_i[:, 0, :]).then_inc(digits_ready, 1)
                    wait(dve, digits_ready, j + 1)

                    def make_onehot(t):
                        wait(dve, ranked, G * j + t - 1)
                        wait(dve, prefixed, 2 * (G * j + t - 1))
                        dve.tensor_scalar(onehot[:, (G * par + t) % 2, 0:width], count16[:, 0:width],
                                          digit[:, 0, t:t + 1], None, ALU.is_equal).then_inc(onehots, 1)
                    make_onehot(0)
                    for t in range(G):
                        if t + 1 < G:
                            make_onehot(t + 1)
                        wait(dve, onehots, G * j + t + 1)
                        wait(dve, ranked, G * j + t)
                        if t == 0:
                            wait(dve, positions, j)
                        wait(dve, prefixed, 2 * (G * j + t) + 1)
                        dve.tensor_tensor_reduce(
                            out=rank_terms[:, 0:width], in0=onehot[:, (G * par + t) % 2, 0:width],
                            in1=bank[0][:, 0:width], scale=1.0, scalar=0.0, op0=ALU.mult, op1=ALU.add,
                            accum_out=position[:, t:t + 1]).then_inc(ranked, 1)
                    wait(dve, ranked, G * (j + 1))
                    wait(dve, placed[par], 16 * G * h)
                    dve.tensor_copy(position_i[:, par], position[:]).then_inc(positions, 1)
                pairs(dve, NG, step)

            @block.tensor
            def _(pe):
                pe.matmul(bank[0][:, 0:width], ident[:], first_place[:, at:at + width], start=True, stop=True)

                def step(h, par):
                    j = 2 * h + par
                    for t in range(G):
                        one = onehot[:, (G * par + t) % 2, 0:width]
                        wait(pe, onehots, G * j + t + 1)
                        pe.matmul(bank[0][:, 0:width], before[:], one, start=False, stop=True,
                                  skip_group_check=True).then_inc(prefixed, 1)
                        wait(pe, ranked, G * j + t + 1)
                        pe.matmul(bank[0][:, 0:width], not_before[:], one, start=False, stop=True,
                                  skip_group_check=True).then_inc(prefixed, 1)
                pairs(pe, NG, step)

            @block.gpsimd
            def _(pool):
                bound = nc.gpsimd.to_reg(SLOTS + 1)

                def step(h, par):
                    wait(pool, positions, 2 * h + par + 1)
                    pool.sem_inc(gated, 1)
                    for t in range(G):
                        scatter(to, position_i[:, par, t:t + 1], rec[:, par, t, :], placed[par], bound)
                pairs(pool, NG, step)
                for par in range(2):
                    pool.wait_ge(placed[par], NG // 2 * 16 * G)
                    pool.sem_inc(gated, 1)

        def make_list(block, sem, q):
            loaded = sem("loaded")
            as_float = sem("as_float")
            flags = sem("flags")
            hidden = sem("hidden")
            ready = sem("ready")
            turned = sem("turned")
            copied = sem("copied")
            key, other = q, 1 - q

            @block.sync
            def _(sp):
                for half in range(2):
                    wait(sp, as_float, half)
                    wait(sp, flags, half)
                    for s in range(3):
                        first = half * HALF * P + s
                        sp.dma_start(prep[:, s], sorted_recs[q][first:first + HALF * P, :]
                                     .rearrange("(t p) c -> t p c", p=P)).then_inc(loaded, 16)

            @block.vector
            def _(dve):
                for half in range(2):
                    dve.wait_ge(loaded, 48 * (half + 1))
                    wait(dve, turned, half)
                    dve.tensor_copy(prep_f[:, 0], prep[:, 1, :, key])
                    dve.tensor_copy(prep_f[:, 1], prep[:, 1, :, other])
                    dve.tensor_copy(prep_f[:, 2].bitcast(I32), prep[:, 1, :, 2])
                    dve.tensor_tensor(prep_f[:, 3], prep[:, 1, :, key], prep[:, 0, :, key], ALU.is_equal)
                    dve.tensor_tensor(prep_f[:, 4], prep[:, 1, :, key], prep[:, 2, :, key], ALU.is_equal)\
                        .then_inc(as_float, 1)
                    dve.wait_ge(as_float, half + 1)
                    dve.tensor_scalar(prep_f[:, 5], prep_f[:, 4], float(FAR), None, ALU.mult)\
                        .then_inc(hidden, 1)
                    dve.wait_ge(hidden, half + 1)
                    dve.tensor_tensor(prep_f[:, 5], prep_f[:, 5], prep_f[:, 0], ALU.add).then_inc(flags, 1)
                    cols = slice(half * HALF, (half + 1) * HALF)
                    dve.wait_ge(turned, half + 1)
                    dve.tensor_copy(list_key[q][:, cols], bank[0][:, 0:HALF])
                    dve.tensor_copy(list_other[q][:, cols], bank[1][:, 0:HALF])
                    if q == 0:
                        dve.tensor_copy(list_w[:, cols], bank[2][:, 0:HALF])
                    dve.tensor_copy(list_keep[q][:, cols], bank[3][:, 0:HALF])
                    dve.tensor_copy(list_write[q][:, cols], bank[4][:, 0:HALF]).then_inc(copied, 1)

            @block.tensor
            def _(pe):
                for half in range(2):
                    pe.wait_ge(flags, half + 1)
                    wait(pe, copied, half)
                    for n, part in enumerate((0, 1, 2, 3, 5)):
                        mm = pe.transpose(bank[n][:, 0:HALF], prep_f[:, part], ident[0:HALF, 0:HALF])
                    mm.then_inc(turned, 1)

        for q, (lo_at, hi_at) in enumerate(((SRC_LO, SRC_HI), (DST_LO, DST_HI))):
            phase(sort_pass, recs, recs_lo[q], q, lo_at, LO, 0)
            phase(sort_pass, recs_lo[q], sorted_recs[q], q, hi_at, HI, LO_BITS)
            phase(make_list, q)

        sort_memory.close()
        turned_x = sb("turned_x", [P, 2, STEP])
        own_x = sb("own_x", [P, 4, STEP])
        mean = sb("mean", [P, 2, STEP])
        dev = sb("dev", [P, 2, STEP])
        scales = sb("scales", [P, 2, 3, T])
        base_x = sb("base_x", [P, 4, T, D])
        rows_x = sb("rows_x", [P, 4, T, D])
        dinv_x = sb("dinv_x", [P, 4, T])
        out_x = sb("out_x", [P, 4, T, D])
        out_y = sb("out_y", [P, 4, T, D])
        out_z = sb("out_z", [P, 4, T, D])
        pre_x = sb("pre_x", [P, 2, T, D])
        plain_x = sb("plain_x", [P, 2, T, D])
        stats_x = sb("stats_x", [P, 2, T, 6])
        moments_x = sb("moments_x", [P, 2, 2, T, 2])
        std_x = sb("std_x", [P, 2, 2, T])
        rstd_x = sb("rstd_x", [P, 2, 2, T])
        shift_x = sb("shift_x", [P, 2, 2, T])
        factor_x = sb("factor_x", [P, 4, 6, T])
        factor_y = sb("factor_y", [P, 2, T])

        class Norm:
            def __init__(self, sem, name):
                self.stats = sem(f"{name}_stats")
                self.moments = sem(f"{name}_moments")
                self.std = sem(f"{name}_std")
                self.rstd = sem(f"{name}_rstd")
                self.done = sem(f"{name}_done")

        def norm_moments(dve, ln, j, rows):
            for t in range(T):
                last = dve.bn_stats(stats[:, t, :], rows[:, t, :])
            last.then_inc(ln.stats, 1)
            wait(dve, ln.stats, j + 1)
            dve.sem_inc(dve_gate, 1)
            for t in range(T):
                last = dve.bn_aggr(moments[:, t, :], stats[:, t, :])
            last.then_inc(ln.moments, 1)

        def norm_std(act, ln, j):
            wait(act, ln.moments, j + 1)
            act.activation(std[:], moments[:, :, 1], ACT.Sqrt, bias=eps_col[:]).then_inc(ln.std, 1)

        def norm_rows(dve, ln, j, rows, to):
            wait(dve, ln.std, j + 1)
            dve.reciprocal(rstd[:], std[:]).then_inc(ln.rstd, 1)
            wait(dve, ln.rstd, j + 1)
            for t in range(T):
                last = dve.tensor_scalar(to[:, t, :], rows[:, t, :], moments[:, t, 0:1], rstd[:, t:t + 1],
                                         ALU.subtract, ALU.mult)
            last.then_inc(ln.done, 1)

        def sweep_one(block, sem):
            loaded = [sem(f"loaded{i}") for i in range(4)]
            stored_uv = [sem(f"stored_uv{i}") for i in range(4)]
            stored_y1 = [sem(f"stored_y1{i}") for i in range(4)]
            turned = sem("turned")
            copied = sem("copied")
            projected = sem("projected")
            with_b0 = sem("with_b0")
            stats0 = sem("stats0")
            moments0 = sem("moments0")
            std0 = sem("std0")
            rstd0 = sem("rstd0")
            squares = sem("squares")
            powers = sem("powers")
            factors = sem("factors")
            uv_made = sem("uv_made")
            base_made = sem("base_made")
            summed = sem("summed")
            stats1 = sem("stats1")
            moments1 = sem("moments1")
            std1 = sem("std1")
            rstd1 = sem("rstd1")
            shift1 = sem("shift1")
            shift2 = sem("shift2")
            y1_made = sem("y1_made")
            @block.sync
            def _(sp):
                def load(h, side):
                    j, par = 4 * h + side, side % 2
                    wait(sp, with_b0, j - 3)
                    wait(sp, turned, j - 3)
                    wait(sp, factors, j - 3)
                    sp.dma_start(rows_x[:, side], by_node(x, j)).then_inc(loaded[side], 16)
                    sp.dma_start(dinv_x[:, side].rearrange("p (t a) -> p t a", a=1),
                                 by_node(dinv_table[0:N, :], j)).then_inc(loaded[side], 16)

                def store_uv(h, side):
                    j, par = 4 * h + side, side % 2
                    wait(sp, uv_made, j + 1)
                    if isinstance(j, int) and j == SWEEP - 1:
                        wait(sp, stored_uv[side - 1], 32 * (h + 1))
                    sp.dma_start(by_node(u_table, j), out_x[:, side]).then_inc(stored_uv[side], 16)
                    sp.dma_start(by_node(v_table, j), out_y[:, side]).then_inc(stored_uv[side], 16)

                def store_y1(h, side):
                    j, par = 4 * h + side, side % 2
                    wait(sp, y1_made, j + 1)
                    if isinstance(j, int) and j == SWEEP - 1:
                        wait(sp, stored_y1[side - 1], 16 * (h + 1))
                    sp.dma_start(by_node(y1_table, j), out_z[:, side]).then_inc(stored_y1[side], 16)
                staggered(sp, SWEEP, [(0, load), (3, store_uv), (6, store_y1)], apart=1, unroll=4)
                for side in range(4):
                    sp.wait_ge(stored_uv[side], 32 * (SWEEP // 4))
                    sp.wait_ge(stored_y1[side], 16 * (SWEEP // 4))

            @block.tensor
            def _(pe):
                def turn(h, side):
                    j, par = 4 * h + side, side % 2
                    wait(pe, loaded[side], 32 * (h + 1))
                    wait(pe, copied, j - 1)
                    for t in range(T):
                        mm = pe.transpose(bank[par][:, t * P:(t + 1) * P], rows_x[:, side, t], ident[:])
                    mm.then_inc(turned, 1)

                def project(h, side):
                    j, par = 4 * h + side, side % 2
                    wait(pe, copied, j + 1)
                    wait(pe, summed, j - 1)
                    for t in range(T):
                        to = bank[2 + par][:, t * D:(t + 1) * D]
                        pe.matmul(to, turned_x[:, par, t * P:(t + 1) * P], w1_c[:], start=True, stop=False)
                        mm = add_bias(pe, to, BIAS_ONE)
                    mm.then_inc(projected, 1)
                staggered(pe, SWEEP, [(0, turn), (2, project)], apart=1, unroll=4)

            @block.vector
            def _(dve):
                def norm0(h, side):
                    j, par = 4 * h + side, side % 2
                    wait(dve, loaded[side], 32 * (h + 1))
                    wait(dve, uv_made, j - 1)
                    wait(dve, base_made, j - 1)
                    dve.tensor_tensor(rows_a[:, par], rows_x[:, side], over_tiles(b0_all[:]), ALU.add)\
                        .then_inc(with_b0, 1)
                    dve.tensor_tensor(factor_x[:, side, 0], dinv_x[:, side], dinv_x[:, side], ALU.mult)\
                        .then_inc(squares, 1)
                    wait(dve, with_b0, j + 1)
                    wait(dve, moments0, j)
                    for t in range(T):
                        last = dve.bn_stats(stats_x[:, 0, t, :], rows_a[:, par, t])
                    last.then_inc(stats0, 1)
                    wait(dve, squares, j + 1)
                    dve.tensor_tensor(factor_x[:, side, 1], factor_x[:, side, 0], dinv_x[:, side], ALU.mult)
                    dve.tensor_tensor(factor_x[:, side, 2], factor_x[:, side, 0], factor_x[:, side, 0], ALU.mult)\
                        .then_inc(powers, 1)
                    wait(dve, stats0, j + 1)
                    dve.sem_inc(dve_gate, 1)
                    for t in range(T):
                        last = dve.bn_aggr(moments_x[:, 0, par, t, :], stats_x[:, 0, t, :])
                    last.then_inc(moments0, 1)

                def scale0(h, side):
                    j, par = 4 * h + side, side % 2
                    wait(dve, std0, j + 1)
                    dve.reciprocal(rstd_x[:, 0, par], std_x[:, 0, par]).then_inc(rstd0, 1)
                    wait(dve, rstd0, j + 1)
                    wait(dve, powers, j + 1)
                    wait(dve, summed, j - 3)
                    dve.tensor_tensor(factor_x[:, side, 3], rstd_x[:, 0, par], dinv_x[:, side], ALU.mult)
                    dve.tensor_tensor(factor_x[:, side, 4], rstd_x[:, 0, par], factor_x[:, side, 1], ALU.mult)
                    dve.tensor_tensor(factor_x[:, side, 5], rstd_x[:, 0, par], factor_x[:, side, 2], ALU.mult)\
                        .then_inc(factors, 1)
                    wait(dve, factors, j + 1)
                    for n in range(2):
                        last = dve.scalar_tensor_tensor(out=shift_x[:, n, par], in0=moments_x[:, 0, par, :, 0],
                                                        scalar=-1.0, in1=factor_x[:, side, 3 + n],
                                                        op0=ALU.mult, op1=ALU.mult)
                    last.then_inc(shift1, 1)
                    for t in range(T):
                        last = dve.scalar_tensor_tensor(out=base_x[:, side, t], in0=rows_a[:, par, t],
                                                        scalar=rstd_x[:, 0, par, t:t + 1], in1=b1_all[:],
                                                        op0=ALU.mult, op1=ALU.add)
                    last.then_inc(base_made, 1)

                def sum_up(h, side):
                    j, par = 4 * h + side, side % 2
                    wait(dve, projected, j + 1)
                    wait(dve, base_made, j + 1)
                    wait(dve, y1_made, j - 1)
                    for t in range(T):
                        last = dve.scalar_tensor_tensor(out=pre_x[:, par, t],
                                                        in0=bank4(2 + par)[:, t],
                                                        scalar=factor_x[:, side, 5, t:t + 1],
                                                        in1=base_x[:, side, t], op0=ALU.mult, op1=ALU.add)
                    last.then_inc(summed, 1)
                    wait(dve, summed, j + 1)
                    wait(dve, moments1, j)
                    for t in range(T):
                        last = dve.bn_stats(stats_x[:, 1, t, :], pre_x[:, par, t])
                    last.then_inc(stats1, 1)
                    wait(dve, stats1, j + 1)
                    dve.sem_inc(dve_gate, 1)
                    for t in range(T):
                        last = dve.bn_aggr(moments_x[:, 1, par, t, :], stats_x[:, 1, t, :])
                    last.then_inc(moments1, 1)

                def scale1(h, side):
                    j, par = 4 * h + side, side % 2
                    wait(dve, std1, j + 1)
                    wait(dve, y1_made, j - 1)
                    dve.reciprocal(rstd_x[:, 1, par], std_x[:, 1, par]).then_inc(rstd1, 1)
                    wait(dve, rstd1, j + 1)
                    dve.scalar_tensor_tensor(out=factor_y[:, par], in0=moments_x[:, 1, par, :, 0],
                                             scalar=-1.0, in1=rstd_x[:, 1, par],
                                             op0=ALU.mult, op1=ALU.mult).then_inc(shift2, 1)
                staggered(dve, SWEEP, [(0, norm0), (3, sum_up), (0, scale0), (3, scale1)], apart=1, unroll=4)

            @block.scalar
            def _(act):
                def copy(h, side):
                    j, par = 4 * h + side, side % 2
                    wait(act, turned, j + 1)
                    wait(act, projected, j - 1)
                    act.copy(turned_x[:, par], bank[par][:]).then_inc(copied, 1)

                def root0(h, side):
                    j, par = 4 * h + side, side % 2
                    wait(act, moments0, j + 1)
                    act.activation(std_x[:, 0, par], moments_x[:, 0, par, :, 1], ACT.Sqrt, bias=eps_col[:])\
                        .then_inc(std0, 1)

                def make_uv(h, side):
                    j, par = 4 * h + side, side % 2
                    wait(act, shift1, j + 1)
                    wait(act, stored_uv[side], 32 * h)
                    for t in range(T):
                        act.activation(out_x[:, side, t], rows_a[:, par, t], ACT.Identity,
                                       scale=factor_x[:, side, 3, t:t + 1], bias=shift_x[:, 0, par, t:t + 1])
                        last = act.activation(out_y[:, side, t], rows_a[:, par, t], ACT.Identity,
                                              scale=factor_x[:, side, 4, t:t + 1], bias=shift_x[:, 1, par, t:t + 1])
                    last.then_inc(uv_made, 1)

                def root1(h, side):
                    j, par = 4 * h + side, side % 2
                    wait(act, moments1, j + 1)
                    act.activation(std_x[:, 1, par], moments_x[:, 1, par, :, 1], ACT.Sqrt, bias=eps_col[:])\
                        .then_inc(std1, 1)

                def make_y1(h, side):
                    j, par = 4 * h + side, side % 2
                    wait(act, shift2, j + 1)
                    wait(act, stored_y1[side], 16 * h)
                    for t in range(T):
                        last = act.activation(out_z[:, side, t], pre_x[:, par, t], ACT.Identity,
                                              scale=rstd_x[:, 1, par, t:t + 1], bias=factor_y[:, par, t:t + 1])
                    last.then_inc(y1_made, 1)
                staggered(act, SWEEP, [(1, make_uv), (0, root0), (1, copy), (4, make_y1), (3, root1)], apart=1, unroll=4)

        phase(sweep_one)

        def steps_of(side):
            return (NSTEP - side + 3) // 4

        def pool_steps(pool, sem, sources, target, gathers, scatters, gathered, scattered, per_step):
            idx_ready = sem("idx_ready")
            idx_w_ready = sem("idx_w_ready")

            def fetch(h, side):
                wait(pool, gathered[side], per_step * h)
                pool.sem_inc(pool_gate, 1)
                for to, lists in sources:
                    last = nc.gpsimd.tensor_copy(to[:, side], lists[:, bass.ds((4 * h + side) * T, T)])
                last.then_inc(idx_ready, 1)

            def fetch_target(h, side):
                wait(pool, scattered[side], 64 * h)
                pool.sem_inc(pool_gate, 1)
                nc.gpsimd.tensor_copy(idx_w[:, side], target[:, bass.ds((4 * h + side) * T, T)])\
                    .then_inc(idx_w_ready, 1)

            def gather_step(h, side):
                wait(pool, idx_ready, 4 * h + side + 1)
                gathers(h, side)

            def scatter_step(h, side):
                wait(pool, idx_w_ready, 4 * h + side + 1)
                scatters(h, side)
            staggered(pool, NSTEP, [(0, fetch), (3, fetch_target), (1, gather_step), (4, scatter_step)], unroll=4)
            for side in range(4):
                pool.wait_ge(scattered[side], 64 * steps_of(side))
                pool.sem_inc(pool_gate, 1)

        def keep_to_row_pe(pe, j, keep_in, keep_turned, keep_copied):
            wait(pe, keep_in, j + 1)
            wait(pe, keep_copied, j)
            for t in range(T):
                mm = pe.transpose(bank[0][:, t * P:(t + 1) * P], keep_cols[:, t:t + 1].broadcast_to([P, P]), ident[:])
            mm.then_inc(keep_turned, 1)

        def keep_to_cols_dve(dve, j, q, keep_in, keep_turned):
            wait(dve, keep_turned, j)
            dve.sem_inc(dve_gate, 1)
            dve.tensor_copy(keep_cols[:], list_keep[q][:, bass.ds(j * T, T)]).then_inc(keep_in, 1)

        def layer_0(block, sem):
            gathered = [sem(f"gathered{i}") for i in range(4)]
            scattered = [sem(f"scattered{i}") for i in range(4)]
            stored = [sem(f"stored{i}") for i in range(4)]
            keep_in = sem("keep_in")
            keep_turned = sem("keep_turned")
            keep_copied = sem("keep_copied")
            weighted = sem("weighted")
            turned = sem("turned")
            scanned = sem("scanned")
            projected = sem("projected")
            summed = sem("summed")
            dinv_kept = sem("dinv_kept")
            scaled = sem("scaled")
            ln = Norm(sem, "y0")

            @block.gpsimd
            def _(pool):
                bound = nc.gpsimd.to_reg(N - 1)

                def gathers(h, side):
                    j, par = 4 * h + side, side % 2
                    wait(pool, turned, j - 3)
                    wait(pool, summed, j - 3)
                    wait(pool, dinv_kept, j - 3)
                    wait(pool, scaled, j - 3)
                    pool.sem_inc(pool_gate, 1)
                    for t in range(T):
                        gather(rows_x[:, side, t], x, idx_a[:, side, t:t + 1], gathered[side], bound)
                    for t in range(T):
                        gather(base_x[:, side, t], x, idx_b[:, side, t:t + 1], gathered[side], bound)
                    for t in range(T):
                        gather(dinv_x[:, side, t:t + 1], dinv_table, idx_b[:, side, t:t + 1], gathered[side], bound)

                def scatters(h, side):
                    wait(pool, scaled, 4 * h + side + 1)
                    pool.sem_inc(pool_gate, 1)
                    for t in range(T):
                        scatter(u_table, idx_w[:, side, t:t + 1], out_y[:, side, t], scattered[side], bound)
                pool_steps(pool, sem, ((idx_a, list_other[0]), (idx_b, list_key[0])), list_write[0],
                           gathers, scatters, gathered, scattered, 192)

            @block.sync
            def _(sp):
                def store(h, side):
                    j, par = 4 * h + side, side % 2
                    wait(sp, scaled, j + 1)
                    sp.dma_start(by_slot(y0_slots, j), out_x[:, side]).then_inc(stored[side], 16)
                    sp.dma_start(by_slot(u_slots, j), out_y[:, side]).then_inc(stored[side], 16)
                staggered(sp, NSTEP, [(0, store)], unroll=4)
                for side in range(4):
                    sp.wait_ge(stored[side], 32 * steps_of(side))

            @block.vector
            def _(dve):
                def scan(h, side):
                    j, par = 4 * h + side, side % 2
                    keep_to_cols_dve(dve, j, 0, keep_in, keep_turned)
                    wait(dve, gathered[side], 192 * (h + 1))
                    dve.sem_inc(dve_gate, 1)
                    for t in range(T):
                        last = dve.tensor_scalar(rows_x[:, side, t], rows_x[:, side, t],
                                                 list_w[:, bass.ds(j * T + t, 1)], None, ALU.mult)
                    last.then_inc(weighted, 1)
                    dve.tensor_copy(dinv_own[:, bass.ds(j * T, T)], dinv_x[:, side]).then_inc(dinv_kept, 1)
                    wait(dve, turned, j + 1)
                    wait(dve, keep_copied, j + 1)
                    wait(dve, scanned, j)
                    wait(dve, projected, j - 1)
                    dve.tensor_tensor_scan(agg[:, par], keep_row[:, par], bank[1][:],
                                           agg[:, 1 - par, STEP - 1:STEP], ALU.mult, ALU.add).then_inc(scanned, 1)

                def finish(h, side):
                    j, par = 4 * h + side, side % 2
                    wait(dve, projected, j + 1)
                    wait(dve, ln.done, j)
                    dve.tensor_tensor(pre[:], bank4(2), base_x[:, side], ALU.add).then_inc(summed, 1)
                    wait(dve, summed, j + 1)
                    norm_moments(dve, ln, j, pre)
                    wait(dve, stored[side], 32 * h)
                    norm_rows(dve, ln, j, pre, out_x[:, side])
                staggered(dve, NSTEP, [(0, scan), (1, finish)], unroll=4)

            @block.scalar
            def _(act):
                def scan(h, side):
                    j, par = 4 * h + side, side % 2
                    wait(act, keep_turned, j + 1)
                    wait(act, scanned, j - 1)
                    act.copy(keep_row[:, par], bank[0][:]).then_inc(keep_copied, 1)

                def finish(h, side):
                    j, par = 4 * h + side, side % 2
                    norm_std(act, ln, j)
                    wait(act, stored[side], 32 * h)
                    wait(act, scattered[side], 64 * h)
                    wait(act, gathered[side], 192 * (h + 1))
                    wait(act, ln.done, j + 1)
                    for t in range(T):
                        last = act.activation(out_y[:, side, t], out_x[:, side, t], ACT.Copy,
                                              scale=dinv_x[:, side, t:t + 1])
                    last.then_inc(scaled, 1)
                staggered(act, NSTEP, [(0, scan), (1, finish)], unroll=4)

            @block.tensor
            def _(pe):
                def scan(h, side):
                    j, par = 4 * h + side, side % 2
                    keep_to_row_pe(pe, j, keep_in, keep_turned, keep_copied)
                    wait(pe, weighted, j + 1)
                    wait(pe, scanned, j)
                    for t in range(T):
                        mm = pe.transpose(bank[1][:, t * P:(t + 1) * P], rows_x[:, side, t], ident[:])
                    mm.then_inc(turned, 1)
                    wait(pe, scanned, j + 1)
                    wait(pe, summed, j)
                    for t in range(T):
                        to = bank[2][:, t * D:(t + 1) * D]
                        pe.matmul(to, agg[:, par, t * P:(t + 1) * P], w0_sb[:], start=True, stop=False)
                        mm = add_bias(pe, to, BIAS_B0)
                    mm.then_inc(projected, 1)
                staggered(pe, NSTEP, [(0, scan)], unroll=4)

        phase(layer_0)

        def hop_1(block, sem):
            gathered = [sem(f"gathered{i}") for i in range(4)]
            scattered = [sem(f"scattered{i}") for i in range(4)]
            stored = [sem(f"stored{i}") for i in range(4)]
            loaded = [sem(f"loaded{i}") for i in range(4)]
            keep_in = sem("keep_in")
            keep_turned = sem("keep_turned")
            keep_copied = sem("keep_copied")
            turned = sem("turned")
            scanned = sem("scanned")
            returned = sem("returned")
            summed = sem("summed")
            inv_deg = sem("inv_deg")
            hopped = sem("hopped")

            @block.gpsimd
            def _(pool):
                bound = nc.gpsimd.to_reg(N - 1)

                def gathers(h, side):
                    wait(pool, turned, 4 * h + side - 3)
                    pool.sem_inc(pool_gate, 1)
                    for t in range(T):
                        gather(rows_x[:, side, t], u_table, idx_a[:, side, t:t + 1], gathered[side], bound)

                def scatters(h, side):
                    wait(pool, hopped, 4 * h + side + 1)
                    pool.sem_inc(pool_gate, 1)
                    for t in range(T):
                        scatter(v_table, idx_w[:, side, t:t + 1], out_x[:, side, t], scattered[side], bound)
                pool_steps(pool, sem, ((idx_a, list_other[0]),), list_write[0],
                           gathers, scatters, gathered, scattered, 64)

            @block.sync
            def _(sp):
                def load(h, side):
                    j, par = 4 * h + side, side % 2
                    wait(sp, summed, j - 3)
                    sp.dma_start(base_x[:, side], by_slot(u_slots, j)).then_inc(loaded[side], 16)

                def store(h, side):
                    j, par = 4 * h + side, side % 2
                    wait(sp, hopped, j + 1)
                    sp.dma_start(by_slot(v_slots, j), out_x[:, side]).then_inc(stored[side], 16)
                staggered(sp, NSTEP, [(0, load), (2, store)], unroll=4)
                for side in range(4):
                    sp.wait_ge(stored[side], 16 * steps_of(side))

            @block.vector
            def _(dve):
                dve.tensor_tensor(dinv2_own[:], dinv_own[:], dinv_own[:], ALU.mult).then_inc(inv_deg, 1)
                dve.wait_ge(inv_deg, 1)

                def scan(h, side):
                    j, par = 4 * h + side, side % 2
                    keep_to_cols_dve(dve, j, 0, keep_in, keep_turned)
                    wait(dve, turned, j + 1)
                    wait(dve, keep_copied, j + 1)
                    wait(dve, scanned, j)
                    wait(dve, returned, j - 1)
                    dve.tensor_tensor_scan(agg[:, par], keep_row[:, par], bank[1][:],
                                           agg[:, 1 - par, STEP - 1:STEP], ALU.mult, ALU.add).then_inc(scanned, 1)

                def finish(h, side):
                    j, par = 4 * h + side, side % 2
                    wait(dve, returned, j + 1)
                    wait(dve, loaded[side], 16 * (h + 1))
                    wait(dve, hopped, j)
                    dve.tensor_tensor(pre[:], bank4(2), base_x[:, side], ALU.add).then_inc(summed, 1)
                staggered(dve, NSTEP, [(0, scan), (1, finish)], unroll=4)

            @block.scalar
            def _(act):
                act.wait_ge(inv_deg, 1)

                def scan(h, side):
                    j, par = 4 * h + side, side % 2
                    wait(act, keep_turned, j + 1)
                    wait(act, scanned, j - 1)
                    act.copy(keep_row[:, par], bank[0][:]).then_inc(keep_copied, 1)

                def finish(h, side):
                    j, par = 4 * h + side, side % 2
                    wait(act, stored[side], 16 * h)
                    wait(act, scattered[side], 64 * h)
                    wait(act, summed, j + 1)
                    act.sem_inc(act_gate, 1)
                    for t in range(T):
                        last = act.activation(out_x[:, side, t], pre[:, t], ACT.Copy,
                                              scale=dinv2_own[:, bass.ds(j * T + t, 1)])
                    last.then_inc(hopped, 1)
                staggered(act, NSTEP, [(0, scan), (1, finish)], unroll=4)

            @block.tensor
            def _(pe):
                def scan(h, side):
                    j, par = 4 * h + side, side % 2
                    keep_to_row_pe(pe, j, keep_in, keep_turned, keep_copied)
                    wait(pe, gathered[side], 64 * (h + 1))
                    wait(pe, scanned, j)
                    for t in range(T):
                        mm = pe.transpose(bank[1][:, t * P:(t + 1) * P], rows_x[:, side, t], ident[:])
                    mm.then_inc(turned, 1)
                    wait(pe, scanned, j + 1)
                    wait(pe, summed, j)
                    for t in range(T):
                        mm = pe.transpose(bank[2][:, t * D:(t + 1) * D], agg[:, par, t * P:(t + 1) * P], ident[:])
                    mm.then_inc(returned, 1)
                staggered(pe, NSTEP, [(0, scan)], unroll=4)

        phase(hop_1)

        def hop_2(block, sem):
            gathered = [sem(f"gathered{i}") for i in range(4)]
            scattered = [sem(f"scattered{i}") for i in range(4)]
            loaded = [sem(f"loaded{i}") for i in range(4)]
            keep_in = sem("keep_in")
            keep_turned = sem("keep_turned")
            keep_copied = sem("keep_copied")
            turned = sem("turned")
            scanned = sem("scanned")
            own_turned = sem("own_turned")
            joined = sem("joined")
            projected = sem("projected")
            with_b1 = sem("with_b1")
            summed = sem("summed")
            ln = Norm(sem, "y1")

            @block.gpsimd
            def _(pool):
                bound = nc.gpsimd.to_reg(N - 1)

                def gathers(h, side):
                    wait(pool, turned, 4 * h + side - 3)
                    pool.sem_inc(pool_gate, 1)
                    for t in range(T):
                        gather(rows_x[:, side, t], v_table, idx_a[:, side, t:t + 1], gathered[side], bound)

                def scatters(h, side):
                    wait(pool, ln.done, 4 * h + side + 1)
                    pool.sem_inc(pool_gate, 1)
                    for t in range(T):
                        scatter(y1_table, idx_w[:, side, t:t + 1], out_x[:, side, t], scattered[side], bound)
                pool_steps(pool, sem, ((idx_a, list_other[0]),), list_write[0],
                           gathers, scatters, gathered, scattered, 64)

            @block.sync
            def _(sp):
                def load(h, side):
                    j, par = 4 * h + side, side % 2
                    wait(sp, own_turned, j - 3)
                    wait(sp, with_b1, j - 3)
                    sp.dma_start(base_x[:, side], by_slot(v_slots, j)).then_inc(loaded[side], 16)
                    sp.dma_start(out_z[:, side], by_slot(y0_slots, j)).then_inc(loaded[side], 16)
                staggered(sp, NSTEP, [(0, load)], unroll=4)

            @block.vector
            def _(dve):
                def scan(h, side):
                    j, par = 4 * h + side, side % 2
                    keep_to_cols_dve(dve, j, 0, keep_in, keep_turned)
                    wait(dve, loaded[side], 32 * (h + 1))
                    wait(dve, ln.done, j - 1)
                    dve.tensor_tensor(pre_x[:, par], out_z[:, side], over_tiles(b1_all[:]), ALU.add).then_inc(with_b1, 1)
                    wait(dve, turned, j + 1)
                    wait(dve, keep_copied, j + 1)
                    wait(dve, scanned, j)
                    wait(dve, joined, j)
                    dve.tensor_tensor_scan(agg[:, par], keep_row[:, par], bank[1][:],
                                           agg[:, 1 - par, STEP - 1:STEP], ALU.mult, ALU.add).then_inc(scanned, 1)
                    wait(dve, scanned, j + 1)
                    wait(dve, own_turned, j + 1)
                    wait(dve, projected, j - 1)
                    dve.tensor_tensor(turned_x[:, par], bank[3][:], agg[:, par], ALU.add).then_inc(joined, 1)

                def finish(h, side):
                    j, par = 4 * h + side, side % 2
                    wait(dve, projected, j + 1)
                    wait(dve, with_b1, j + 1)
                    dve.sem_inc(dve_gate, 1)
                    for t in range(T):
                        last = dve.scalar_tensor_tensor(out=pre_x[:, par, t], in0=bank4(2)[:, t],
                                                        scalar=dinv_own[:, bass.ds(j * T + t, 1)], in1=pre_x[:, par, t],
                                                        op0=ALU.mult, op1=ALU.add)
                    last.then_inc(summed, 1)
                    wait(dve, summed, j + 1)
                    norm_moments(dve, ln, j, pre_x[:, par])
                    wait(dve, scattered[side], 64 * h)
                    norm_rows(dve, ln, j, pre_x[:, par], out_x[:, side])
                staggered(dve, NSTEP, [(0, scan), (1, finish)], unroll=4)

            @block.scalar
            def _(act):
                def scan(h, side):
                    j, par = 4 * h + side, side % 2
                    wait(act, keep_turned, j + 1)
                    wait(act, scanned, j - 1)
                    act.copy(keep_row[:, par], bank[0][:]).then_inc(keep_copied, 1)

                def finish(h, side):
                    j, par = 4 * h + side, side % 2
                    norm_std(act, ln, j)
                staggered(act, NSTEP, [(0, scan), (1, finish)], unroll=4)

            @block.tensor
            def _(pe):
                def scan(h, side):
                    j, par = 4 * h + side, side % 2
                    keep_to_row_pe(pe, j, keep_in, keep_turned, keep_copied)
                    wait(pe, loaded[side], 32 * (h + 1))
                    wait(pe, joined, j)
                    for t in range(T):
                        mm = pe.transpose(bank[3][:, t * P:(t + 1) * P], base_x[:, side, t], ident[:])
                    mm.then_inc(own_turned, 1)
                    wait(pe, gathered[side], 64 * (h + 1))
                    wait(pe, scanned, j)
                    for t in range(T):
                        mm = pe.transpose(bank[1][:, t * P:(t + 1) * P], rows_x[:, side, t], ident[:])
                    mm.then_inc(turned, 1)
                    wait(pe, joined, j + 1)
                    wait(pe, summed, j)
                    for t in range(T):
                        mm = pe.matmul(bank[2][:, t * D:(t + 1) * D], turned_x[:, par, t * P:(t + 1) * P], w1_t[:],
                                       start=True, stop=True)
                    mm.then_inc(projected, 1)
                staggered(pe, NSTEP, [(0, scan)], unroll=4)

        phase(hop_2)

        def sweep_two(block, sem):
            loaded = [sem(f"loaded{i}") for i in range(4)]
            stored_y2 = [sem(f"stored_y2{i}") for i in range(4)]
            stored_y3 = [sem(f"stored_y3{i}") for i in range(4)]
            turned = sem("turned")
            copied = sem("copied")
            projected = sem("projected")
            stats2 = sem("stats2")
            moments2 = sem("moments2")
            std2 = sem("std2")
            rstd2 = sem("rstd2")
            shift2 = sem("shift2")
            y2_made = sem("y2_made")
            scaled = sem("scaled")
            summed = sem("summed")
            stats3 = sem("stats3")
            moments3 = sem("moments3")
            std3 = sem("std3")
            rstd3 = sem("rstd3")
            shift3 = sem("shift3")
            y3_made = sem("y3_made")

            def before_norm(side, t):
                return bank4(4 + side)[:, t]

            def through_r(par, t):
                return bank4(2 + par)[:, t]

            @block.sync
            def _(sp):
                def load(h, side):
                    j, par = 4 * h + side, side % 2
                    wait(sp, turned, j - 3)
                    sp.dma_start(rows_x[:, side], by_node(y1_table, j)).then_inc(loaded[side], 16)

                def store_y2(h, side):
                    j, par = 4 * h + side, side % 2
                    wait(sp, y2_made, j + 1)
                    if isinstance(j, int) and j == SWEEP - 1:
                        wait(sp, stored_y2[side - 1], 16 * (h + 1))
                    sp.dma_start(by_node(y2_table, j), out_x[:, side]).then_inc(stored_y2[side], 16)

                def store_y3(h, side):
                    j, par = 4 * h + side, side % 2
                    wait(sp, y3_made, j + 1)
                    if isinstance(j, int) and j == SWEEP - 1:
                        wait(sp, stored_y3[side - 1], 16 * (h + 1))
                    sp.dma_start(by_node(out, j), out_y[:, side]).then_inc(stored_y3[side], 16)
                staggered(sp, SWEEP, [(0, load), (5, store_y2), (8, store_y3)], apart=1, unroll=4)
                for side in range(4):
                    sp.wait_ge(stored_y2[side], 16 * (SWEEP // 4))
                    sp.wait_ge(stored_y3[side], 16 * (SWEEP // 4))

            @block.tensor
            def _(pe):
                def turn(h, side):
                    j, par = 4 * h + side, side % 2
                    wait(pe, loaded[side], 16 * (h + 1))
                    wait(pe, copied, j - 1)
                    for t in range(T):
                        mm = pe.transpose(bank[par][:, t * P:(t + 1) * P], rows_x[:, side, t], ident[:])
                    mm.then_inc(turned, 1)

                def project(h, side):
                    j, par = 4 * h + side, side % 2
                    wait(pe, copied, j + 1)
                    wait(pe, y2_made, j - 3)
                    wait(pe, scaled, j - 1)
                    for t in range(T):
                        for n, to in enumerate((before_norm(side, t), through_r(par, t))):
                            pe.matmul(to, turned_x[:, par, t * P:(t + 1) * P], w_two[:, n * D:(n + 1) * D],
                                      start=True, stop=False)
                            mm = add_bias(pe, to, BIAS_TWO + n * D)
                    mm.then_inc(projected, 1)
                staggered(pe, SWEEP, [(0, turn), (2, project)], apart=1, unroll=4)

            @block.vector
            def _(dve):
                def norm2(h, side):
                    j, par = 4 * h + side, side % 2
                    wait(dve, projected, j + 1)
                    wait(dve, moments2, j)
                    for t in range(T):
                        last = dve.bn_stats(stats_x[:, 0, t, :], before_norm(side, t))
                    last.then_inc(stats2, 1)
                    wait(dve, stats2, j + 1)
                    dve.sem_inc(dve_gate, 1)
                    for t in range(T):
                        last = dve.bn_aggr(moments_x[:, 0, par, t, :], stats_x[:, 0, t, :])
                    last.then_inc(moments2, 1)

                def scale2(h, side):
                    j, par = 4 * h + side, side % 2
                    wait(dve, std2, j + 1)
                    wait(dve, y2_made, j - 1)
                    dve.reciprocal(rstd_x[:, 0, par], std_x[:, 0, par]).then_inc(rstd2, 1)
                    wait(dve, rstd2, j + 1)
                    dve.scalar_tensor_tensor(out=shift_x[:, 0, par], in0=moments_x[:, 0, par, :, 0], scalar=-1.0,
                                             in1=rstd_x[:, 0, par], op0=ALU.mult, op1=ALU.mult).then_inc(shift2, 1)
                    wait(dve, summed, j - 3)
                    for t in range(T):
                        last = dve.scalar_tensor_tensor(out=base_x[:, side, t], in0=through_r(par, t),
                                                        scalar=rstd_x[:, 0, par, t:t + 1], in1=b3_all[:],
                                                        op0=ALU.mult, op1=ALU.add)
                    last.then_inc(scaled, 1)

                def sum_up(h, side):
                    j, par = 4 * h + side, side % 2
                    wait(dve, scaled, j + 1)
                    wait(dve, y2_made, j + 1)
                    wait(dve, y3_made, j - 1)
                    dve.scalar_tensor_tensor(out=pre_x[:, par], in0=base_x[:, side], scalar=0.0, in1=out_x[:, side],
                                             op0=ALU.max, op1=ALU.add).then_inc(summed, 1)
                    wait(dve, summed, j + 1)
                    wait(dve, moments3, j)
                    for t in range(T):
                        last = dve.bn_stats(stats_x[:, 1, t, :], pre_x[:, par, t])
                    last.then_inc(stats3, 1)
                    wait(dve, stats3, j + 1)
                    dve.sem_inc(dve_gate, 1)
                    for t in range(T):
                        last = dve.bn_aggr(moments_x[:, 1, par, t, :], stats_x[:, 1, t, :])
                    last.then_inc(moments3, 1)

                def scale3(h, side):
                    j, par = 4 * h + side, side % 2
                    wait(dve, std3, j + 1)
                    wait(dve, y3_made, j - 1)
                    dve.reciprocal(rstd_x[:, 1, par], std_x[:, 1, par]).then_inc(rstd3, 1)
                    wait(dve, rstd3, j + 1)
                    dve.scalar_tensor_tensor(out=shift_x[:, 1, par], in0=moments_x[:, 1, par, :, 0], scalar=-1.0,
                                             in1=rstd_x[:, 1, par], op0=ALU.mult, op1=ALU.mult).then_inc(shift3, 1)
                staggered(dve, SWEEP, [(3, norm2), (5, sum_up), (3, scale2), (5, scale3)], apart=1, unroll=4)

            @block.scalar
            def _(act):
                def copy(h, side):
                    j, par = 4 * h + side, side % 2
                    wait(act, turned, j + 1)
                    wait(act, projected, j - 1)
                    act.copy(turned_x[:, par], bank[par][:]).then_inc(copied, 1)

                def root2(h, side):
                    j, par = 4 * h + side, side % 2
                    wait(act, moments2, j + 1)
                    act.activation(std_x[:, 0, par], moments_x[:, 0, par, :, 1], ACT.Sqrt, bias=eps_col[:])\
                        .then_inc(std2, 1)

                def make_y2(h, side):
                    j, par = 4 * h + side, side % 2
                    wait(act, shift2, j + 1)
                    wait(act, stored_y2[side], 16 * h)
                    wait(act, summed, j - 3)
                    for t in range(T):
                        last = act.activation(out_x[:, side, t], before_norm(side, t), ACT.Identity,
                                              scale=rstd_x[:, 0, par, t:t + 1], bias=shift_x[:, 0, par, t:t + 1])
                    last.then_inc(y2_made, 1)

                def root3(h, side):
                    j, par = 4 * h + side, side % 2
                    wait(act, moments3, j + 1)
                    act.activation(std_x[:, 1, par], moments_x[:, 1, par, :, 1], ACT.Sqrt, bias=eps_col[:])\
                        .then_inc(std3, 1)

                def make_y3(h, side):
                    j, par = 4 * h + side, side % 2
                    wait(act, shift3, j + 1)
                    wait(act, stored_y3[side], 16 * h)
                    for t in range(T):
                        last = act.activation(out_y[:, side, t], pre_x[:, par, t], ACT.Identity,
                                              scale=rstd_x[:, 1, par, t:t + 1], bias=shift_x[:, 1, par, t:t + 1])
                    last.then_inc(y3_made, 1)
                staggered(act, SWEEP, [(4, make_y2), (3, root2), (1, copy), (6, make_y3), (5, root3)], apart=1, unroll=4)

        phase(sweep_two)

        def layer_2(block, sem):
            gathered = [sem(f"gathered{i}") for i in range(4)]
            scattered = [sem(f"scattered{i}") for i in range(4)]
            stored = [sem(f"stored{i}") for i in range(4)]
            keep_in = sem("keep_in")
            keep_turned = sem("keep_turned")
            keep_copied = sem("keep_copied")
            turned_own = sem("turned_own")
            turned_src = sem("turned_src")
            copied_own = sem("copied_own")
            copied_src = sem("copied_src")
            message = sem("message")
            messages_out = sem("messages_out")
            summed_n = sem("summed_n")
            summed_m = sem("summed_m")
            summed_sq = sem("summed_sq")
            found_max = sem("found_max")
            found_min = sem("found_min")
            inverted_n = sem("inverted_n")
            inverted = sem("inverted")
            mean_made = sem("mean_made")
            mean_squared = sem("mean_squared")
            sq_scaled = sem("sq_scaled")
            var_made = sem("var_made")
            var_cut = sem("var_cut")
            dev_made = sem("dev_made")
            n_turned = sem("n_turned")
            log_made = sem("log_made")
            scales_made = sem("scales_made")
            projected = sem("projected")
            plain_out = sem("plain_out")
            amplified = sem("amplified")
            summed = sem("summed")
            ln = Norm(sem, "y2")

            @block.gpsimd
            def _(pool):
                bound = nc.gpsimd.to_reg(N - 1)

                def gathers(h, side):
                    j, par = 4 * h + side, side % 2
                    wait(pool, turned_own, j - 3)
                    wait(pool, turned_src, j - 3)
                    pool.sem_inc(pool_gate, 1)
                    for t in range(T):
                        gather(rows_x[:, side, t], y1_table, idx_a[:, side, t:t + 1], gathered[side], bound)
                    for t in range(T):
                        gather(base_x[:, side, t], y1_table, idx_b[:, side, t:t + 1], gathered[side], bound)

                def scatters(h, side):
                    wait(pool, ln.done, 4 * h + side + 1)
                    pool.sem_inc(pool_gate, 1)
                    for t in range(T):
                        scatter(y2_table, idx_w[:, side, t:t + 1], out_x[:, side, t], scattered[side], bound)
                pool_steps(pool, sem, ((idx_a, list_key[1]), (idx_b, list_other[1])), list_write[1],
                           gathers, scatters, gathered, scattered, 128)

            @block.sync
            def _(sp):
                def store(h, side):
                    wait(sp, ln.done, 4 * h + side + 1)
                    sp.dma_start(by_slot(y2_slots, 4 * h + side), out_x[:, side]).then_inc(stored[side], 16)
                staggered(sp, NSTEP, [(0, store)], unroll=4)
                for side in range(4):
                    sp.wait_ge(stored[side], 16 * steps_of(side))

            @block.tensor
            def _(pe):
                def turn(h, side):
                    j = 4 * h + side
                    keep_to_row_pe(pe, j, keep_in, keep_turned, keep_copied)
                    wait(pe, gathered[side], 128 * (h + 1))
                    wait(pe, copied_own, j)
                    for t in range(T):
                        mm = pe.transpose(bank[1][:, t * P:(t + 1) * P], rows_x[:, side, t], ident[:])
                    mm.then_inc(turned_own, 1)
                    wait(pe, copied_src, j)
                    for t in range(T):
                        mm = pe.transpose(bank[2][:, t * P:(t + 1) * P], base_x[:, side, t], ident[:])
                    mm.then_inc(turned_src, 1)

                def messages(h, side):
                    j, par = 4 * h + side, side % 2
                    wait(pe, copied_own, j + 1)
                    wait(pe, copied_src, j + 1)
                    wait(pe, messages_out, j)
                    pe.matmul(bank[3][:], w_dst_t[:], own_x[:, side], start=True, stop=False)
                    pe.matmul(bank[3][:], w_src_t[:], turned_x[:, par], start=False, stop=True).then_inc(message, 1)

                def counts(h, side):
                    j, par = 4 * h + side, side % 2
                    wait(pe, summed_n, j + 1)
                    wait(pe, log_made, j)
                    wait(pe, inverted, j)
                    for t in range(T):
                        mm = pe.matmul(bank[4][:, t:t + 1], agg_n[:, par, t * P:(t + 1) * P], ident[:, 0:1],
                                       start=True, stop=True)
                    mm.then_inc(n_turned, 1)

                def project(h, side, ts):
                    j, par = 4 * h + side, side % 2
                    wait(pe, found_max, j + 1)
                    wait(pe, found_min, j + 1)
                    wait(pe, mean_made, j + 1)
                    wait(pe, dev_made, j + 1)
                    for t in ts:
                        tile = T * j + t
                        cols = slice(t * P, (t + 1) * P)
                        wait(pe, summed, tile - 1)
                        wait(pe, plain_out, tile - 1)
                        to = bank[5 + t % 2]
                        pe.matmul(to[:, 0:D], own_x[:, side, cols], w_own[:], start=True, stop=False,
                                  skip_group_check=True)
                        add_bias(pe, to[:, 0:D], BIAS_B2, last=False)
                        for n, a in enumerate((agg_max[:, par, cols], agg_min[:, par, cols], mean[:, par, cols],
                                               dev[:, par, cols])):
                            mm = pe.matmul(to[:, 0:3 * D], a, w_agg[:, n], start=False, stop=(n == 3),
                                           skip_group_check=True)
                        mm.then_inc(projected, 1)

                def project_first(h, side):
                    project(h, side, (0, 1))

                def project_second(h, side):
                    project(h, side, (2, 3))
                staggered(pe, NSTEP, [(1, messages), (2, project_first), (0, turn), (1, counts),
                                      (2, project_second)], unroll=4)

            @block.scalar
            def _(act):
                def take_messages(h, side):
                    j = 4 * h + side
                    wait(act, message, j + 1)
                    wait(act, summed_sq, j)
                    wait(act, found_max, j)
                    wait(act, found_min, j)
                    act.activation(msg[:], bank[3][:], ACT.Identity, bias=b_pre_col[:])
                    act.activation(msg_sq[:], bank[3][:], ACT.Square, bias=b_pre_col[:]).then_inc(messages_out, 1)

                def square_mean(h, side):
                    j, par = 4 * h + side, side % 2
                    wait(act, mean_made, j + 1)
                    wait(act, var_made, j)
                    act.activation(mean_sq[:], mean[:, par], ACT.Square).then_inc(mean_squared, 1)

                def root_var(h, side):
                    j, par = 4 * h + side, side % 2
                    wait(act, var_cut, j + 1)
                    wait(act, projected, T * (j - 1))
                    act.activation(dev[:, par], var[:], ACT.Sqrt, bias=eps_col[:]).then_inc(dev_made, 1)

                def take_turned(h, side):
                    j, par = 4 * h + side, side % 2
                    wait(act, keep_turned, j + 1)
                    wait(act, summed_n, j - 1)
                    wait(act, summed_m, j - 1)
                    wait(act, summed_sq, j - 1)
                    wait(act, found_max, j - 1)
                    wait(act, found_min, j - 1)
                    act.copy(keep_row[:, par], bank[0][:])
                    act.activation(low_row[:, par], bank[0][:], ACT.Copy, scale=BIG, bias=-BIG)
                    act.activation(high_row[:, par], bank[0][:], ACT.Copy, scale=-BIG, bias=BIG)\
                        .then_inc(keep_copied, 1)
                    wait(act, turned_own, j + 1)
                    wait(act, projected, T * (j - 3))
                    act.copy(own_x[:, side], bank[1][:]).then_inc(copied_own, 1)

                def log_counts(h, side):
                    j, par = 4 * h + side, side % 2
                    wait(act, n_turned, j + 1)
                    wait(act, summed, T * (j - 1))
                    wait(act, scales_made, j - 1)
                    act.activation(scales[:, par, 1], bank[4][:, 0:T], ACT.Ln, bias=one_col[:])\
                        .then_inc(log_made, 1)

                def take_plain(h, side, ts):
                    j, par = 4 * h + side, side % 2
                    for t in ts:
                        tile = T * j + t
                        wait(act, projected, tile + 1)
                        wait(act, amplified, tile - T)
                        act.copy(plain_x[:, par, t], bank[5 + t % 2][:, 0:D]).then_inc(plain_out, 1)

                def root_norm(h, side):
                    norm_std(act, ln, 4 * h + side)
                staggered(act, NSTEP, [
                    (1, take_messages), (1, square_mean), (2, lambda h, side: take_plain(h, side, (0,))),
                    (1, root_var), (2, lambda h, side: take_plain(h, side, (1,))), (0, take_turned),
                    (1, log_counts), (2, lambda h, side: take_plain(h, side, (2, 3))), (2, root_norm)], unroll=4)

            @block.vector
            def _(dve):
                last_of = slice(STEP - 1, STEP)

                def keep_cols_in(h, side):
                    keep_to_cols_dve(dve, 4 * h + side, 1, keep_in, keep_turned)

                def count_and_sum(h, side):
                    j, par = 4 * h + side, side % 2
                    wait(dve, keep_copied, j + 1)
                    wait(dve, summed_n, j)
                    wait(dve, n_turned, j - 1)
                    dve.tensor_tensor_scan(agg_n[:, par], keep_row[:, par], ones_step[:],
                                           agg_n[:, 1 - par, last_of], ALU.mult, ALU.add).then_inc(summed_n, 1)
                    wait(dve, summed_n, j + 1)
                    dve.reciprocal(inv_n[:], agg_n[:, par]).then_inc(inverted_n, 1)
                    wait(dve, messages_out, j + 1)
                    wait(dve, summed_m, j)
                    dve.tensor_tensor_scan(agg[:, par], keep_row[:, par], msg[:],
                                           agg[:, 1 - par, last_of], ALU.mult, ALU.add).then_inc(summed_m, 1)
                    wait(dve, summed_m, j + 1)
                    wait(dve, inverted_n, j + 1)
                    wait(dve, projected, T * (j - 1))
                    dve.tensor_tensor(mean[:, par], agg[:, par], inv_n[:], ALU.mult).then_inc(mean_made, 1)

                def variance(h, side):
                    j, par = 4 * h + side, side % 2
                    wait(dve, summed_sq, j)
                    dve.tensor_tensor_scan(agg_sq[:, par], keep_row[:, par], msg_sq[:],
                                           agg_sq[:, 1 - par, last_of], ALU.mult, ALU.add).then_inc(summed_sq, 1)
                    wait(dve, summed_sq, j + 1)
                    wait(dve, dev_made, j)
                    dve.tensor_tensor(var[:], agg_sq[:, par], inv_n[:], ALU.mult).then_inc(sq_scaled, 1)
                    wait(dve, sq_scaled, j + 1)
                    wait(dve, mean_squared, j + 1)
                    dve.tensor_tensor(var[:], var[:], mean_sq[:], ALU.subtract).then_inc(var_made, 1)
                    wait(dve, var_made, j + 1)
                    dve.tensor_scalar(var[:], var[:], 0.0, None, ALU.max).then_inc(var_cut, 1)

                def copy_src(h, side):
                    j, par = 4 * h + side, side % 2
                    wait(dve, turned_src, j + 1)
                    wait(dve, message, j - 1)
                    dve.tensor_copy(turned_x[:, par], bank[2][:]).then_inc(copied_src, 1)

                def extremes(h, side):
                    j, par = 4 * h + side, side % 2
                    wait(dve, found_max, j)
                    wait(dve, projected, T * (j - 1))
                    dve.tensor_tensor_scan(agg_max[:, par], low_row[:, par], msg[:],
                                           agg_max[:, 1 - par, last_of], ALU.add, ALU.max).then_inc(found_max, 1)
                    wait(dve, found_min, j)
                    dve.tensor_tensor_scan(agg_min[:, par], high_row[:, par], msg[:],
                                           agg_min[:, 1 - par, last_of], ALU.add, ALU.min).then_inc(found_min, 1)

                def invert(h, side):
                    j, par = 4 * h + side, side % 2
                    wait(dve, log_made, j + 1)
                    dve.sem_inc(dve_gate, 1)
                    dve.reciprocal(inv_count[:, bass.ds(j * T, T)], bank[4][:, 0:T]).then_inc(inverted, 1)
                    wait(dve, log_made, j + 1)
                    wait(dve, summed, T * (j - 1))
                    dve.reciprocal(scales[:, par, 2], scales[:, par, 1]).then_inc(scales_made, 1)

                def add_scaled(h, side, ts):
                    j, par = 4 * h + side, side % 2
                    wait(dve, scales_made, j + 1)
                    wait(dve, ln.done, j)
                    for t in ts:
                        tile = T * j + t
                        psum = bank[5 + t % 2]
                        wait(dve, plain_out, tile + 1)
                        dve.scalar_tensor_tensor(out=pre[:, t], in0=psum[:, D:2 * D],
                                                 scalar=scales[:, par, 1, t:t + 1],
                                                 in1=plain_x[:, par, t], op0=ALU.mult, op1=ALU.add)\
                            .then_inc(amplified, 1)
                        wait(dve, amplified, tile + 1)
                        dve.scalar_tensor_tensor(out=pre[:, t], in0=psum[:, 2 * D:3 * D],
                                                 scalar=scales[:, par, 2, t:t + 1], in1=pre[:, t],
                                                 op0=ALU.mult, op1=ALU.add).then_inc(summed, 1)

                def norm(h, side):
                    j = 4 * h + side
                    wait(dve, summed, T * (j + 1))
                    norm_moments(dve, ln, j, pre)
                    wait(dve, stored[side], 16 * h)
                    wait(dve, scattered[side], 64 * h)
                    norm_rows(dve, ln, j, pre, out_x[:, side])
                staggered(dve, NSTEP, [
                    (0, keep_cols_in), (1, count_and_sum), (2, lambda h, side: add_scaled(h, side, (0,))),
                    (1, variance), (2, lambda h, side: add_scaled(h, side, (1,))), (0, copy_src),
                    (1, extremes), (2, lambda h, side: add_scaled(h, side, (2,))), (1, invert),
                    (2, lambda h, side: add_scaled(h, side, (3,))), (2, norm)], unroll=4)

        phase(layer_2)

        def layer_3(block, sem):
            gathered = [sem(f"gathered{i}") for i in range(4)]
            scattered = [sem(f"scattered{i}") for i in range(4)]
            loaded = [sem(f"loaded{i}") for i in range(4)]
            keep_in = sem("keep_in")
            keep_turned = sem("keep_turned")
            keep_copied = sem("keep_copied")
            turned = sem("turned")
            scanned = sem("scanned")
            own_turned = sem("own_turned")
            own_copied = sem("own_copied")
            own_projected = sem("own_projected")
            own_out = sem("own_out")
            projected = sem("projected")
            joined = sem("joined")
            summed = sem("summed")
            ln = Norm(sem, "y3")

            @block.gpsimd
            def _(pool):
                bound = nc.gpsimd.to_reg(N - 1)

                def gathers(h, side):
                    wait(pool, turned, 4 * h + side - 3)
                    pool.sem_inc(pool_gate, 1)
                    for t in range(T):
                        gather(rows_x[:, side, t], y2_table, idx_a[:, side, t:t + 1], gathered[side], bound)

                def scatters(h, side):
                    wait(pool, ln.done, 4 * h + side + 1)
                    pool.sem_inc(pool_gate, 1)
                    for t in range(T):
                        scatter(out, idx_w[:, side, t:t + 1], out_x[:, side, t], scattered[side], bound)
                pool_steps(pool, sem, ((idx_a, list_other[1]),), list_write[1],
                           gathers, scatters, gathered, scattered, 64)

            @block.sync
            def _(sp):
                def load(h, side):
                    j, par = 4 * h + side, side % 2
                    wait(sp, own_turned, j - 3)
                    wait(sp, summed, j - 3)
                    sp.dma_start(base_x[:, side], by_slot(y2_slots, j)).then_inc(loaded[side], 16)
                staggered(sp, NSTEP, [(0, load)], unroll=4)

            @block.vector
            def _(dve):
                def scan(h, side):
                    j, par = 4 * h + side, side % 2
                    keep_to_cols_dve(dve, j, 1, keep_in, keep_turned)
                    wait(dve, turned, j + 1)
                    wait(dve, keep_copied, j + 1)
                    wait(dve, scanned, j)
                    wait(dve, projected, j - 1)
                    dve.tensor_tensor_scan(agg[:, par], keep_row[:, par], bank[1][:],
                                           agg[:, 1 - par, STEP - 1:STEP], ALU.mult, ALU.add).then_inc(scanned, 1)

                def finish(h, side):
                    j, par = 4 * h + side, side % 2
                    wait(dve, projected, j + 1)
                    wait(dve, own_out, j + 1)
                    wait(dve, ln.done, j)
                    dve.sem_inc(dve_gate, 1)
                    for t in range(T):
                        last = dve.scalar_tensor_tensor(out=pre_b[:, t], in0=bank4(2)[:, t],
                                                        scalar=inv_count[:, bass.ds(j * T + t, 1)],
                                                        in1=plain_x[:, par, t], op0=ALU.mult, op1=ALU.add)
                    last.then_inc(joined, 1)
                    wait(dve, joined, j + 1)
                    dve.scalar_tensor_tensor(out=pre[:], in0=pre_b[:], scalar=0.0, in1=base_x[:, side],
                                             op0=ALU.max, op1=ALU.add).then_inc(summed, 1)
                    wait(dve, summed, j + 1)
                    norm_moments(dve, ln, j, pre)
                    wait(dve, scattered[side], 64 * h)
                    norm_rows(dve, ln, j, pre, out_x[:, side])
                staggered(dve, NSTEP, [(0, scan), (1, finish)], unroll=4)

            @block.scalar
            def _(act):
                def scan(h, side):
                    j, par = 4 * h + side, side % 2
                    wait(act, keep_turned, j + 1)
                    wait(act, scanned, j - 1)
                    act.copy(keep_row[:, par], bank[0][:]).then_inc(keep_copied, 1)
                    wait(act, own_turned, j + 1)
                    wait(act, own_projected, j - 1)
                    act.copy(turned_x[:, par], bank[3][:]).then_inc(own_copied, 1)
                    wait(act, own_projected, j + 1)
                    wait(act, joined, j - 1)
                    act.copy(plain_x[:, par], bank4(4)).then_inc(own_out, 1)

                def finish(h, side):
                    j, par = 4 * h + side, side % 2
                    norm_std(act, ln, j)
                staggered(act, NSTEP, [(0, scan), (1, finish)], unroll=4)

            @block.tensor
            def _(pe):
                def scan(h, side):
                    j, par = 4 * h + side, side % 2
                    keep_to_row_pe(pe, j, keep_in, keep_turned, keep_copied)
                    wait(pe, loaded[side], 16 * (h + 1))
                    wait(pe, own_copied, j)
                    for t in range(T):
                        mm = pe.transpose(bank[3][:, t * P:(t + 1) * P], base_x[:, side, t], ident[:])
                    mm.then_inc(own_turned, 1)
                    wait(pe, gathered[side], 64 * (h + 1))
                    wait(pe, scanned, j)
                    for t in range(T):
                        mm = pe.transpose(bank[1][:, t * P:(t + 1) * P], rows_x[:, side, t], ident[:])
                    mm.then_inc(turned, 1)
                    wait(pe, own_copied, j + 1)
                    wait(pe, own_out, j)
                    for t in range(T):
                        to = bank[4][:, t * D:(t + 1) * D]
                        pe.matmul(to, turned_x[:, par, t * P:(t + 1) * P], w_r_t[:], start=True, stop=False)
                        mm = add_bias(pe, to, BIAS_B3)
                    mm.then_inc(own_projected, 1)
                    wait(pe, scanned, j + 1)
                    wait(pe, joined, j)
                    for t in range(T):
                        mm = pe.matmul(bank[2][:, t * D:(t + 1) * D], agg[:, par, t * P:(t + 1) * P], w_l_t[:],
                                       start=True, stop=True)
                    mm.then_inc(projected, 1)
                staggered(pe, NSTEP, [(0, scan)], unroll=4)

        phase(layer_3)


_INS = ["x", "src", "dst", "edge_weight", "L0_gnn_weight", "L0_gnn_bias_param", "L1_gnn_W", "L1_gnn_b",
        "L2_gnn_W_pre", "L2_gnn_b_pre", "L2_gnn_W_post", "L2_gnn_b_post", "L2_gnn_W_lin", "L2_gnn_b_lin",
        "L3_gnn_W_l", "L3_gnn_W_r", "L3_gnn_b"]


def kernel(**inputs):
    import numpy as _np
    import concourse.bacc as _bacc
    from concourse.bass_utils import run_bass_kernel_spmd as _run

    nc = _bacc.Bacc("TRN2", target_bir_lowering=False, num_devices=1)
    arrays, args = {}, []
    for name in _INS:
        a = _np.ascontiguousarray(inputs[name])
        arrays[f"in_{name}_dram"] = a
        args.append(nc.dram_tensor(f"in_{name}_dram", a.shape, mybir.dt.from_np(a.dtype), kind="ExternalInput").ap())
    args.append(nc.dram_tensor("out_0_dram", (N, D), F32, kind="ExternalOutput").ap())
    gnn_kernel(nc, *args)
    r = _run(nc, [arrays], core_ids=[0])
    return r.results[0]["out_0_dram"]
```

```python
from contextlib import ExitStack

import concourse.bass as bass
from concourse import mybir

ALU = mybir.AluOpType
ACT = mybir.ActivationFunctionType
F32 = mybir.dt.float32
F16 = mybir.dt.float16
BF16 = mybir.dt.bfloat16
I32 = mybir.dt.int32

P = 128
D = 128
EPS = 1e-5
LN2 = 0.6931471805599453

N = 100000
E = 25000
T = 4
STEP = T * P
NSTEP = 50
SLOTS = NSTEP * STEP
TILES = SLOTS // P
PAD_KEY = N
EDGE_ROWS = E // TILES
FAR = 1 << 20

LO_BITS = 8
LO = 1 << LO_BITS
HI_PARTS = 4
HI_ROWS = -(-(N + 1) // (LO * HI_PARTS))
HI = HI_PARTS * HI_ROWS

G = 5
NG = TILES // G

SWEEP = -(-N // STEP)
HALF = TILES // 2
SORTED = 2
SORT_STEPS = TILES // SORTED
BIG = 3.0e38


def wait(eng, sem, count):
    if isinstance(count, int) and count <= 0:
        return
    eng.wait_ge(sem, count)


def pairs(eng, steps, body):
    body(0, 0)
    body(0, 1)
    with eng.Fori(1, steps // 2, 1) as h:
        body(h, 0)
        body(h, 1)


def staggered(eng, steps, stages, apart=0, beside=None):
    own = [(lag, body, count[0] if count else steps) for lag, body, *count in
           (stage for stage in stages if not isinstance(stage, int))]
    others, other_steps, ratio = beside if beside else ([], 4 * steps, 1)

    def run(turn, place, lag, body, count):
        side = (place - lag) % 4
        h = turn + (place - lag - side) // 4
        if not isinstance(h, int) or 0 <= 4 * h + side < count:
            body(h, side)

    def at(turn, place):
        for stage in stages:
            if isinstance(stage, int):
                for lag, body in others:
                    run(turn * ratio, place * ratio + stage, lag, body, other_steps)
            else:
                lag, body, *count = stage
                run(turn, place, lag, body, count[0] if count else steps)
    longest = max([lag for lag, _, _ in own] + [-(-lag // ratio) for lag, _ in others])
    first = -(-longest // 4) + 1
    last = min([count for _, _, count in own] + [other_steps // ratio]) // 4 - apart
    for n in range(4 * first):
        at(n // 4, n % 4)
    with eng.Fori(first, last, 1) as h:
        for place in range(4):
            at(h, place)
    for n in range(4 * last, max([lag + count for lag, _, count in own]
                                 + [-(-(lag + other_steps) // ratio) for lag, _ in others])):
        at(n // 4, n % 4)


def gnn_kernel(nc, x, src, dst, edge_weight, w0, b0, w1, b1, w_pre, b_pre, w_post, b_post,
               w_lin, b_lin, w_l, w_r, b3, out):
    with ExitStack() as ctx:
        def sb(name, shape, dt=F32):
            return ctx.enter_context(nc.sbuf_tensor(name, shape, dt))

        def sem(name):
            return ctx.enter_context(nc.semaphore(name))

        def dram(name, shape, dt=F32):
            return nc.dram_tensor(name, shape, dt, kind="Internal").ap()

        recs = dram("recs", (SLOTS, 4), I32)
        recs_lo = [dram(f"recs_lo{q}", (SLOTS, 4), I32) for q in range(2)]
        sorted_recs = [dram(f"sorted_recs{q}", (SLOTS + 2, 4), I32) for q in range(2)]
        dinv_table = dram("dinv_table", (HI * LO, 1))
        u_table = dram("u_table", (N, D))
        v_table = dram("v_table", (N, D))
        y1_table = dram("y1_table", (N, D))
        y2_table = dram("y2_table", (N, D))
        y0_slots = dram("y0_slots", (SLOTS, D))
        u_slots = dram("u_slots", (SLOTS, D))
        v_slots = dram("v_slots", (SLOTS, D))
        y2_slots = dram("y2_slots", (SLOTS, D))

        bank = [ctx.enter_context(nc.psum_tensor(f"bank{i}", [P, 512], F32)) for i in range(8)]

        ident = sb("ident", [P, P])
        before = sb("before", [P, P], F16)
        not_before = sb("not_before", [P, P], F16)
        ones16 = sb("ones16", [P, P], F16)
        zeros16 = sb("zeros16", [P, 512], F16)
        count16 = sb("count16", [P, HI], F16)
        ones_row = sb("ones_row", [1, P])
        ones_step = sb("ones_step", [P, 512])
        eps_col = sb("eps_col", [P, 1])
        one_col = sb("one_col", [P, 1])
        w0_sb = sb("w0_sb", [P, D])
        w1_t = sb("w1_t", [P, D])
        w_dst_t = sb("w_dst_t", [P, D])
        w_src_t = sb("w_src_t", [P, D])
        w_lin_t = sb("w_lin_t", [P, D])
        w_l_t = sb("w_l_t", [P, D])
        w_r_t = sb("w_r_t", [P, D])
        w_own = sb("w_own", [P, D])
        w_agg = sb("w_agg", [P, 4, 3 * D])
        b_pre_col = sb("b_pre_col", [P, 1])
        center = sb("center", [P, P])
        w1_c = sb("w1_c", [P, D])
        w_r_c = sb("w_r_c", [P, D])
        w_two = sb("w_two", [P, 2 * D])
        bias3 = sb("bias3", [3, 6 * D], BF16)
        ones3 = sb("ones3", [3, P], BF16)
        b3_all = sb("b3_all", [P, D])
        b0_all = sb("b0_all", [P, D])
        b1_all = sb("b1_all", [P, D])

        list_w = sb("list_w", [P, TILES])
        list_key = [sb(f"list_key{q}", [P, TILES], I32) for q in range(2)]
        list_other = [sb(f"list_other{q}", [P, TILES], I32) for q in range(2)]
        list_write = [sb(f"list_write{q}", [P, TILES], I32) for q in range(2)]
        list_keep = [sb(f"list_keep{q}", [P, TILES]) for q in range(2)]
        dinv_own = sb("dinv_own", [P, TILES])
        dinv2_own = sb("dinv2_own", [P, TILES])
        inv_count = sb("inv_count", [P, TILES])

        idx_a = sb("idx_a", [P, 4, T], I32)
        idx_b = sb("idx_b", [P, 4, T], I32)
        idx_w = sb("idx_w", [P, 4, T], I32)
        keep_cols = sb("keep_cols", [P, T])
        keep_row = sb("keep_row", [P, 2, STEP])
        low_row = sb("low_row", [P, 2, STEP])
        high_row = sb("high_row", [P, 2, STEP])
        agg = sb("agg", [P, 2, STEP])
        agg_max = sb("agg_max", [P, 2, STEP])
        agg_min = sb("agg_min", [P, 2, STEP])
        agg_sq = sb("agg_sq", [P, 2, STEP])
        agg_n = sb("agg_n", [P, 2, STEP])
        msg = sb("msg", [P, STEP])
        msg_sq = sb("msg_sq", [P, STEP])
        inv_n = sb("inv_n", [P, 2, STEP])
        mean_sq = sb("mean_sq", [P, STEP])
        var = sb("var", [P, STEP])
        pre = sb("pre", [P, T, D])
        pre_b = sb("pre_b", [P, T, D])
        stats = sb("stats", [P, T, 6])
        moments = sb("moments", [P, T, 2])
        std = sb("std", [P, T])
        rstd = sb("rstd", [P, T])

        rec = sb("rec", [P, 2, G, 4], I32)
        digit_i = sb("digit_i", [P, 4, G], I32)
        digit = sb("digit", [P, 4, G])
        recs_x = sb("recs_x", [P, 4, 2, SORTED, 4], I32)
        digits_i = sb("digits_i", [P, 2, SORTED], I32)
        digits = sb("digits", [P, 2, SORTED])
        onehot_x = sb("onehot_x", [P, 2, SORTED, 2, HI], F16)
        rank_terms = sb("rank_terms", [P, 2, HI])
        position_x = sb("position_x", [P, 2, SORTED, 2])
        index_x = sb("index_x", [P, 4, SORTED, 2], I32)
        onehot = sb("onehot", [P, 2, 2 * (LO + HI)], F16)
        totals = sb("totals", [P, 2 * (LO + HI)])
        inclusive = sb("inclusive", [P, 2 * (LO + HI)])
        first_place = sb("first_place", [P, 2 * (LO + HI)])
        degree = sb("degree", [P, HI_PARTS * LO])
        fence = sb("fence", [2, 4], I32)
        prep = sb("prep", [HALF, 3, P, 4], I32)
        prep_f = sb("prep_f", [HALF, 6, P])


        set_up_memory = ExitStack()

        def set_up_sb(name, shape, dt=F32):
            return set_up_memory.enter_context(nc.sbuf_tensor(name, shape, dt))
        w1_raw = set_up_sb("w1_raw", [P, D])
        w_pre_raw = set_up_sb("w_pre_raw", [P, 2 * D])
        w_post_sb = set_up_sb("w_post_sb", [P, 13 * D])
        w_lin_raw = set_up_sb("w_lin_raw", [P, D])
        w_l_raw = set_up_sb("w_l_raw", [P, D])
        w_r_raw = set_up_sb("w_r_raw", [P, D])
        b0_row = set_up_sb("b0_row", [1, D])
        b1_row = set_up_sb("b1_row", [1, D])
        b3_row = set_up_sb("b3_row", [1, D])
        b_lin_row = set_up_sb("b_lin_row", [1, D])
        b_post_col = set_up_sb("b_post_col", [P, 1])
        b2_row = set_up_sb("b2_row", [1, D])
        b2_alone = set_up_sb("b2_alone", [1, D])
        w_own_t = set_up_sb("w_own_t", [P, D])
        b0_col = set_up_sb("b0_col", [P, 1])
        b2_alone_col = set_up_sb("b2_alone_col", [P, 1])
        bias = set_up_sb("bias", [1, 6 * D])
        bias_rest = set_up_sb("bias_rest", [1, 2, 6 * D])
        bias_part = set_up_sb("bias_part", [1, 3, 6 * D], BF16)
        count_i = set_up_sb("count_i", [P, HI], I32)
        std_cols = set_up_sb("std_cols", [P, 3])
        raw_i = set_up_sb("raw_i", [P, 3, TILES], I32)
        rec_all = set_up_sb("rec_all", [P, TILES, 4], I32)

        def by_slot(table, j):
            return table[bass.ds(j * STEP, STEP), :].rearrange("(t p) d -> p t d", p=P)

        def by_node(table, j):
            start = N - STEP if isinstance(j, int) and j == SWEEP - 1 else j * STEP
            return table[bass.ds(start, STEP), :].rearrange("(p t) d -> p t d", t=T)

        def tiles(a):
            return a.rearrange("p (t d) -> p t d", t=T)

        def bank4(i):
            return tiles(bank[i][:])

        def over_tiles(a):
            return a.rearrange("p (t d) -> p t d", t=1).broadcast_to([a.shape[0], T, D])

        def gather(to, table, idx, done, bound):
            nc.gpsimd.indirect_dma_start(
                out=to, out_offset=None, in_=table, in_offset=bass.IndirectOffsetOnAxis(ap=idx, axis=0),
                bounds_check=bound, oob_is_err=False).then_inc(done, 16)

        def scatter(table, idx, rows, done, bound):
            nc.gpsimd.indirect_dma_start(
                out=table, out_offset=bass.IndirectOffsetOnAxis(ap=idx, axis=0), in_=rows, in_offset=None,
                bounds_check=bound, oob_is_err=False).then_inc(done, 16)

        pool_gate = nc.alloc_semaphore("pool_gate")
        dve_gate = nc.alloc_semaphore("dve_gate")
        act_gate = nc.alloc_semaphore("act_gate")

        def phase(build, *args):
            sems = []

            def sem(name):
                sems.append(nc.alloc_semaphore(f"{name}_{len(sems)}_{nc.next_id()}"))
                return sems[-1]
            block = nc.Block()
            with block as b:
                build(b, sem, *args)
            nc.clear_and_free_semaphores(sems)
            nc.all_engine_barrier()

        BIAS_ONE, BIAS_TWO, BIAS_B0, BIAS_B2, BIAS_B3 = 0, D, 3 * D, 4 * D, 5 * D

        def add_bias(pe, to, at, width=D, last=True):
            return pe.matmul(to, ones3[:], bias3[:, at:at + width], start=False, stop=last,
                             skip_group_check=not last)

        def set_up(block, sem):
            filled = sem("filled")
            set_dve = sem("set_dve")
            selected = sem("selected")
            loaded = sem("loaded")
            edges_in = sem("edges_in")
            counted = sem("counted")
            interleaved = sem("interleaved")
            recs_out = sem("recs_out")
            w_turned = sem("w_turned")
            w_copied = sem("w_copied")
            merged = sem("merged")
            merged_out = sem("merged_out")
            bias_made = sem("bias_made")
            bias_split = sem("bias_split")
            raw = ((w1_raw, w1_t), (w_lin_raw, w_lin_t), (w_l_raw, w_l_t), (w_r_raw, w_r_t))

            @block.sync
            def _(sp):
                for to, what in ((w0_sb, w0), (w1_raw, w1), (w_pre_raw, w_pre), (w_post_sb, w_post),
                                 (w_lin_raw, w_lin), (w_l_raw, w_l), (w_r_raw, w_r)):
                    sp.dma_start(to[:], what).then_inc(loaded, 16)
                for to, what in ((b0_row, b0), (b1_row, b1), (b3_row, b3), (b_lin_row, b_lin)):
                    sp.dma_start(to[:], what.rearrange("(a d) -> a d", a=1)).then_inc(loaded, 16)
                for to, what in ((b_post_col, b_post), (b_pre_col, b_pre), (b0_col, b0)):
                    sp.dma_start(to[:], what.rearrange("(d a) -> d a", a=1)).then_inc(loaded, 16)
                sp.wait_ge(filled, 1)
                for n, what in enumerate((src, dst)):
                    sp.dma_start(raw_i[0:EDGE_ROWS, n, :], what.rearrange("(p j) -> p j", j=TILES))\
                        .then_inc(edges_in, 16)
                sp.dma_start(raw_i[0:EDGE_ROWS, 2, :].bitcast(F32),
                             edge_weight.rearrange("(p j) -> p j", j=TILES)).then_inc(edges_in, 16)
                sp.wait_ge(interleaved, 1)
                sp.dma_start(recs.rearrange("(p j) c -> p j c", j=TILES), rec_all[:]).then_inc(recs_out, 16)
                for q in range(2):
                    sp.dma_start(sorted_recs[q][0:1, :], fence[0:1, :]).then_inc(recs_out, 16)
                    sp.dma_start(sorted_recs[q][SLOTS + 1:SLOTS + 2, :], fence[1:2, :]).then_inc(recs_out, 16)
                sp.wait_ge(bias_split, 3)
                for n in range(3):
                    sp.dma_start(bias3[n:n + 1, :], bias_part[0:1, n, :]).then_inc(recs_out, 16)
                sp.wait_ge(recs_out, 128)

            @block.gpsimd
            def _(pool):
                nc.gpsimd.memset(raw_i[:, 0:2, :], PAD_KEY)
                nc.gpsimd.memset(raw_i[:, 2, :], 0)
                nc.gpsimd.memset(ident[:], 0.0)
                nc.gpsimd.memset(before[:], 1.0)
                nc.gpsimd.memset(not_before[:], 1.0)
                nc.gpsimd.memset(fence[:], PAD_KEY + 1).then_inc(filled, 1)
                pool.wait_ge(filled, 1)
                nc.gpsimd.affine_select(out=ident[:], in_=ident[:], compare_op=ALU.not_equal, fill=1.0,
                                        base=0, pattern=[[-1, P]], channel_multiplier=1)
                nc.gpsimd.affine_select(out=before[:], in_=before[:], compare_op=ALU.is_gt, fill=0.0,
                                        base=0, pattern=[[1, P]], channel_multiplier=-1)
                nc.gpsimd.affine_select(out=not_before[:], in_=not_before[:], compare_op=ALU.is_ge, fill=0.0,
                                        base=0, pattern=[[-1, P]], channel_multiplier=1)
                nc.gpsimd.memset(center[:], -1.0 / D)
                nc.gpsimd.iota(count_i[:], pattern=[[1, HI]], base=0, channel_multiplier=0)\
                    .then_inc(selected, 1)

            @block.tensor
            def _(pe):
                pe.wait_ge(loaded, 16 * 14)
                pe.wait_ge(selected, 1)
                pe.wait_ge(set_dve, 1)
                for n, (a, _) in enumerate(raw):
                    pe.transpose(bank[n][:, 0:D], a[:], ident[:]).then_inc(w_turned, 1)
                for n in range(2):
                    pe.transpose(bank[4 + n][:, 0:D], w_pre_raw[:, n * D:(n + 1) * D], ident[:])\
                        .then_inc(w_turned, 1)
                for n, b in enumerate((b0_row, b1_row)):
                    pe.matmul(bank[6 + n][:, 0:D], ones_row[:], b[:], start=True, stop=True)\
                        .then_inc(w_turned, 1)
                pe.wait_ge(w_copied, 8)
                for n in range(13):
                    to = bank[n // 4][:, (n % 4) * D:(n % 4 + 1) * D]
                    mm = pe.matmul(to, w_post_sb[:, n * D:(n + 1) * D], w_lin_t[:], start=True, stop=True)
                pe.matmul(bank[4][0:1, 0:D], b_post_col[:], w_lin_t[:], start=True, stop=True)\
                    .then_inc(merged, 1)
                pe.wait_ge(merged_out, 1)
                for n in range(3):
                    mm = pe.matmul(bank[5][0:1, 0:D], std_cols[:, n:n + 1], w_agg[:, 3, n * D:(n + 1) * D],
                                   start=(n == 0), stop=(n == 2))
                mm.then_inc(merged, 1)
                pe.wait_ge(merged_out, 2)
                pe.matmul(bank[0][:, 0:D], center[:], w1_t[:], start=True, stop=True)
                pe.matmul(bank[1][:, 0:D], center[:], w_r_t[:], start=True, stop=True)
                pe.transpose(bank[2][:, 0:D], w_own[:], ident[:])
                pe.matmul(bank[3][:, 0:1], b2_alone[:], ones_row[:, 0:1], start=True, stop=True)
                pe.matmul(bank[6][:, 0:D], ones_row[:], b3_row[:], start=True, stop=True).then_inc(merged, 1)
                pe.wait_ge(merged_out, 3)
                pe.matmul(bank[4][:, 0:D], w_own_t[:], w_r_c[:], start=True, stop=True)
                pe.matmul(bank[5][0:1, 0:D], b0_col[:], w1_c[:], start=True, stop=True)
                pe.matmul(bank[7][0:1, 0:D], b2_alone_col[:], w_r_c[:], start=True, stop=True)\
                    .then_inc(merged, 1)

            @block.vector
            def _(dve):
                dve.memset(ones16[:], 1.0)
                dve.memset(zeros16[:], 0.0)
                dve.memset(ones_row[:], 1.0)
                dve.memset(ones3[:], 1.0)
                dve.memset(ones_step[:], 1.0)
                dve.memset(eps_col[:], EPS)
                dve.memset(one_col[:], 1.0)
                dve.memset(std_cols[:, 0:1], EPS ** 0.5)
                dve.memset(std_cols[:, 1:2], EPS ** 0.5 * LN2)
                dve.memset(std_cols[:, 2:3], EPS ** 0.5 / LN2)
                dve.memset(agg[:], 0.0)
                dve.memset(agg_max[:], 0.0)
                dve.memset(agg_min[:], 0.0)
                dve.memset(agg_sq[:], 0.0)
                dve.memset(agg_n[:], 0.0).then_inc(set_dve, 1)
                dve.wait_ge(selected, 1)
                dve.tensor_copy(count16[:], count_i[:])
                dve.wait_ge(edges_in, 48)
                for n in range(3):
                    dve.tensor_copy(rec_all[:, :, n], raw_i[:, n, :])
                dve.tensor_scalar(rec_all[:, :, 3], raw_i[:, 2, :], 0, None, ALU.bitwise_and)\
                    .then_inc(interleaved, 1)
                for n, (_, to) in enumerate(raw):
                    dve.wait_ge(w_turned, n + 1)
                    dve.tensor_copy(to[:], bank[n][:, 0:D]).then_inc(w_copied, 1)
                for n, to in enumerate((w_dst_t, w_src_t, b0_all, b1_all)):
                    dve.wait_ge(w_turned, n + 5)
                    dve.tensor_copy(to[:], bank[4 + n][:, 0:D]).then_inc(w_copied, 1)
                dve.wait_ge(merged, 1)
                dve.tensor_tensor(w_own[:], bank[0][:, 0:D], ident[:], ALU.add)
                dve.tensor_tensor(b2_row[:], bank[4][0:1, 0:D], b_lin_row[:], ALU.add)
                for n in range(1, 13):
                    a, s = (n - 1) % 4, (n - 1) // 4
                    last = dve.tensor_copy(w_agg[:, a, s * D:(s + 1) * D],
                                           bank[n // 4][:, (n % 4) * D:(n % 4 + 1) * D])
                last.then_inc(merged_out, 1)
                dve.wait_ge(merged, 2)
                dve.wait_ge(merged_out, 1)
                dve.tensor_tensor(center[:], center[:], ident[:], ALU.add)
                dve.tensor_tensor(b2_alone[:], bank[5][0:1, 0:D], b2_row[:], ALU.add).then_inc(merged_out, 1)
                dve.wait_ge(merged, 3)
                dve.tensor_copy(w1_c[:], bank[0][:, 0:D])
                dve.tensor_copy(w_r_c[:], bank[1][:, 0:D])
                dve.tensor_copy(w_own_t[:], bank[2][:, 0:D])
                dve.tensor_copy(b2_alone_col[:], bank[3][:, 0:1])
                dve.tensor_copy(b3_all[:], bank[6][:, 0:D]).then_inc(merged_out, 1)
                dve.wait_ge(merged, 4)
                dve.wait_ge(merged_out, 2)
                dve.tensor_copy(w_two[:, 0:D], w_own[:])
                dve.tensor_copy(w_two[:, D:2 * D], bank[4][:, 0:D])
                dve.tensor_copy(bias[:, BIAS_ONE:BIAS_ONE + D], bank[5][0:1, 0:D])
                dve.tensor_copy(bias[:, BIAS_TWO:BIAS_TWO + D], b2_alone[:])
                dve.tensor_copy(bias[:, BIAS_TWO + D:BIAS_TWO + 2 * D], bank[7][0:1, 0:D])
                dve.tensor_copy(bias[:, BIAS_B0:BIAS_B0 + D], b0_row[:])
                dve.tensor_copy(bias[:, BIAS_B2:BIAS_B2 + D], b2_row[:])
                dve.tensor_copy(bias[:, BIAS_B3:BIAS_B3 + D], b3_row[:]).then_inc(bias_made, 1)
                dve.wait_ge(bias_made, 1)
                rest = bias[:]
                for n in range(3):
                    dve.tensor_copy(bias_part[:, n, :], rest).then_inc(bias_split, 1)
                    dve.wait_ge(bias_split, n + 1)
                    if n < 2:
                        dve.tensor_tensor(bias_rest[:, n, :], rest, bias_part[:, n, :], ALU.subtract)\
                            .then_inc(bias_made, 1)
                        dve.wait_ge(bias_made, n + 2)
                        rest = bias_rest[:, n, :]

        phase(set_up)

        set_up_memory.close()
        turned_x = sb("turned_x", [P, 2, STEP])
        own_x = sb("own_x", [P, 4, STEP])
        mean = sb("mean", [P, 2, STEP])
        dev = sb("dev", [P, 2, STEP])
        scales = sb("scales", [P, 2, 3, T])
        u_x = sb("u_x", [P, 4, T, D])
        with_b0_x = sb("with_b0_x", [P, 4, T, D])
        base_x = sb("base_x", [P, 4, T, D])
        rows_x = sb("rows_x", [P, 4, T, D])
        dinv_x = sb("dinv_x", [P, 4, T])
        out_x = sb("out_x", [P, 4, T, D])
        out_y = sb("out_y", [P, 4, T, D])
        out_z = sb("out_z", [P, 4, T, D])
        pre_x = sb("pre_x", [P, 2, T, D])
        plain_x = sb("plain_x", [P, 2, T, D])
        stats_x = sb("stats_x", [P, 2, T, 6])
        moments_x = sb("moments_x", [P, 2, 2, T, 2])
        std_x = sb("std_x", [P, 2, 2, T])
        rstd_x = sb("rstd_x", [P, 2, 2, T])
        shift_x = sb("shift_x", [P, 2, 2, T])
        factor_x = sb("factor_x", [P, 4, 6, T])
        factor_y = sb("factor_y", [P, 2, T])

        SRC_LO, DST_LO, SRC_HI, DST_HI = 0, LO, 2 * LO, 2 * LO + HI
        FIELDS = ((0, SRC_LO, LO, 0), (1, DST_LO, LO, 0), (0, SRC_HI, HI, LO_BITS), (1, DST_HI, HI, LO_BITS))

        def digit_of(dve, to, field, par, shift):
            return dve.tensor_scalar(to, rec[:, par, :, field], shift, (LO - 1) if shift == 0 else 0xFFFF,
                                     ALU.logical_shift_right, ALU.bitwise_and)

        def census(block, sem):
            loaded = [sem(f"loaded{i}") for i in range(2)]
            digits_int = sem("digits_int")
            digits_ready = sem("digits_ready")
            onehots = sem("onehots")
            counted = sem("counted")
            copied = sem("copied")
            summed_up = sem("summed_up")
            places = sem("places")
            std_made = sem("std_made")
            inverted = sem("inverted")
            table_out = sem("table_out")

            @block.sync
            def _(sp):
                def load(h, par):
                    wait(sp, digits_int, 2 * h + par - 1)
                    sp.dma_start(rec[:, par], recs[bass.ds((2 * h + par) * G * P, G * P), :]
                                 .rearrange("(t p) c -> p t c", p=P)).then_inc(loaded[par], 16)
                pairs(sp, NG, load)
                sp.wait_ge(inverted, 1)
                sp.dma_start(dinv_table.rearrange("(c p l) a -> p c (l a)", c=HI_PARTS, l=LO),
                             degree[0:HI_ROWS, :].rearrange("p (c l) -> p c l", c=HI_PARTS))\
                    .then_inc(table_out, 16)
                sp.wait_ge(table_out, 16)

            @block.vector
            def _(dve):
                def step(h, par):
                    j = 2 * h + par
                    wait(dve, loaded[par], 16 * (h + 1))
                    wait(dve, onehots, G * j)
                    for n, (field, _, _, shift) in enumerate(FIELDS):
                        last = digit_of(dve, digit_i[:, n, :], field, par, shift)
                    last.then_inc(digits_int, 1)
                    wait(dve, digits_int, j + 1)
                    dve.tensor_copy(digit[:], digit_i[:]).then_inc(digits_ready, 1)
                    wait(dve, digits_ready, j + 1)
                    for t in range(G):
                        tile = G * j + t
                        side = (G * par + t) % 2
                        wait(dve, counted, tile - 1)
                        for n, (_, at, width, _) in enumerate(FIELDS):
                            last = dve.tensor_scalar(onehot[:, side, at:at + width], count16[:, 0:width],
                                                     digit[:, n, t:t + 1], None, ALU.is_equal)
                        last.then_inc(onehots, 1)
                pairs(dve, NG, step)
                dve.wait_ge(counted, TILES)
                dve.tensor_copy(totals[:, 0:2 * LO], bank[0][:])
                dve.tensor_copy(totals[:, SRC_HI:SRC_HI + HI], bank[1][:, 0:HI])
                dve.tensor_copy(totals[:, DST_HI:DST_HI + HI], bank[2][:, 0:HI]).then_inc(copied, 1)
                dve.wait_ge(copied, 1)
                for n, (_, at, width, _) in enumerate(FIELDS):
                    last = dve.tensor_tensor_scan(inclusive[:, at:at + width], ones_step[:, 0:width],
                                                  totals[:, at:at + width], 0.0, ALU.mult, ALU.add)
                last.then_inc(summed_up, 1)
                dve.wait_ge(summed_up, 1)
                dve.tensor_tensor(first_place[:], inclusive[:], totals[:], ALU.subtract).then_inc(places, 1)
                dve.wait_ge(places, 1)
                dve.tensor_scalar(first_place[:, SRC_HI:], first_place[:, SRC_HI:], 1.0, None, ALU.add)
                dve.wait_ge(std_made, 1)
                dve.reciprocal(degree[0:HI_ROWS, :], degree[0:HI_ROWS, :]).then_inc(inverted, 1)

            @block.scalar
            def _(act):
                act.wait_ge(counted, TILES)
                for n in range(2):
                    last = act.activation(degree[0:HI_ROWS, n * 512:(n + 1) * 512], bank[3 + n][0:HI_ROWS, :],
                                          ACT.Sqrt, bias=one_col[0:HI_ROWS, :])
                last.then_inc(std_made, 1)

            @block.tensor
            def _(pe):
                for n in range(5):
                    pe.matmul(bank[n][:], zeros16[:, 0:P], zeros16[:], start=True, stop=True)

                def step(h, par):
                    j = 2 * h + par
                    for t in range(G):
                        side = (G * par + t) % 2
                        wait(pe, onehots, G * j + t + 1)
                        pe.matmul(bank[0][:], ones16[:], onehot[:, side, 0:2 * LO], start=False, stop=True,
                                  skip_group_check=True)
                        pe.matmul(bank[1][:, 0:HI], ones16[:], onehot[:, side, SRC_HI:SRC_HI + HI],
                                  start=False, stop=True, skip_group_check=True)
                        pe.matmul(bank[2][:, 0:HI], ones16[:], onehot[:, side, DST_HI:DST_HI + HI],
                                  start=False, stop=True, skip_group_check=True)
                        for c in range(HI_PARTS):
                            at = DST_HI + c * HI_ROWS
                            mm = pe.matmul(bank[3 + c // 2][0:HI_ROWS, (c % 2) * LO:(c % 2 + 1) * LO],
                                           onehot[:, side, at:at + HI_ROWS], onehot[:, side, DST_LO:DST_LO + LO],
                                           start=False, stop=True, skip_group_check=True)
                        mm.then_inc(counted, 1)
                pairs(pe, NG, step)

        phase(census)

        def make_list(block, sem, q):
            loaded = sem("loaded")
            as_float = sem("as_float")
            flags = sem("flags")
            hidden = sem("hidden")
            ready = sem("ready")
            turned = sem("turned")
            copied = sem("copied")
            key, other = q, 1 - q

            @block.sync
            def _(sp):
                for half in range(2):
                    wait(sp, as_float, half)
                    wait(sp, flags, half)
                    for s in range(3):
                        first = half * HALF * P + s
                        sp.dma_start(prep[:, s], sorted_recs[q][first:first + HALF * P, :]
                                     .rearrange("(t p) c -> t p c", p=P)).then_inc(loaded, 16)

            @block.vector
            def _(dve):
                for half in range(2):
                    dve.wait_ge(loaded, 48 * (half + 1))
                    wait(dve, turned, half)
                    dve.tensor_copy(prep_f[:, 0], prep[:, 1, :, key])
                    dve.tensor_copy(prep_f[:, 1], prep[:, 1, :, other])
                    dve.tensor_copy(prep_f[:, 2].bitcast(I32), prep[:, 1, :, 2])
                    dve.tensor_tensor(prep_f[:, 3], prep[:, 1, :, key], prep[:, 0, :, key], ALU.is_equal)
                    dve.tensor_tensor(prep_f[:, 4], prep[:, 1, :, key], prep[:, 2, :, key], ALU.is_equal)\
                        .then_inc(as_float, 1)
                    dve.wait_ge(as_float, half + 1)
                    dve.tensor_scalar(prep_f[:, 5], prep_f[:, 4], float(FAR), None, ALU.mult)\
                        .then_inc(hidden, 1)
                    dve.wait_ge(hidden, half + 1)
                    dve.tensor_tensor(prep_f[:, 5], prep_f[:, 5], prep_f[:, 0], ALU.add).then_inc(flags, 1)
                    cols = slice(half * HALF, (half + 1) * HALF)
                    dve.wait_ge(turned, half + 1)
                    dve.tensor_copy(list_key[q][:, cols], bank[0][:, 0:HALF])
                    dve.tensor_copy(list_other[q][:, cols], bank[1][:, 0:HALF])
                    if q == 0:
                        dve.tensor_copy(list_w[:, cols], bank[2][:, 0:HALF])
                    dve.tensor_copy(list_keep[q][:, cols], bank[3][:, 0:HALF])
                    dve.tensor_copy(list_write[q][:, cols], bank[4][:, 0:HALF]).then_inc(copied, 1)

            @block.tensor
            def _(pe):
                for half in range(2):
                    pe.wait_ge(flags, half + 1)
                    wait(pe, copied, half)
                    for n, part in enumerate((0, 1, 2, 3, 5)):
                        mm = pe.transpose(bank[n][:, 0:HALF], prep_f[:, part], ident[0:HALF, 0:HALF])
                    mm.then_inc(turned, 1)

        class Norm:
            def __init__(self, sem, name):
                self.stats = sem(f"{name}_stats")
                self.moments = sem(f"{name}_moments")
                self.std = sem(f"{name}_std")
                self.rstd = sem(f"{name}_rstd")
                self.done = sem(f"{name}_done")

        def norm_moments(dve, ln, j, rows):
            for t in range(T):
                last = dve.bn_stats(stats[:, t, :], rows[:, t, :])
            last.then_inc(ln.stats, 1)
            wait(dve, ln.stats, j + 1)
            dve.sem_inc(dve_gate, 1)
            for t in range(T):
                last = dve.bn_aggr(moments[:, t, :], stats[:, t, :])
            last.then_inc(ln.moments, 1)

        def norm_std(act, ln, j):
            wait(act, ln.moments, j + 1)
            act.activation(std[:], moments[:, :, 1], ACT.Sqrt, bias=eps_col[:]).then_inc(ln.std, 1)

        def norm_rows(dve, ln, j, rows, to):
            wait(dve, ln.std, j + 1)
            dve.reciprocal(rstd[:], std[:]).then_inc(ln.rstd, 1)
            wait(dve, ln.rstd, j + 1)
            for t in range(T):
                last = dve.tensor_scalar(to[:, t, :], rows[:, t, :], moments[:, t, 0:1], rstd[:, t:t + 1],
                                         ALU.subtract, ALU.mult)
            last.then_inc(ln.done, 1)

        def sweep_and_sort(block, sem, start, steps, tables, targets, columns, width, shift):
            recs_in = [sem(f"recs_in{i}") for i in range(4)]
            digits_cut = sem("digits_cut")
            digits_ready = sem("digits_ready")
            onehots = sem("onehots")
            prefixed = sem("prefixed")
            passed_on = sem("passed_on")
            ranked = sem("ranked")
            positions = sem("positions")
            placed = [sem(f"placed{i}") for i in range(4)]
            gated = sem("gated")
            per_place = 16 * 2 * SORTED
            loaded = [sem(f"loaded{i}") for i in range(4)]
            stored_uv = [sem(f"stored_uv{i}") for i in range(4)]
            stored_y1 = [sem(f"stored_y1{i}") for i in range(4)]
            turned = sem("turned")
            copied = sem("copied")
            projected = sem("projected")
            with_b0 = sem("with_b0")
            stats0 = sem("stats0")
            moments0 = sem("moments0")
            std0 = sem("std0")
            rstd0 = sem("rstd0")
            squares = sem("squares")
            powers = sem("powers")
            factors = sem("factors")
            uv_made = sem("uv_made")
            base_made = sem("base_made")
            summed = sem("summed")
            stats1 = sem("stats1")
            moments1 = sem("moments1")
            std1 = sem("std1")
            rstd1 = sem("rstd1")
            shift1 = sem("shift1")
            shift2 = sem("shift2")
            y1_made = sem("y1_made")
            @block.sync
            def _(sp):
                def load_recs(h, side):
                    j = 4 * h + side
                    wait(sp, placed[side], per_place * h)
                    for q in range(2):
                        sp.dma_start(recs_x[:, side, q], tables[q][bass.ds(j * SORTED * P, SORTED * P), :]
                                     .rearrange("(t p) c -> p t c", p=P)).then_inc(recs_in[side], 16)

                def load(h, side):
                    j, par = 4 * h + side, side % 2
                    wait(sp, with_b0, j - 3)
                    wait(sp, turned, j - 3)
                    wait(sp, factors, j - 3)
                    sp.dma_start(rows_x[:, side], by_node(x, start + j)).then_inc(loaded[side], 16)
                    sp.dma_start(dinv_x[:, side].rearrange("p (t a) -> p t a", a=1),
                                 by_node(dinv_table[0:N, :], start + j)).then_inc(loaded[side], 16)

                def store_uv(h, side):
                    j, par = 4 * h + side, side % 2
                    wait(sp, uv_made, j + 1)
                    if isinstance(j, int) and start + j == SWEEP - 1:
                        wait(sp, stored_uv[side - 1], 32 * (h + 1))
                    sp.dma_start(by_node(u_table, start + j), out_x[:, side]).then_inc(stored_uv[side], 16)
                    sp.dma_start(by_node(v_table, start + j), out_y[:, side]).then_inc(stored_uv[side], 16)

                def store_y1(h, side):
                    j, par = 4 * h + side, side % 2
                    wait(sp, y1_made, j + 1)
                    if isinstance(j, int) and start + j == SWEEP - 1:
                        wait(sp, stored_y1[side - 1], 16 * (h + 1))
                    sp.dma_start(by_node(y1_table, start + j), out_z[:, side]).then_inc(stored_y1[side], 16)
                staggered(sp, steps, [(0, load), (1, load_recs, SORT_STEPS), (3, store_uv), (6, store_y1)], apart=1)
                for side in range(4):
                    sp.wait_ge(stored_uv[side], 32 * (steps // 4))
                    sp.wait_ge(stored_y1[side], 16 * (steps // 4))

            def ranks(q):
                return bank[4 + q][:, 0:width]

            @block.gpsimd
            def _(pool):
                bound = nc.gpsimd.to_reg(SLOTS + 1)

                def place(h, side):
                    wait(pool, positions, 4 * h + side + 1)
                    pool.sem_inc(gated, 1)
                    for q in range(2):
                        for t in range(SORTED):
                            scatter(targets[q], index_x[:, side, t, q:q + 1], recs_x[:, side, q, t, :],
                                    placed[side], bound)

                def add_b0(h, side):
                    j = 4 * h + side
                    wait(pool, loaded[side], 32 * (h + 1))
                    wait(pool, uv_made, j - 3)
                    wait(pool, base_made, j - 3)
                    wait(pool, factors, j - 3)
                    wait(pool, summed, j - 3)
                    nc.gpsimd.tensor_tensor(with_b0_x[:, side], rows_x[:, side], over_tiles(b0_all[:]), ALU.add)\
                        .then_inc(with_b0, 1)
                    nc.gpsimd.tensor_tensor(factor_x[:, side, 0], dinv_x[:, side], dinv_x[:, side], ALU.mult)\
                        .then_inc(squares, 1)
                    wait(pool, squares, j + 1)
                    nc.gpsimd.tensor_tensor(factor_x[:, side, 1], factor_x[:, side, 0], dinv_x[:, side], ALU.mult)
                    nc.gpsimd.tensor_tensor(factor_x[:, side, 2], factor_x[:, side, 0], factor_x[:, side, 0],
                                            ALU.mult).then_inc(powers, 1)
                staggered(pool, steps, [(0, add_b0), (3, place, SORT_STEPS)])
                for side in range(4):
                    pool.wait_ge(placed[side], per_place * (SORT_STEPS // 4))
                    pool.sem_inc(gated, 1)

            @block.tensor
            def _(pe):
                for q in range(2):
                    pe.matmul(ranks(q), ident[:], first_place[:, columns[q]:columns[q] + width],
                              start=True, stop=True)

                def count_before(h, side, t):
                    for q in range(2):
                        n = 2 * (SORTED * (4 * h + side) + t) + q
                        wait(pe, onehots, n + 1)
                        pe.matmul(ranks(q), before[:], onehot_x[:, side % 2, t, q, 0:width], start=False, stop=True,
                                  skip_group_check=True).then_inc(prefixed, 1)

                def pass_on(h, side, t):
                    for q in range(2):
                        n = 2 * (SORTED * (4 * h + side) + t) + q
                        wait(pe, ranked, n + 1)
                        pe.matmul(ranks(q), not_before[:], onehot_x[:, side % 2, t, q, 0:width], start=False,
                                  stop=True, skip_group_check=True).then_inc(passed_on, 1)

                def rank_first(h, side):
                    count_before(h, side, 0)

                def rank_second(h, side):
                    pass_on(h, side, 0)
                    count_before(h, side, 1)

                def rank_last(h, side):
                    pass_on(h, side, 1)

                def turn(h, side):
                    j, par = 4 * h + side, side % 2
                    wait(pe, loaded[side], 32 * (h + 1))
                    wait(pe, copied, j - 1)
                    for t in range(T):
                        mm = pe.transpose(bank[par][:, t * P:(t + 1) * P], rows_x[:, side, t], ident[:])
                    mm.then_inc(turned, 1)

                def project(h, side):
                    j, par = 4 * h + side, side % 2
                    wait(pe, copied, j + 1)
                    wait(pe, summed, j - 1)
                    for t in range(T):
                        to = bank[2 + par][:, t * D:(t + 1) * D]
                        pe.matmul(to, turned_x[:, par, t * P:(t + 1) * P], w1_c[:], start=True, stop=False)
                        mm = add_bias(pe, to, BIAS_ONE)
                    mm.then_inc(projected, 1)
                staggered(pe, steps, [
                    (2, rank_first, SORT_STEPS), (0, turn), (2, rank_second, SORT_STEPS), (2, project),
                    (2, rank_last, SORT_STEPS)], apart=1)

            @block.vector
            def _(dve):
                def cut_digits(h, side):
                    j = 4 * h + side
                    wait(dve, recs_in[side], 32 * (h + 1))
                    wait(dve, onehots, 2 * SORTED * j)
                    for q in range(2):
                        last = dve.tensor_scalar(digits_i[:, q], recs_x[:, side, q, :, q], shift,
                                                 (LO - 1) if shift == 0 else 0xFFFF,
                                                 ALU.logical_shift_right, ALU.bitwise_and)
                    last.then_inc(digits_cut, 1)

                def round_digits(h, side):
                    j = 4 * h + side
                    wait(dve, digits_cut, j + 1)
                    dve.tensor_copy(digits[:], digits_i[:]).then_inc(digits_ready, 1)

                def make_onehots(h, side):
                    j, par = 4 * h + side, side % 2
                    wait(dve, digits_ready, j + 1)
                    wait(dve, ranked, 2 * SORTED * (j - 1))
                    wait(dve, passed_on, 2 * SORTED * (j - 1))
                    for t in range(SORTED):
                        for q in range(2):
                            dve.tensor_scalar(onehot_x[:, par, t, q, 0:width], count16[:, 0:width],
                                              digits[:, q, t:t + 1], None, ALU.is_equal).then_inc(onehots, 1)

                def rank(h, side, t):
                    par = side % 2
                    for q in range(2):
                        n = 2 * (SORTED * (4 * h + side) + t) + q
                        wait(dve, prefixed, n + 1)
                        wait(dve, ranked, n - 1)
                        if t == 0:
                            wait(dve, positions, 4 * h + side - 1)
                        dve.tensor_tensor_reduce(
                            out=rank_terms[:, q, 0:width], in0=onehot_x[:, par, t, q, 0:width], in1=ranks(q),
                            scale=1.0, scalar=0.0, op0=ALU.mult, op1=ALU.add,
                            accum_out=position_x[:, par, t, q:q + 1]).then_inc(ranked, 1)

                def rank_first(h, side):
                    rank(h, side, 0)

                def rank_second(h, side):
                    rank(h, side, 1)

                def take_places(h, side):
                    j = 4 * h + side
                    wait(dve, ranked, 2 * SORTED * (j + 1))
                    wait(dve, placed[side], per_place * h)
                    dve.tensor_copy(index_x[:, side], position_x[:, side % 2]).then_inc(positions, 1)

                def stats_of_y0(h, side):
                    j = 4 * h + side
                    wait(dve, with_b0, j + 1)
                    wait(dve, moments0, j)
                    for t in range(T):
                        last = dve.bn_stats(stats_x[:, 0, t, :], with_b0_x[:, side, t])
                    last.then_inc(stats0, 1)

                def moments_of_y0(h, side):
                    j, par = 4 * h + side, side % 2
                    wait(dve, stats0, j + 1)
                    dve.sem_inc(dve_gate, 1)
                    for t in range(T):
                        last = dve.bn_aggr(moments_x[:, 0, par, t, :], stats_x[:, 0, t, :])
                    last.then_inc(moments0, 1)

                def root_inverse_0(h, side):
                    j, par = 4 * h + side, side % 2
                    wait(dve, std0, j + 1)
                    dve.reciprocal(rstd_x[:, 0, par], std_x[:, 0, par]).then_inc(rstd0, 1)

                def make_factors(h, side):
                    j, par = 4 * h + side, side % 2
                    wait(dve, rstd0, j + 1)
                    wait(dve, powers, j + 1)
                    dve.tensor_tensor(factor_x[:, side, 3], rstd_x[:, 0, par], dinv_x[:, side], ALU.mult)
                    dve.tensor_tensor(factor_x[:, side, 4], rstd_x[:, 0, par], factor_x[:, side, 1], ALU.mult)
                    dve.tensor_tensor(factor_x[:, side, 5], rstd_x[:, 0, par], factor_x[:, side, 2], ALU.mult)\
                        .then_inc(factors, 1)

                def make_base(h, side):
                    j, par = 4 * h + side, side % 2
                    wait(dve, rstd0, j + 1)
                    wait(dve, summed, j - 3)
                    for t in range(T):
                        last = dve.scalar_tensor_tensor(out=base_x[:, side, t], in0=with_b0_x[:, side, t],
                                                        scalar=rstd_x[:, 0, par, t:t + 1], in1=b1_all[:],
                                                        op0=ALU.mult, op1=ALU.add)
                    last.then_inc(base_made, 1)

                def make_shifts(h, side):
                    j, par = 4 * h + side, side % 2
                    wait(dve, factors, j + 1)
                    wait(dve, uv_made, j - 1)
                    for n in range(2):
                        last = dve.scalar_tensor_tensor(out=shift_x[:, n, par], in0=moments_x[:, 0, par, :, 0],
                                                        scalar=-1.0, in1=factor_x[:, side, 3 + n],
                                                        op0=ALU.mult, op1=ALU.mult)
                    last.then_inc(shift1, 1)

                def sum_up(h, side):
                    j, par = 4 * h + side, side % 2
                    wait(dve, projected, j + 1)
                    wait(dve, base_made, j + 1)
                    wait(dve, y1_made, j - 1)
                    for t in range(T):
                        last = dve.scalar_tensor_tensor(out=pre_x[:, par, t], in0=bank4(2 + par)[:, t],
                                                        scalar=factor_x[:, side, 5, t:t + 1],
                                                        in1=base_x[:, side, t], op0=ALU.mult, op1=ALU.add)
                    last.then_inc(summed, 1)

                def stats_of_y1(h, side):
                    j, par = 4 * h + side, side % 2
                    wait(dve, summed, j + 1)
                    wait(dve, moments1, j)
                    for t in range(T):
                        last = dve.bn_stats(stats_x[:, 1, t, :], pre_x[:, par, t])
                    last.then_inc(stats1, 1)

                def moments_of_y1(h, side):
                    j, par = 4 * h + side, side % 2
                    wait(dve, stats1, j + 1)
                    dve.sem_inc(dve_gate, 1)
                    for t in range(T):
                        last = dve.bn_aggr(moments_x[:, 1, par, t, :], stats_x[:, 1, t, :])
                    last.then_inc(moments1, 1)

                def root_inverse_1(h, side):
                    j, par = 4 * h + side, side % 2
                    wait(dve, std1, j + 1)
                    wait(dve, y1_made, j - 1)
                    dve.reciprocal(rstd_x[:, 1, par], std_x[:, 1, par]).then_inc(rstd1, 1)

                def make_shift_1(h, side):
                    j, par = 4 * h + side, side % 2
                    wait(dve, rstd1, j + 1)
                    dve.scalar_tensor_tensor(out=factor_y[:, par], in0=moments_x[:, 1, par, :, 0],
                                             scalar=-1.0, in1=rstd_x[:, 1, par],
                                             op0=ALU.mult, op1=ALU.mult).then_inc(shift2, 1)
                staggered(dve, steps, [
                    (2, rank_first, SORT_STEPS), (0, stats_of_y0), (3, sum_up), (0, moments_of_y0),
                    (2, rank_second, SORT_STEPS), (3, stats_of_y1), (2, take_places, SORT_STEPS),
                    (1, cut_digits, SORT_STEPS), (0, root_inverse_0), (3, moments_of_y1),
                    (1, round_digits, SORT_STEPS), (0, make_factors), (0, make_base), (0, make_shifts),
                    (3, root_inverse_1), (1, make_onehots, SORT_STEPS), (3, make_shift_1)], apart=1)

            @block.scalar
            def _(act):
                def copy(h, side):
                    j, par = 4 * h + side, side % 2
                    wait(act, turned, j + 1)
                    wait(act, projected, j - 1)
                    act.copy(turned_x[:, par], bank[par][:]).then_inc(copied, 1)

                def root0(h, side):
                    j, par = 4 * h + side, side % 2
                    wait(act, moments0, j + 1)
                    act.activation(std_x[:, 0, par], moments_x[:, 0, par, :, 1], ACT.Sqrt, bias=eps_col[:])\
                        .then_inc(std0, 1)

                def make_uv(h, side):
                    j, par = 4 * h + side, side % 2
                    wait(act, shift1, j + 1)
                    wait(act, stored_uv[side], 32 * h)
                    for t in range(T):
                        act.activation(out_x[:, side, t], with_b0_x[:, side, t], ACT.Identity,
                                       scale=factor_x[:, side, 3, t:t + 1], bias=shift_x[:, 0, par, t:t + 1])
                        last = act.activation(out_y[:, side, t], with_b0_x[:, side, t], ACT.Identity,
                                              scale=factor_x[:, side, 4, t:t + 1], bias=shift_x[:, 1, par, t:t + 1])
                    last.then_inc(uv_made, 1)

                def root1(h, side):
                    j, par = 4 * h + side, side % 2
                    wait(act, moments1, j + 1)
                    act.activation(std_x[:, 1, par], moments_x[:, 1, par, :, 1], ACT.Sqrt, bias=eps_col[:])\
                        .then_inc(std1, 1)

                def make_y1(h, side):
                    j, par = 4 * h + side, side % 2
                    wait(act, shift2, j + 1)
                    wait(act, stored_y1[side], 16 * h)
                    for t in range(T):
                        last = act.activation(out_z[:, side, t], pre_x[:, par, t], ACT.Identity,
                                              scale=rstd_x[:, 1, par, t:t + 1], bias=factor_y[:, par, t:t + 1])
                    last.then_inc(y1_made, 1)
                staggered(act, steps, [(1, make_uv), (0, root0), (1, copy), (4, make_y1), (3, root1)], apart=1)

        HALF_SWEEP = SWEEP // 8 * 4
        phase(sweep_and_sort, 0, HALF_SWEEP, (recs, recs), recs_lo, (SRC_LO, DST_LO), LO, 0)
        phase(sweep_and_sort, HALF_SWEEP, SWEEP - HALF_SWEEP, recs_lo, sorted_recs, (SRC_HI, DST_HI), HI, LO_BITS)
        for q in range(2):
            phase(make_list, q)

        def steps_of(side):
            return (NSTEP - side + 3) // 4

        def pool_steps(pool, sem, sources, target, gathers, scatters, gathered, scattered, per_step,
                       late_scatters=None, late_scattered=None):
            idx_ready = sem("idx_ready")
            idx_w_ready = sem("idx_w_ready")

            def fetch(h, side):
                wait(pool, gathered[side], per_step * h)
                pool.sem_inc(pool_gate, 1)
                for to, lists in sources:
                    last = nc.gpsimd.tensor_copy(to[:, side], lists[:, bass.ds((4 * h + side) * T, T)])
                last.then_inc(idx_ready, 1)

            def fetch_target(h, side):
                wait(pool, scattered[side], 64 * h)
                if late_scatters:
                    wait(pool, late_scattered[side], 128 * h)
                pool.sem_inc(pool_gate, 1)
                nc.gpsimd.tensor_copy(idx_w[:, side], target[:, bass.ds((4 * h + side) * T, T)])\
                    .then_inc(idx_w_ready, 1)

            def gather_step(h, side):
                wait(pool, idx_ready, 4 * h + side + 1)
                gathers(h, side)

            def scatter_step(h, side):
                wait(pool, idx_w_ready, 4 * h + side + 1)
                scatters(h, side)
            stages = [(0, fetch), (3, fetch_target), (1, gather_step), (4, scatter_step)]
            if late_scatters:
                stages.append((6, late_scatters))
            staggered(pool, NSTEP, stages)
            for side in range(4):
                pool.wait_ge(scattered[side], 64 * steps_of(side))
                if late_scatters:
                    pool.wait_ge(late_scattered[side], 128 * steps_of(side))
                pool.sem_inc(pool_gate, 1)

        def keep_to_row_pe(pe, j, keep_in, keep_turned, keep_copied, to=0):
            wait(pe, keep_in, j + 1)
            wait(pe, keep_copied, j)
            for t in range(T):
                mm = pe.transpose(bank[to][:, t * P:(t + 1) * P], keep_cols[:, t:t + 1].broadcast_to([P, P]), ident[:])
            mm.then_inc(keep_turned, 1)

        def keep_to_cols_dve(dve, j, q, keep_in, keep_turned):
            wait(dve, keep_turned, j)
            dve.sem_inc(dve_gate, 1)
            dve.tensor_copy(keep_cols[:], list_keep[q][:, bass.ds(j * T, T)]).then_inc(keep_in, 1)

        def sweep_two(sem, start, steps):
            loaded = [sem(f"loaded{i}") for i in range(4)]
            stored_y2 = [sem(f"stored_y2{i}") for i in range(4)]
            stored_y3 = [sem(f"stored_y3{i}") for i in range(4)]
            turned = sem("turned")
            copied = sem("copied")
            projected = sem("projected")
            stats2 = sem("stats2")
            moments2 = sem("moments2")
            std2 = sem("std2")
            rstd2 = sem("rstd2")
            shift2 = sem("shift2")
            y2_made = sem("y2_made")
            scaled = sem("scaled")
            summed = sem("summed")
            stats3 = sem("stats3")
            moments3 = sem("moments3")
            std3 = sem("std3")
            rstd3 = sem("rstd3")
            shift3 = sem("shift3")
            y3_made = sem("y3_made")

            def before_norm(side):
                return bank4(3 + side % 2)

            def through_r(par):
                return bank4(1 + par)

            def on_sync(sp):
                def load(h, side):
                    j, par = 4 * h + side, side % 2
                    wait(sp, turned, j - 3)
                    sp.dma_start(rows_x[:, side], by_node(y1_table, start + j)).then_inc(loaded[side], 16)

                def store_y2(h, side):
                    j, par = 4 * h + side, side % 2
                    wait(sp, y2_made, j + 1)
                    if isinstance(j, int) and start + j == SWEEP - 1:
                        wait(sp, stored_y2[side - 1], 16 * (h + 1))
                    sp.dma_start(by_node(y2_table, start + j), out_x[:, side]).then_inc(stored_y2[side], 16)

                def store_y3(h, side):
                    j, par = 4 * h + side, side % 2
                    wait(sp, y3_made, j + 1)
                    if isinstance(j, int) and start + j == SWEEP - 1:
                        wait(sp, stored_y3[side - 1], 16 * (h + 1))
                    sp.dma_start(by_node(out, start + j), out_y[:, side]).then_inc(stored_y3[side], 16)
                return [(0, load), (5, store_y2), (7, store_y3)], steps

            def all_stored(sp):
                for side in range(4):
                    sp.wait_ge(stored_y2[side], 16 * (steps // 4))
                    sp.wait_ge(stored_y3[side], 16 * (steps // 4))

            def on_tensor(pe):
                def turn(h, side):
                    j, par = 4 * h + side, side % 2
                    wait(pe, loaded[side], 16 * (h + 1))
                    wait(pe, copied, j)
                    for t in range(T):
                        mm = pe.transpose(bank[0][:, t * P:(t + 1) * P], rows_x[:, side, t], ident[:])
                    mm.then_inc(turned, 1)

                def project(h, side):
                    j, par = 4 * h + side, side % 2
                    wait(pe, copied, j + 1)
                    wait(pe, y2_made, j - 1)
                    wait(pe, scaled, j - 1)
                    for n, to in enumerate((before_norm(side), through_r(par))):
                        pe.matmul(to, ones3[:], over_tiles(bias3[:, BIAS_TWO + n * D:BIAS_TWO + (n + 1) * D]),
                                  start=True, stop=True)
                        for t in range(T):
                            mm = pe.matmul(to[:, t], turned_x[:, par, t * P:(t + 1) * P],
                                           w_two[:, n * D:(n + 1) * D], start=False, stop=True,
                                           skip_group_check=True)
                    mm.then_inc(projected, 1)
                return [(2, project), (0, turn)], steps

            def on_vector(dve):
                def stats_of_y2(h, side):
                    j = 4 * h + side
                    wait(dve, projected, j + 1)
                    wait(dve, moments2, j)
                    for t in range(T):
                        last = dve.bn_stats(stats_x[:, 0, t, :], before_norm(side)[:, t])
                    last.then_inc(stats2, 1)

                def moments_of_y2(h, side):
                    j, par = 4 * h + side, side % 2
                    wait(dve, stats2, j + 1)
                    dve.sem_inc(dve_gate, 1)
                    for t in range(T):
                        last = dve.bn_aggr(moments_x[:, 0, par, t, :], stats_x[:, 0, t, :])
                    last.then_inc(moments2, 1)

                def root_inverse_2(h, side):
                    j, par = 4 * h + side, side % 2
                    wait(dve, std2, j + 1)
                    wait(dve, y2_made, j - 1)
                    dve.reciprocal(rstd_x[:, 0, par], std_x[:, 0, par]).then_inc(rstd2, 1)

                def make_base(h, side):
                    j, par = 4 * h + side, side % 2
                    wait(dve, rstd2, j + 1)
                    wait(dve, summed, j - 3)
                    for t in range(T):
                        last = dve.scalar_tensor_tensor(out=base_x[:, side, t], in0=through_r(par)[:, t],
                                                        scalar=rstd_x[:, 0, par, t:t + 1], in1=b3_all[:],
                                                        op0=ALU.mult, op1=ALU.add)
                    last.then_inc(scaled, 1)

                def make_shift_2(h, side):
                    j, par = 4 * h + side, side % 2
                    wait(dve, rstd2, j + 1)
                    dve.scalar_tensor_tensor(out=shift_x[:, 0, par], in0=moments_x[:, 0, par, :, 0], scalar=-1.0,
                                             in1=rstd_x[:, 0, par], op0=ALU.mult, op1=ALU.mult).then_inc(shift2, 1)

                def sum_up(h, side):
                    j, par = 4 * h + side, side % 2
                    wait(dve, scaled, j + 1)
                    wait(dve, y2_made, j + 1)
                    wait(dve, y3_made, j - 1)
                    dve.scalar_tensor_tensor(out=pre_x[:, par], in0=base_x[:, side], scalar=0.0, in1=out_x[:, side],
                                             op0=ALU.max, op1=ALU.add).then_inc(summed, 1)

                def stats_of_y3(h, side):
                    j, par = 4 * h + side, side % 2
                    wait(dve, summed, j + 1)
                    wait(dve, moments3, j)
                    for t in range(T):
                        last = dve.bn_stats(stats_x[:, 1, t, :], pre_x[:, par, t])
                    last.then_inc(stats3, 1)

                def moments_of_y3(h, side):
                    j, par = 4 * h + side, side % 2
                    wait(dve, stats3, j + 1)
                    dve.sem_inc(dve_gate, 1)
                    for t in range(T):
                        last = dve.bn_aggr(moments_x[:, 1, par, t, :], stats_x[:, 1, t, :])
                    last.then_inc(moments3, 1)

                def root_inverse_3(h, side):
                    j, par = 4 * h + side, side % 2
                    wait(dve, std3, j + 1)
                    wait(dve, y3_made, j - 1)
                    dve.reciprocal(rstd_x[:, 1, par], std_x[:, 1, par]).then_inc(rstd3, 1)

                def make_shift_3(h, side):
                    j, par = 4 * h + side, side % 2
                    wait(dve, rstd3, j + 1)
                    dve.scalar_tensor_tensor(out=shift_x[:, 1, par], in0=moments_x[:, 1, par, :, 0], scalar=-1.0,
                                             in1=rstd_x[:, 1, par], op0=ALU.mult, op1=ALU.mult).then_inc(shift3, 1)
                return [(3, stats_of_y2), (5, sum_up), (3, moments_of_y2), (5, stats_of_y3), (3, root_inverse_2),
                        (5, moments_of_y3), (3, make_shift_2), (3, make_base), (5, root_inverse_3),
                        (5, make_shift_3)], steps

            def on_scalar(act):
                def copy(h, side):
                    j, par = 4 * h + side, side % 2
                    wait(act, turned, j + 1)
                    wait(act, projected, j - 1)
                    act.copy(turned_x[:, par], bank[0][:]).then_inc(copied, 1)

                def root2(h, side):
                    j, par = 4 * h + side, side % 2
                    wait(act, moments2, j + 1)
                    act.activation(std_x[:, 0, par], moments_x[:, 0, par, :, 1], ACT.Sqrt, bias=eps_col[:])\
                        .then_inc(std2, 1)

                def make_y2(h, side):
                    j, par = 4 * h + side, side % 2
                    wait(act, shift2, j + 1)
                    wait(act, stored_y2[side], 16 * h)
                    wait(act, summed, j - 3)
                    for t in range(T):
                        last = act.activation(out_x[:, side, t], before_norm(side)[:, t], ACT.Identity,
                                              scale=rstd_x[:, 0, par, t:t + 1], bias=shift_x[:, 0, par, t:t + 1])
                    last.then_inc(y2_made, 1)

                def root3(h, side):
                    j, par = 4 * h + side, side % 2
                    wait(act, moments3, j + 1)
                    act.activation(std_x[:, 1, par], moments_x[:, 1, par, :, 1], ACT.Sqrt, bias=eps_col[:])\
                        .then_inc(std3, 1)

                def make_y3(h, side):
                    j, par = 4 * h + side, side % 2
                    wait(act, shift3, j + 1)
                    wait(act, stored_y3[side], 16 * h)
                    for t in range(T):
                        last = act.activation(out_y[:, side, t], pre_x[:, par, t], ACT.Identity,
                                              scale=rstd_x[:, 1, par, t:t + 1], bias=shift_x[:, 1, par, t:t + 1])
                    last.then_inc(y3_made, 1)
                return [(4, make_y2), (3, root2), (1, copy), (6, make_y3), (5, root3)], steps
            return on_sync, all_stored, on_tensor, on_vector, on_scalar

        BESIDE_L0 = 3 * NSTEP // 4 * 4

        def layer_0(block, sem):
            gathered = [sem(f"gathered{i}") for i in range(4)]
            scattered = [sem(f"scattered{i}") for i in range(4)]
            stored = [sem(f"stored{i}") for i in range(4)]
            keep_in = sem("keep_in")
            keep_turned = sem("keep_turned")
            keep_copied = sem("keep_copied")
            weighted = sem("weighted")
            turned = sem("turned")
            scanned = sem("scanned")
            projected = sem("projected")
            summed = sem("summed")
            dinv_kept = sem("dinv_kept")
            scaled = sem("scaled")
            ln = Norm(sem, "y0")

            on_sync, all_stored, on_tensor, on_vector, on_scalar = sweep_two(sem, 0, BESIDE_L0)

            @block.gpsimd
            def _(pool):
                bound = nc.gpsimd.to_reg(N - 1)

                def gathers(h, side):
                    j, par = 4 * h + side, side % 2
                    wait(pool, turned, j - 3)
                    wait(pool, summed, j - 3)
                    wait(pool, dinv_kept, j - 3)
                    wait(pool, scaled, j - 3)
                    pool.sem_inc(pool_gate, 1)
                    for t in range(T):
                        gather(own_x[:, side, t * D:(t + 1) * D], x, idx_a[:, side, t:t + 1], gathered[side], bound)
                    for t in range(T):
                        gather(with_b0_x[:, side, t], x, idx_b[:, side, t:t + 1], gathered[side], bound)
                    for t in range(T):
                        gather(dinv_x[:, side, t:t + 1], dinv_table, idx_b[:, side, t:t + 1], gathered[side], bound)

                def scatters(h, side):
                    wait(pool, scaled, 4 * h + side + 1)
                    pool.sem_inc(pool_gate, 1)
                    for t in range(T):
                        scatter(u_table, idx_w[:, side, t:t + 1], u_x[:, side, t], scattered[side], bound)
                pool_steps(pool, sem, ((idx_a, list_other[0]), (idx_b, list_key[0])), list_write[0],
                           gathers, scatters, gathered, scattered, 192)

            @block.sync
            def _(sp):
                def store(h, side):
                    j, par = 4 * h + side, side % 2
                    wait(sp, scaled, j + 1)
                    sp.dma_start(by_slot(y0_slots, j), out_z[:, side]).then_inc(stored[side], 16)
                    sp.dma_start(by_slot(u_slots, j), u_x[:, side]).then_inc(stored[side], 16)
                staggered(sp, NSTEP, [0, 1, (2, store), 2], beside=(*on_sync(sp), 3))
                all_stored(sp)
                for side in range(4):
                    sp.wait_ge(stored[side], 32 * steps_of(side))

            @block.vector
            def _(dve):
                def weight(h, side):
                    j = 4 * h + side
                    keep_to_cols_dve(dve, j, 0, keep_in, keep_turned)
                    wait(dve, gathered[side], 192 * (h + 1))
                    dve.sem_inc(dve_gate, 1)
                    for t in range(T):
                        last = dve.tensor_scalar(own_x[:, side, t * D:(t + 1) * D], own_x[:, side, t * D:(t + 1) * D],
                                                 list_w[:, bass.ds(j * T + t, 1)], None, ALU.mult)
                    last.then_inc(weighted, 1)
                    dve.tensor_copy(dinv_own[:, bass.ds(j * T, T)], dinv_x[:, side]).then_inc(dinv_kept, 1)

                def scan(h, side):
                    j, par = 4 * h + side, side % 2
                    wait(dve, turned, j + 1)
                    wait(dve, keep_copied, j + 1)
                    wait(dve, scanned, j)
                    wait(dve, projected, j - 1)
                    dve.tensor_tensor_scan(agg[:, par], keep_row[:, par], bank[6][:],
                                           agg[:, 1 - par, STEP - 1:STEP], ALU.mult, ALU.add).then_inc(scanned, 1)

                def add_own(h, side):
                    j = 4 * h + side
                    wait(dve, projected, j + 1)
                    wait(dve, ln.done, j)
                    dve.tensor_tensor(pre[:], bank4(7), with_b0_x[:, side], ALU.add).then_inc(summed, 1)

                def finish(h, side):
                    j = 4 * h + side
                    wait(dve, summed, j + 1)
                    norm_moments(dve, ln, j, pre)
                    wait(dve, stored[side], 32 * h)
                    norm_rows(dve, ln, j, pre, out_z[:, side])
                staggered(dve, NSTEP, [(0, weight), (1, add_own), 0, (0, scan), 1, 2, (1, finish)],
                          beside=(*on_vector(dve), 3))

            @block.scalar
            def _(act):
                def scan(h, side):
                    j, par = 4 * h + side, side % 2
                    wait(act, keep_turned, j + 1)
                    wait(act, scanned, j - 1)
                    act.copy(keep_row[:, par], bank[5][:]).then_inc(keep_copied, 1)

                def finish(h, side):
                    j, par = 4 * h + side, side % 2
                    norm_std(act, ln, j)
                    wait(act, stored[side], 32 * h)
                    wait(act, scattered[side], 64 * h)
                    wait(act, gathered[side], 192 * (h + 1))
                    wait(act, ln.done, j + 1)
                    for t in range(T):
                        last = act.activation(u_x[:, side, t], out_z[:, side, t], ACT.Copy,
                                              scale=dinv_x[:, side, t:t + 1])
                    last.then_inc(scaled, 1)
                staggered(act, NSTEP, [(0, scan), 0, 1, 2, (1, finish)], beside=(*on_scalar(act), 3))

            @block.tensor
            def _(pe):
                def turn_rows(h, side):
                    j = 4 * h + side
                    keep_to_row_pe(pe, j, keep_in, keep_turned, keep_copied, 5)
                    wait(pe, weighted, j + 1)
                    wait(pe, scanned, j)
                    for t in range(T):
                        mm = pe.transpose(bank[6][:, t * P:(t + 1) * P], own_x[:, side, t * D:(t + 1) * D], ident[:])
                    mm.then_inc(turned, 1)

                def project(h, side):
                    j, par = 4 * h + side, side % 2
                    wait(pe, scanned, j + 1)
                    wait(pe, summed, j)
                    for t in range(T):
                        to = bank[7][:, t * D:(t + 1) * D]
                        pe.matmul(to, agg[:, par, t * P:(t + 1) * P], w0_sb[:], start=True, stop=False)
                        mm = add_bias(pe, to, BIAS_B0)
                    mm.then_inc(projected, 1)
                staggered(pe, NSTEP, [(0, turn_rows), 0, 1, (0, project), 2], beside=(*on_tensor(pe), 3))

        phase(layer_0)

        def hop_1(block, sem):
            gathered = [sem(f"gathered{i}") for i in range(4)]
            scattered = [sem(f"scattered{i}") for i in range(4)]
            stored = [sem(f"stored{i}") for i in range(4)]
            loaded = [sem(f"loaded{i}") for i in range(4)]
            keep_in = sem("keep_in")
            keep_turned = sem("keep_turned")
            keep_copied = sem("keep_copied")
            turned = sem("turned")
            scanned = sem("scanned")
            returned = sem("returned")
            summed = sem("summed")
            inv_deg = sem("inv_deg")
            hopped = sem("hopped")

            on_sync, all_stored, on_tensor, on_vector, on_scalar = sweep_two(sem, BESIDE_L0, SWEEP - BESIDE_L0)

            @block.gpsimd
            def _(pool):
                bound = nc.gpsimd.to_reg(N - 1)

                def gathers(h, side):
                    wait(pool, turned, 4 * h + side - 3)
                    pool.sem_inc(pool_gate, 1)
                    for t in range(T):
                        gather(own_x[:, side, t * D:(t + 1) * D], u_table, idx_a[:, side, t:t + 1], gathered[side], bound)

                def scatters(h, side):
                    wait(pool, hopped, 4 * h + side + 1)
                    pool.sem_inc(pool_gate, 1)
                    for t in range(T):
                        scatter(v_table, idx_w[:, side, t:t + 1], out_z[:, side, t], scattered[side], bound)
                pool_steps(pool, sem, ((idx_a, list_other[0]),), list_write[0],
                           gathers, scatters, gathered, scattered, 64)

            @block.sync
            def _(sp):
                def load(h, side):
                    j, par = 4 * h + side, side % 2
                    wait(sp, summed, j - 3)
                    sp.dma_start(with_b0_x[:, side], by_slot(u_slots, j)).then_inc(loaded[side], 16)

                def store(h, side):
                    j, par = 4 * h + side, side % 2
                    wait(sp, hopped, j + 1)
                    sp.dma_start(by_slot(v_slots, j), out_z[:, side]).then_inc(stored[side], 16)
                staggered(sp, NSTEP, [(0, load), 0, (2, store)], apart=1, beside=(*on_sync(sp), 1))
                all_stored(sp)
                for side in range(4):
                    sp.wait_ge(stored[side], 16 * steps_of(side))

            @block.vector
            def _(dve):
                dve.tensor_tensor(dinv2_own[:], dinv_own[:], dinv_own[:], ALU.mult).then_inc(inv_deg, 1)
                dve.wait_ge(inv_deg, 1)

                def scan(h, side):
                    j, par = 4 * h + side, side % 2
                    keep_to_cols_dve(dve, j, 0, keep_in, keep_turned)
                    wait(dve, turned, j + 1)
                    wait(dve, keep_copied, j + 1)
                    wait(dve, scanned, j)
                    wait(dve, returned, j - 1)
                    dve.tensor_tensor_scan(agg[:, par], keep_row[:, par], bank[6][:],
                                           agg[:, 1 - par, STEP - 1:STEP], ALU.mult, ALU.add).then_inc(scanned, 1)

                def finish(h, side):
                    j, par = 4 * h + side, side % 2
                    wait(dve, returned, j + 1)
                    wait(dve, loaded[side], 16 * (h + 1))
                    wait(dve, hopped, j)
                    dve.tensor_tensor(pre[:], bank4(7), with_b0_x[:, side], ALU.add).then_inc(summed, 1)
                staggered(dve, NSTEP, [(0, scan), 0, (1, finish)], apart=1, beside=(*on_vector(dve), 1))

            @block.scalar
            def _(act):
                act.wait_ge(inv_deg, 1)

                def scan(h, side):
                    j, par = 4 * h + side, side % 2
                    wait(act, keep_turned, j + 1)
                    wait(act, scanned, j - 1)
                    act.copy(keep_row[:, par], bank[5][:]).then_inc(keep_copied, 1)

                def finish(h, side):
                    j, par = 4 * h + side, side % 2
                    wait(act, stored[side], 16 * h)
                    wait(act, scattered[side], 64 * h)
                    wait(act, summed, j + 1)
                    act.sem_inc(act_gate, 1)
                    for t in range(T):
                        last = act.activation(out_z[:, side, t], pre[:, t], ACT.Copy,
                                              scale=dinv2_own[:, bass.ds(j * T + t, 1)])
                    last.then_inc(hopped, 1)
                staggered(act, NSTEP, [(0, scan), 0, (1, finish)], apart=1, beside=(*on_scalar(act), 1))

            @block.tensor
            def _(pe):
                def turn_rows(h, side):
                    j = 4 * h + side
                    keep_to_row_pe(pe, j, keep_in, keep_turned, keep_copied, 5)
                    wait(pe, gathered[side], 64 * (h + 1))
                    wait(pe, scanned, j)
                    for t in range(T):
                        mm = pe.transpose(bank[6][:, t * P:(t + 1) * P], own_x[:, side, t * D:(t + 1) * D], ident[:])
                    mm.then_inc(turned, 1)

                def turn_back(h, side):
                    j, par = 4 * h + side, side % 2
                    wait(pe, scanned, j + 1)
                    wait(pe, summed, j)
                    for t in range(T):
                        mm = pe.transpose(bank[7][:, t * D:(t + 1) * D], agg[:, par, t * P:(t + 1) * P], ident[:])
                    mm.then_inc(returned, 1)
                staggered(pe, NSTEP, [(0, turn_rows), 0, (0, turn_back)], apart=1, beside=(*on_tensor(pe), 1))

        phase(hop_1)

        def hop_2(block, sem):
            gathered = [sem(f"gathered{i}") for i in range(4)]
            scattered = [sem(f"scattered{i}") for i in range(4)]
            loaded = [sem(f"loaded{i}") for i in range(4)]
            keep_in = sem("keep_in")
            keep_turned = sem("keep_turned")
            keep_copied = sem("keep_copied")
            turned = sem("turned")
            scanned = sem("scanned")
            own_turned = sem("own_turned")
            joined = sem("joined")
            projected = sem("projected")
            with_b1 = sem("with_b1")
            summed = sem("summed")
            ln = Norm(sem, "y1")
            late_scattered = [sem(f"late_scattered{i}") for i in range(4)]
            y1_turned = sem("y1_turned")
            y1_copied = sem("y1_copied")
            onwards = sem("onwards")
            ln2 = Norm(sem, "y2")
            shift2 = sem("shift2")
            based = sem("based")
            y3_summed = sem("y3_summed")
            ln3 = Norm(sem, "y3")
            shift3 = sem("shift3")
            y3_base, y3_pre = low_row, high_row
            y3_rows = with_b0_x

            @block.gpsimd
            def _(pool):
                bound = nc.gpsimd.to_reg(N - 1)

                def gathers(h, side):
                    wait(pool, turned, 4 * h + side - 3)
                    pool.sem_inc(pool_gate, 1)
                    for t in range(T):
                        gather(rows_x[:, side, t], v_table, idx_a[:, side, t:t + 1], gathered[side], bound)

                def scatters(h, side):
                    wait(pool, ln.done, 4 * h + side + 1)
                    pool.sem_inc(pool_gate, 1)
                    for t in range(T):
                        scatter(y1_table, idx_w[:, side, t:t + 1], out_x[:, side, t], scattered[side], bound)

                def late_scatters(h, side):
                    wait(pool, ln2.done, 4 * h + side + 1)
                    wait(pool, ln3.done, 4 * h + side + 1)
                    pool.sem_inc(pool_gate, 1)
                    for t in range(T):
                        scatter(y2_table, idx_w[:, side, t:t + 1], out_y[:, side, t], late_scattered[side], bound)
                    for t in range(T):
                        scatter(out, idx_w[:, side, t:t + 1], y3_rows[:, side, t], late_scattered[side], bound)
                pool_steps(pool, sem, ((idx_a, list_other[0]),), list_write[0],
                           gathers, scatters, gathered, scattered, 64, late_scatters, late_scattered)

            @block.sync
            def _(sp):
                def load(h, side):
                    j, par = 4 * h + side, side % 2
                    wait(sp, own_turned, j - 3)
                    wait(sp, with_b1, j - 3)
                    sp.dma_start(base_x[:, side], by_slot(v_slots, j)).then_inc(loaded[side], 16)
                    sp.dma_start(out_z[:, side], by_slot(y0_slots, j)).then_inc(loaded[side], 16)
                staggered(sp, NSTEP, [(0, load)])

            @block.vector
            def _(dve):
                def scan(h, side):
                    j, par = 4 * h + side, side % 2
                    keep_to_cols_dve(dve, j, 0, keep_in, keep_turned)
                    wait(dve, loaded[side], 32 * (h + 1))
                    wait(dve, ln.done, j - 1)
                    dve.tensor_tensor(pre_x[:, par], out_z[:, side], over_tiles(b1_all[:]), ALU.add).then_inc(with_b1, 1)
                    wait(dve, turned, j + 1)
                    wait(dve, keep_copied, j + 1)
                    wait(dve, scanned, j)
                    wait(dve, joined, j)
                    dve.tensor_tensor_scan(agg[:, par], keep_row[:, par], bank[1][:],
                                           agg[:, 1 - par, STEP - 1:STEP], ALU.mult, ALU.add).then_inc(scanned, 1)
                    wait(dve, scanned, j + 1)
                    wait(dve, own_turned, j + 1)
                    wait(dve, projected, j - 1)
                    dve.tensor_tensor(turned_x[:, par], bank[3][:], agg[:, par], ALU.add).then_inc(joined, 1)

                def finish(h, side):
                    j, par = 4 * h + side, side % 2
                    wait(dve, projected, j + 1)
                    wait(dve, with_b1, j + 1)
                    dve.sem_inc(dve_gate, 1)
                    for t in range(T):
                        last = dve.scalar_tensor_tensor(out=pre_x[:, par, t], in0=bank4(2)[:, t],
                                                        scalar=dinv_own[:, bass.ds(j * T + t, 1)], in1=pre_x[:, par, t],
                                                        op0=ALU.mult, op1=ALU.add)
                    last.then_inc(summed, 1)
                    wait(dve, summed, j + 1)
                    norm_moments(dve, ln, j, pre_x[:, par])
                    wait(dve, scattered[side], 64 * h)
                    wait(dve, y1_turned, j - 3)
                    norm_rows(dve, ln, j, pre_x[:, par], out_x[:, side])

                def norm_y2(h, side):
                    j, par = 4 * h + side, side % 2
                    wait(dve, onwards, j + 1)
                    for t in range(T):
                        last = dve.bn_stats(stats_x[:, 0, t, :], bank4(5)[:, t])
                    last.then_inc(ln2.stats, 1)
                    wait(dve, ln2.stats, j + 1)
                    dve.sem_inc(dve_gate, 1)
                    for t in range(T):
                        last = dve.bn_aggr(moments_x[:, 0, par, t, :], stats_x[:, 0, t, :])
                    last.then_inc(ln2.moments, 1)
                    wait(dve, ln2.std, j + 1)
                    dve.reciprocal(rstd_x[:, 0, par], std_x[:, 0, par]).then_inc(ln2.rstd, 1)
                    wait(dve, ln2.rstd, j + 1)
                    dve.scalar_tensor_tensor(out=shift_x[:, 0, par], in0=moments_x[:, 0, par, :, 0], scalar=-1.0,
                                             in1=rstd_x[:, 0, par], op0=ALU.mult, op1=ALU.mult).then_inc(shift2, 1)
                    wait(dve, y3_summed, j - 1)
                    for t in range(T):
                        last = dve.scalar_tensor_tensor(out=tiles(y3_base[:, par])[:, t], in0=bank4(6)[:, t],
                                                        scalar=rstd_x[:, 0, par, t:t + 1], in1=b3_all[:],
                                                        op0=ALU.mult, op1=ALU.add)
                    last.then_inc(based, 1)

                def norm_y3(h, side):
                    j, par = 4 * h + side, side % 2
                    wait(dve, based, j + 1)
                    wait(dve, ln2.done, j + 1)
                    wait(dve, ln3.done, j - 1)
                    dve.scalar_tensor_tensor(out=tiles(y3_pre[:, par]), in0=tiles(y3_base[:, par]), scalar=0.0,
                                             in1=out_y[:, side], op0=ALU.max, op1=ALU.add).then_inc(y3_summed, 1)
                    wait(dve, y3_summed, j + 1)
                    for t in range(T):
                        last = dve.bn_stats(stats_x[:, 1, t, :], tiles(y3_pre[:, par])[:, t])
                    last.then_inc(ln3.stats, 1)
                    wait(dve, ln3.stats, j + 1)
                    dve.sem_inc(dve_gate, 1)
                    for t in range(T):
                        last = dve.bn_aggr(moments_x[:, 1, par, t, :], stats_x[:, 1, t, :])
                    last.then_inc(ln3.moments, 1)
                    wait(dve, ln3.std, j + 1)
                    dve.reciprocal(rstd_x[:, 1, par], std_x[:, 1, par]).then_inc(ln3.rstd, 1)
                    wait(dve, ln3.rstd, j + 1)
                    dve.scalar_tensor_tensor(out=shift_x[:, 1, par], in0=moments_x[:, 1, par, :, 0], scalar=-1.0,
                                             in1=rstd_x[:, 1, par], op0=ALU.mult, op1=ALU.mult).then_inc(shift3, 1)
                staggered(dve, NSTEP, [(0, scan), (2, norm_y2), (1, finish), (3, norm_y3)])

            @block.scalar
            def _(act):
                def scan(h, side):
                    j, par = 4 * h + side, side % 2
                    wait(act, keep_turned, j + 1)
                    wait(act, scanned, j - 1)
                    act.copy(keep_row[:, par], bank[0][:]).then_inc(keep_copied, 1)

                def finish(h, side):
                    j, par = 4 * h + side, side % 2
                    norm_std(act, ln, j)

                def copy_y1(h, side):
                    j, par = 4 * h + side, side % 2
                    wait(act, y1_turned, j + 1)
                    wait(act, onwards, j - 3)
                    act.copy(own_x[:, side], bank[4][:]).then_inc(y1_copied, 1)

                def make_y2(h, side):
                    j, par = 4 * h + side, side % 2
                    wait(act, ln2.moments, j + 1)
                    act.activation(std_x[:, 0, par], moments_x[:, 0, par, :, 1], ACT.Sqrt, bias=eps_col[:])\
                        .then_inc(ln2.std, 1)
                    wait(act, shift2, j + 1)
                    wait(act, late_scattered[side], 128 * h)
                    wait(act, y3_summed, j - 3)
                    for t in range(T):
                        last = act.activation(out_y[:, side, t], bank4(5)[:, t], ACT.Identity,
                                              scale=rstd_x[:, 0, par, t:t + 1], bias=shift_x[:, 0, par, t:t + 1])
                    last.then_inc(ln2.done, 1)

                def make_y3(h, side):
                    j, par = 4 * h + side, side % 2
                    wait(act, ln3.moments, j + 1)
                    act.activation(std_x[:, 1, par], moments_x[:, 1, par, :, 1], ACT.Sqrt, bias=eps_col[:])\
                        .then_inc(ln3.std, 1)
                    wait(act, shift3, j + 1)
                    wait(act, late_scattered[side], 128 * h)
                    for t in range(T):
                        last = act.activation(y3_rows[:, side, t], tiles(y3_pre[:, par])[:, t], ACT.Identity,
                                              scale=rstd_x[:, 1, par, t:t + 1], bias=shift_x[:, 1, par, t:t + 1])
                    last.then_inc(ln3.done, 1)
                staggered(act, NSTEP, [(0, scan), (2, make_y2), (1, finish), (1, copy_y1), (3, make_y3)])

            @block.tensor
            def _(pe):
                def scan(h, side):
                    j, par = 4 * h + side, side % 2
                    keep_to_row_pe(pe, j, keep_in, keep_turned, keep_copied)
                    wait(pe, loaded[side], 32 * (h + 1))
                    wait(pe, joined, j)
                    for t in range(T):
                        mm = pe.transpose(bank[3][:, t * P:(t + 1) * P], base_x[:, side, t], ident[:])
                    mm.then_inc(own_turned, 1)
                    wait(pe, gathered[side], 64 * (h + 1))
                    wait(pe, scanned, j)
                    for t in range(T):
                        mm = pe.transpose(bank[1][:, t * P:(t + 1) * P], rows_x[:, side, t], ident[:])
                    mm.then_inc(turned, 1)
                    wait(pe, joined, j + 1)
                    wait(pe, summed, j)
                    for t in range(T):
                        mm = pe.matmul(bank[2][:, t * D:(t + 1) * D], turned_x[:, par, t * P:(t + 1) * P], w1_t[:],
                                       start=True, stop=True)
                    mm.then_inc(projected, 1)

                def turn_y1(h, side):
                    j = 4 * h + side
                    wait(pe, ln.done, j + 1)
                    wait(pe, y1_copied, j)
                    for t in range(T):
                        mm = pe.transpose(bank[4][:, t * P:(t + 1) * P], out_x[:, side, t], ident[:])
                    mm.then_inc(y1_turned, 1)

                def project_on(h, side):
                    j = 4 * h + side
                    wait(pe, y1_copied, j + 1)
                    wait(pe, ln2.done, j)
                    wait(pe, based, j)
                    for n, to in enumerate((bank4(5), bank4(6))):
                        pe.matmul(to, ones3[:], over_tiles(bias3[:, BIAS_TWO + n * D:BIAS_TWO + (n + 1) * D]),
                                  start=True, stop=True)
                        for t in range(T):
                            mm = pe.matmul(to[:, t], own_x[:, side, t * P:(t + 1) * P],
                                           w_two[:, n * D:(n + 1) * D], start=False, stop=True,
                                           skip_group_check=True)
                    mm.then_inc(onwards, 1)
                staggered(pe, NSTEP, [(2, project_on), (0, scan), (1, turn_y1)])

        phase(hop_2)

        def layer_2(block, sem):
            gathered = [sem(f"gathered{i}") for i in range(4)]
            scattered = [sem(f"scattered{i}") for i in range(4)]
            stored = [sem(f"stored{i}") for i in range(4)]
            keep_in = sem("keep_in")
            keep_turned = sem("keep_turned")
            keep_copied = sem("keep_copied")
            turned_own = sem("turned_own")
            turned_src = sem("turned_src")
            copied_own = sem("copied_own")
            copied_src = sem("copied_src")
            message = sem("message")
            messages_out = sem("messages_out")
            summed_n = sem("summed_n")
            summed_m = sem("summed_m")
            summed_sq = sem("summed_sq")
            found_max = sem("found_max")
            found_min = sem("found_min")
            inverted_n = sem("inverted_n")
            inverted = sem("inverted")
            mean_made = sem("mean_made")
            mean_squared = sem("mean_squared")
            sq_scaled = sem("sq_scaled")
            var_made = sem("var_made")
            var_cut = sem("var_cut")
            dev_made = sem("dev_made")
            n_turned = sem("n_turned")
            log_made = sem("log_made")
            scales_made = sem("scales_made")
            projected = sem("projected")
            plain_out = sem("plain_out")
            amplified = sem("amplified")
            summed = sem("summed")
            ln = Norm(sem, "y2")

            @block.gpsimd
            def _(pool):
                bound = nc.gpsimd.to_reg(N - 1)

                def gathers(h, side):
                    j, par = 4 * h + side, side % 2
                    wait(pool, turned_own, j - 3)
                    wait(pool, turned_src, j - 3)
                    pool.sem_inc(pool_gate, 1)
                    for t in range(T):
                        gather(rows_x[:, side, t], y1_table, idx_a[:, side, t:t + 1], gathered[side], bound)
                    for t in range(T):
                        gather(base_x[:, side, t], y1_table, idx_b[:, side, t:t + 1], gathered[side], bound)

                def scatters(h, side):
                    wait(pool, ln.done, 4 * h + side + 1)
                    pool.sem_inc(pool_gate, 1)
                    for t in range(T):
                        scatter(y2_table, idx_w[:, side, t:t + 1], out_x[:, side, t], scattered[side], bound)
                pool_steps(pool, sem, ((idx_a, list_key[1]), (idx_b, list_other[1])), list_write[1],
                           gathers, scatters, gathered, scattered, 128)

            @block.sync
            def _(sp):
                def store(h, side):
                    wait(sp, ln.done, 4 * h + side + 1)
                    sp.dma_start(by_slot(y2_slots, 4 * h + side), out_x[:, side]).then_inc(stored[side], 16)
                staggered(sp, NSTEP, [(0, store)])
                for side in range(4):
                    sp.wait_ge(stored[side], 16 * steps_of(side))

            @block.tensor
            def _(pe):
                def turn(h, side):
                    j = 4 * h + side
                    keep_to_row_pe(pe, j, keep_in, keep_turned, keep_copied)
                    wait(pe, gathered[side], 128 * (h + 1))
                    wait(pe, copied_own, j)
                    for t in range(T):
                        mm = pe.transpose(bank[1][:, t * P:(t + 1) * P], rows_x[:, side, t], ident[:])
                    mm.then_inc(turned_own, 1)
                    wait(pe, copied_src, j)
                    for t in range(T):
                        mm = pe.transpose(bank[2][:, t * P:(t + 1) * P], base_x[:, side, t], ident[:])
                    mm.then_inc(turned_src, 1)

                def messages(h, side):
                    j, par = 4 * h + side, side % 2
                    wait(pe, copied_own, j + 1)
                    wait(pe, copied_src, j + 1)
                    wait(pe, messages_out, j)
                    pe.matmul(bank[3][:], w_dst_t[:], own_x[:, side], start=True, stop=False)
                    pe.matmul(bank[3][:], w_src_t[:], turned_x[:, par], start=False, stop=True).then_inc(message, 1)

                def counts(h, side):
                    j, par = 4 * h + side, side % 2
                    wait(pe, summed_n, j + 1)
                    wait(pe, log_made, j)
                    wait(pe, inverted, j)
                    for t in range(T):
                        mm = pe.matmul(bank[4][:, t:t + 1], agg_n[:, par, t * P:(t + 1) * P], ident[:, 0:1],
                                       start=True, stop=True)
                    mm.then_inc(n_turned, 1)

                def project(h, side, ts):
                    j, par = 4 * h + side, side % 2
                    wait(pe, found_max, j + 1)
                    wait(pe, found_min, j + 1)
                    wait(pe, mean_made, j + 1)
                    wait(pe, dev_made, j + 1)
                    for t in ts:
                        tile = T * j + t
                        cols = slice(t * P, (t + 1) * P)
                        wait(pe, summed, tile - 1)
                        wait(pe, plain_out, tile - 1)
                        to = bank[5 + t % 2]
                        pe.matmul(to[:, 0:D], own_x[:, side, cols], w_own[:], start=True, stop=False,
                                  skip_group_check=True)
                        add_bias(pe, to[:, 0:D], BIAS_B2, last=False)
                        for n, a in enumerate((agg_max[:, par, cols], agg_min[:, par, cols], mean[:, par, cols],
                                               dev[:, par, cols])):
                            mm = pe.matmul(to[:, 0:3 * D], a, w_agg[:, n], start=False, stop=(n == 3),
                                           skip_group_check=True)
                        mm.then_inc(projected, 1)

                def project_first(h, side):
                    project(h, side, (0, 1))

                def project_second(h, side):
                    project(h, side, (2, 3))
                staggered(pe, NSTEP, [(1, messages), (2, project_first), (0, turn), (1, counts),
                                      (2, project_second)])

            @block.scalar
            def _(act):
                def take_messages(h, side):
                    j = 4 * h + side
                    wait(act, message, j + 1)
                    wait(act, summed_sq, j)
                    wait(act, found_max, j)
                    wait(act, found_min, j)
                    act.activation(msg[:], bank[3][:], ACT.Identity, bias=b_pre_col[:])
                    act.activation(msg_sq[:], bank[3][:], ACT.Square, bias=b_pre_col[:]).then_inc(messages_out, 1)

                def square_mean(h, side):
                    j, par = 4 * h + side, side % 2
                    wait(act, mean_made, j + 1)
                    wait(act, var_made, j)
                    act.activation(mean_sq[:], mean[:, par], ACT.Square).then_inc(mean_squared, 1)

                def root_var(h, side):
                    j, par = 4 * h + side, side % 2
                    wait(act, var_cut, j + 1)
                    wait(act, projected, T * (j - 1))
                    act.activation(dev[:, par], var[:], ACT.Sqrt, bias=eps_col[:]).then_inc(dev_made, 1)

                def take_turned(h, side):
                    j, par = 4 * h + side, side % 2
                    wait(act, keep_turned, j + 1)
                    wait(act, summed_n, j - 1)
                    wait(act, summed_m, j - 1)
                    wait(act, summed_sq, j - 1)
                    wait(act, found_max, j - 1)
                    wait(act, found_min, j - 1)
                    act.copy(keep_row[:, par], bank[0][:])
                    act.activation(low_row[:, par], bank[0][:], ACT.Copy, scale=BIG, bias=-BIG)
                    act.activation(high_row[:, par], bank[0][:], ACT.Copy, scale=-BIG, bias=BIG)\
                        .then_inc(keep_copied, 1)
                    wait(act, turned_own, j + 1)
                    wait(act, projected, T * (j - 3))
                    act.copy(own_x[:, side], bank[1][:]).then_inc(copied_own, 1)

                def log_counts(h, side):
                    j, par = 4 * h + side, side % 2
                    wait(act, n_turned, j + 1)
                    wait(act, summed, T * (j - 1))
                    wait(act, scales_made, j - 1)
                    act.activation(scales[:, par, 1], bank[4][:, 0:T], ACT.Ln, bias=one_col[:])\
                        .then_inc(log_made, 1)

                def take_plain(h, side, ts):
                    j, par = 4 * h + side, side % 2
                    for t in ts:
                        tile = T * j + t
                        wait(act, projected, tile + 1)
                        wait(act, amplified, tile - T)
                        act.copy(plain_x[:, par, t], bank[5 + t % 2][:, 0:D]).then_inc(plain_out, 1)

                def root_norm(h, side):
                    norm_std(act, ln, 4 * h + side)
                staggered(act, NSTEP, [
                    (1, take_messages), (1, square_mean), (2, lambda h, side: take_plain(h, side, (0,))),
                    (1, root_var), (2, lambda h, side: take_plain(h, side, (1,))), (0, take_turned),
                    (2, lambda h, side: take_plain(h, side, (2, 3))), (2, root_norm), (1, log_counts)])

            @block.vector
            def _(dve):
                last_of = slice(STEP - 1, STEP)

                def keep_cols_in(h, side):
                    keep_to_cols_dve(dve, 4 * h + side, 1, keep_in, keep_turned)

                def count(h, side):
                    j, par = 4 * h + side, side % 2
                    wait(dve, keep_copied, j + 1)
                    wait(dve, summed_n, j)
                    wait(dve, n_turned, j - 1)
                    dve.tensor_tensor_scan(agg_n[:, par], keep_row[:, par], ones_step[:],
                                           agg_n[:, 1 - par, last_of], ALU.mult, ALU.add).then_inc(summed_n, 1)
                    wait(dve, summed_n, j + 1)
                    dve.reciprocal(inv_n[:, par], agg_n[:, par]).then_inc(inverted_n, 1)

                def sum_messages(h, side):
                    j, par = 4 * h + side, side % 2
                    wait(dve, messages_out, j + 1)
                    wait(dve, summed_m, j)
                    dve.tensor_tensor_scan(agg[:, par], keep_row[:, par], msg[:],
                                           agg[:, 1 - par, last_of], ALU.mult, ALU.add).then_inc(summed_m, 1)
                    wait(dve, summed_m, j + 1)
                    wait(dve, inverted_n, j + 1)
                    wait(dve, projected, T * (j - 1))
                    dve.tensor_tensor(mean[:, par], agg[:, par], inv_n[:, par], ALU.mult).then_inc(mean_made, 1)

                def variance(h, side):
                    j, par = 4 * h + side, side % 2
                    wait(dve, summed_sq, j)
                    dve.tensor_tensor_scan(agg_sq[:, par], keep_row[:, par], msg_sq[:],
                                           agg_sq[:, 1 - par, last_of], ALU.mult, ALU.add).then_inc(summed_sq, 1)
                    wait(dve, summed_sq, j + 1)
                    wait(dve, dev_made, j)
                    dve.tensor_tensor(var[:], agg_sq[:, par], inv_n[:, par], ALU.mult).then_inc(sq_scaled, 1)
                    wait(dve, sq_scaled, j + 1)
                    wait(dve, mean_squared, j + 1)
                    dve.tensor_tensor(var[:], var[:], mean_sq[:], ALU.subtract).then_inc(var_made, 1)
                    wait(dve, var_made, j + 1)
                    dve.tensor_scalar(var[:], var[:], 0.0, None, ALU.max).then_inc(var_cut, 1)

                def copy_src(h, side):
                    j, par = 4 * h + side, side % 2
                    wait(dve, turned_src, j + 1)
                    wait(dve, message, j - 1)
                    dve.tensor_copy(turned_x[:, par], bank[2][:]).then_inc(copied_src, 1)

                def extremes(h, side):
                    j, par = 4 * h + side, side % 2
                    wait(dve, found_max, j)
                    wait(dve, projected, T * (j - 1))
                    dve.tensor_tensor_scan(agg_max[:, par], low_row[:, par], msg[:],
                                           agg_max[:, 1 - par, last_of], ALU.add, ALU.max).then_inc(found_max, 1)
                    wait(dve, found_min, j)
                    dve.tensor_tensor_scan(agg_min[:, par], high_row[:, par], msg[:],
                                           agg_min[:, 1 - par, last_of], ALU.add, ALU.min).then_inc(found_min, 1)

                def invert(h, side):
                    j, par = 4 * h + side, side % 2
                    wait(dve, log_made, j + 1)
                    dve.sem_inc(dve_gate, 1)
                    dve.reciprocal(inv_count[:, bass.ds(j * T, T)], bank[4][:, 0:T]).then_inc(inverted, 1)
                    wait(dve, log_made, j + 1)
                    wait(dve, summed, T * (j - 1))
                    dve.reciprocal(scales[:, par, 2], scales[:, par, 1]).then_inc(scales_made, 1)

                def add_scaled(h, side, ts):
                    j, par = 4 * h + side, side % 2
                    wait(dve, scales_made, j + 1)
                    wait(dve, ln.done, j)
                    for t in ts:
                        tile = T * j + t
                        psum = bank[5 + t % 2]
                        wait(dve, plain_out, tile + 1)
                        dve.scalar_tensor_tensor(out=pre[:, t], in0=psum[:, D:2 * D],
                                                 scalar=scales[:, par, 1, t:t + 1],
                                                 in1=plain_x[:, par, t], op0=ALU.mult, op1=ALU.add)\
                            .then_inc(amplified, 1)
                        wait(dve, amplified, tile + 1)
                        dve.scalar_tensor_tensor(out=pre[:, t], in0=psum[:, 2 * D:3 * D],
                                                 scalar=scales[:, par, 2, t:t + 1], in1=pre[:, t],
                                                 op0=ALU.mult, op1=ALU.add).then_inc(summed, 1)

                def norm(h, side):
                    j = 4 * h + side
                    wait(dve, summed, T * (j + 1))
                    norm_moments(dve, ln, j, pre)
                    wait(dve, stored[side], 16 * h)
                    wait(dve, scattered[side], 64 * h)
                    norm_rows(dve, ln, j, pre, out_x[:, side])
                staggered(dve, NSTEP, [
                    (0, keep_cols_in), (2, invert), (1, sum_messages), (2, lambda h, side: add_scaled(h, side, (0,))),
                    (1, variance), (2, lambda h, side: add_scaled(h, side, (1,))), (0, copy_src),
                    (1, extremes), (0, count), (2, lambda h, side: add_scaled(h, side, (2,))),
                    (2, lambda h, side: add_scaled(h, side, (3,))), (2, norm)])

        phase(layer_2)

        def layer_3(block, sem):
            gathered = [sem(f"gathered{i}") for i in range(4)]
            scattered = [sem(f"scattered{i}") for i in range(4)]
            loaded = [sem(f"loaded{i}") for i in range(4)]
            keep_in = sem("keep_in")
            keep_turned = sem("keep_turned")
            keep_copied = sem("keep_copied")
            turned = sem("turned")
            scanned = sem("scanned")
            own_turned = sem("own_turned")
            own_copied = sem("own_copied")
            own_projected = sem("own_projected")
            own_out = sem("own_out")
            projected = sem("projected")
            joined = sem("joined")
            summed = sem("summed")
            ln = Norm(sem, "y3")

            @block.gpsimd
            def _(pool):
                bound = nc.gpsimd.to_reg(N - 1)

                def gathers(h, side):
                    wait(pool, turned, 4 * h + side - 3)
                    pool.sem_inc(pool_gate, 1)
                    for t in range(T):
                        gather(rows_x[:, side, t], y2_table, idx_a[:, side, t:t + 1], gathered[side], bound)

                def scatters(h, side):
                    wait(pool, ln.done, 4 * h + side + 1)
                    pool.sem_inc(pool_gate, 1)
                    for t in range(T):
                        scatter(out, idx_w[:, side, t:t + 1], out_x[:, side, t], scattered[side], bound)
                pool_steps(pool, sem, ((idx_a, list_other[1]),), list_write[1],
                           gathers, scatters, gathered, scattered, 64)

            @block.sync
            def _(sp):
                def load(h, side):
                    j, par = 4 * h + side, side % 2
                    wait(sp, own_turned, j - 3)
                    wait(sp, summed, j - 3)
                    sp.dma_start(base_x[:, side], by_slot(y2_slots, j)).then_inc(loaded[side], 16)
                staggered(sp, NSTEP, [(0, load)])

            @block.vector
            def _(dve):
                def scan(h, side):
                    j, par = 4 * h + side, side % 2
                    keep_to_cols_dve(dve, j, 1, keep_in, keep_turned)
                    wait(dve, turned, j + 1)
                    wait(dve, keep_copied, j + 1)
                    wait(dve, scanned, j)
                    wait(dve, projected, j - 1)
                    dve.tensor_tensor_scan(agg[:, par], keep_row[:, par], bank[1][:],
                                           agg[:, 1 - par, STEP - 1:STEP], ALU.mult, ALU.add).then_inc(scanned, 1)

                def finish(h, side):
                    j, par = 4 * h + side, side % 2
                    wait(dve, projected, j + 1)
                    wait(dve, own_out, j + 1)
                    wait(dve, ln.done, j)
                    dve.sem_inc(dve_gate, 1)
                    for t in range(T):
                        last = dve.scalar_tensor_tensor(out=pre_b[:, t], in0=bank4(2)[:, t],
                                                        scalar=inv_count[:, bass.ds(j * T + t, 1)],
                                                        in1=plain_x[:, par, t], op0=ALU.mult, op1=ALU.add)
                    last.then_inc(joined, 1)
                    wait(dve, joined, j + 1)
                    dve.scalar_tensor_tensor(out=pre[:], in0=pre_b[:], scalar=0.0, in1=base_x[:, side],
                                             op0=ALU.max, op1=ALU.add).then_inc(summed, 1)
                    wait(dve, summed, j + 1)
                    norm_moments(dve, ln, j, pre)
                    wait(dve, scattered[side], 64 * h)
                    norm_rows(dve, ln, j, pre, out_x[:, side])
                staggered(dve, NSTEP, [(0, scan), (1, finish)])

            @block.scalar
            def _(act):
                def scan(h, side):
                    j, par = 4 * h + side, side % 2
                    wait(act, keep_turned, j + 1)
                    wait(act, scanned, j - 1)
                    act.copy(keep_row[:, par], bank[0][:]).then_inc(keep_copied, 1)
                    wait(act, own_turned, j + 1)
                    wait(act, own_projected, j - 1)
                    act.copy(turned_x[:, par], bank[3][:]).then_inc(own_copied, 1)
                    wait(act, own_projected, j + 1)
                    wait(act, joined, j - 1)
                    act.copy(plain_x[:, par], bank4(4)).then_inc(own_out, 1)

                def finish(h, side):
                    j, par = 4 * h + side, side % 2
                    norm_std(act, ln, j)
                staggered(act, NSTEP, [(0, scan), (1, finish)])

            @block.tensor
            def _(pe):
                def scan(h, side):
                    j, par = 4 * h + side, side % 2
                    keep_to_row_pe(pe, j, keep_in, keep_turned, keep_copied)
                    wait(pe, loaded[side], 16 * (h + 1))
                    wait(pe, own_copied, j)
                    for t in range(T):
                        mm = pe.transpose(bank[3][:, t * P:(t + 1) * P], base_x[:, side, t], ident[:])
                    mm.then_inc(own_turned, 1)
                    wait(pe, gathered[side], 64 * (h + 1))
                    wait(pe, scanned, j)
                    for t in range(T):
                        mm = pe.transpose(bank[1][:, t * P:(t + 1) * P], rows_x[:, side, t], ident[:])
                    mm.then_inc(turned, 1)
                    wait(pe, own_copied, j + 1)
                    wait(pe, own_out, j)
                    for t in range(T):
                        to = bank[4][:, t * D:(t + 1) * D]
                        pe.matmul(to, turned_x[:, par, t * P:(t + 1) * P], w_r_t[:], start=True, stop=False)
                        mm = add_bias(pe, to, BIAS_B3)
                    mm.then_inc(own_projected, 1)
                    wait(pe, scanned, j + 1)
                    wait(pe, joined, j)
                    for t in range(T):
                        mm = pe.matmul(bank[2][:, t * D:(t + 1) * D], agg[:, par, t * P:(t + 1) * P], w_l_t[:],
                                       start=True, stop=True)
                    mm.then_inc(projected, 1)
                staggered(pe, NSTEP, [(0, scan)])

        phase(layer_3)


_INS = ["x", "src", "dst", "edge_weight", "L0_gnn_weight", "L0_gnn_bias_param", "L1_gnn_W", "L1_gnn_b",
        "L2_gnn_W_pre", "L2_gnn_b_pre", "L2_gnn_W_post", "L2_gnn_b_post", "L2_gnn_W_lin", "L2_gnn_b_lin",
        "L3_gnn_W_l", "L3_gnn_W_r", "L3_gnn_b"]


def kernel(**inputs):
    import numpy as _np
    import concourse.bacc as _bacc
    from concourse.bass_utils import run_bass_kernel_spmd as _run

    nc = _bacc.Bacc("TRN2", target_bir_lowering=False, num_devices=1)
    arrays, args = {}, []
    for name in _INS:
        a = _np.ascontiguousarray(inputs[name])
        arrays[f"in_{name}_dram"] = a
        args.append(nc.dram_tensor(f"in_{name}_dram", a.shape, mybir.dt.from_np(a.dtype), kind="ExternalInput").ap())
    args.append(nc.dram_tensor("out_0_dram", (N, D), F32, kind="ExternalOutput").ap())
    gnn_kernel(nc, *args)
    r = _run(nc, [arrays], core_ids=[0])
    return r.results[0]["out_0_dram"]
```
